# Optimizing a Trainium2 kernel written in Bass

```python
import numpy as np
import jax
import jax.numpy as jnp

def _softmax(x, axis=-1):
    return jax.nn.softmax(x, axis=axis)

def _gelu(x):
    return jax.nn.gelu(x, approximate=True)

def _silu(x):
    return jax.nn.silu(x)

def _sigmoid(x):
    return jax.nn.sigmoid(x)

def _layernorm(x, axis=-1, eps=1e-05):
    m = jnp.mean(x, axis=axis, keepdims=True)
    v = jnp.var(x, axis=axis, keepdims=True)
    return (x - m) / jnp.sqrt(v + eps)

def _scatter_add(tgt, idx, src, axis=0):
    return tgt.at[idx].add(src)

def _segment_sum(src, seg, n):
    return jax.ops.segment_sum(src, seg, n)
kernel_name = 'mk_early_fusion_d2_tok_img256_r4_73f6a3'

def setup_inputs(seed: int=0):
    np.random.seed(seed)
    _w = jnp.asarray

    def _rec_inputs():
        import jax
        import jax.numpy as jnp
        _rk = jax.random.key(seed)
        x = -0.000125008 + 0.999885 * jax.random.normal(jax.random.fold_in(_rk, 1), (32, 64, 64, 64), jnp.float32)
        txt = -0.000570488 + 0.251296 * jax.random.normal(jax.random.fold_in(_rk, 2), (32, 128, 64), jnp.float32)
        return (x, txt)
    x, txt = _rec_inputs()

    def _L0_tok_setup():
        import jax, jax.numpy as jnp
        import numpy as np
        B, C, H, W = (32, 64, 64, 64)
        STRIDE, HEADS = (4, 8)

        def _ln(x, w, b):
            mu = x.mean(-1, keepdims=True)
            var = ((x - mu) ** 2).mean(-1, keepdims=True)
            return (x - mu) * jax.lax.rsqrt(var + 1e-05) * w + b
        key = jax.random.key(seed)
        ks = jax.random.split(key, 4)
        return {'features': jax.random.normal(ks[0], (B, C, H, W), dtype=jnp.float32), 'ln_q_w': jnp.ones((C,), jnp.float32), 'ln_q_b': jnp.zeros((C,), jnp.float32), 'Wq': jax.random.normal(ks[1], (C, C), dtype=jnp.float32) * 0.02, 'ln_kv_w': jnp.ones((C,), jnp.float32), 'ln_kv_b': jnp.zeros((C,), jnp.float32), 'Wkv': jax.random.normal(ks[2], (2 * C, C), dtype=jnp.float32) * 0.02, 'proj_w': jax.random.normal(ks[3], (C, C), dtype=jnp.float32) * 0.02, 'proj_b': jnp.zeros((C,), jnp.float32), 'conv_stride': STRIDE, 'num_heads': HEADS}
    _L0_tok_all = _L0_tok_setup()
    _L0_tok_in = {k: v for k, v in _L0_tok_all.items() if k in ('ln_q_w', 'ln_q_b', 'Wq', 'ln_kv_w', 'ln_kv_b', 'Wkv', 'proj_w', 'proj_b')}
    del _L0_tok_all

    def _L0_attn_setup():
        import jax, jax.numpy as jnp
        import numpy as np
        import math
        H = 8
        DH = 16
        DEPTH = 1
        LAMBDA_INIT = 0.8 - 0.6 * math.exp(-0.3 * DEPTH)
        LN_EPS = 1e-05
        key = jax.random.key(seed)
        ks = jax.random.split(key, 12)
        dim = 64
        inner = 2 * H * DH
        b, n = (2, 512)
        s = lambda fan_in: 1.0 / math.sqrt(fan_in)
        return {'x': jax.random.normal(ks[0], (b, n, dim), jnp.float32), 'Wq': jax.random.normal(ks[1], (dim, inner), jnp.float32) * s(dim), 'Wkv': jax.random.normal(ks[2], (dim, 2 * inner), jnp.float32) * s(dim), 'Wout': jax.random.normal(ks[3], (inner, dim), jnp.float32) * s(inner), 'bout': jnp.zeros((dim,), jnp.float32), 'Wg': jax.random.normal(ks[4], (dim, inner), jnp.float32) * s(dim), 'bg': jnp.ones((inner,), jnp.float32), 'lq1': jax.random.normal(ks[5], (DH,), jnp.float32) * 0.1, 'lk1': jax.random.normal(ks[6], (DH,), jnp.float32) * 0.1, 'lq2': jax.random.normal(ks[7], (DH,), jnp.float32) * 0.1, 'lk2': jax.random.normal(ks[8], (DH,), jnp.float32) * 0.1, 'ln_gamma': jnp.ones((2 * DH,), jnp.float32), 'ln_beta': jnp.zeros((2 * DH,), jnp.float32)}
    _L0_attn_all = _L0_attn_setup()
    _L0_attn_in = {k: v for k, v in _L0_attn_all.items() if k in ('Wq', 'Wkv', 'Wout', 'bout', 'Wg', 'bg', 'lq1', 'lk1', 'lq2', 'lk2', 'ln_gamma', 'ln_beta')}
    del _L0_attn_all

    def _L0_ffn_setup():
        import jax, jax.numpy as jnp
        import numpy as np
        B, A = (1024, 8)
        IN, OUT = (64, 64)
        SH1, SH2 = (64, 128)
        EH1, EH2 = (128, 64)
        E, TOPK = (4, 2)

        def _shared_mlp(x, W1, b1, W2, b2, W3, b3):
            h = jax.nn.relu(x @ W1 + b1)
            h = jax.nn.relu(h @ W2 + b2)
            return h @ W3 + b3

        def _experts_mlp(x, eW1, eb1, eW2, eb2, eW3, eb3):
            h = jax.nn.relu(jnp.einsum('baf,efh->ebah', x, eW1) + eb1[:, None, None, :])
            h = jax.nn.relu(jnp.einsum('ebah,ehg->ebag', h, eW2) + eb2[:, None, None, :])
            o = jnp.einsum('ebag,ego->ebao', h, eW3) + eb3[:, None, None, :]
            return jnp.moveaxis(o, 0, -1)
        key = jax.random.key(seed)
        ks = jax.random.split(key, 16)
        s = 0.05
        return {'x': jax.random.normal(ks[0], (B, A, IN), jnp.float32), 'sW1': jax.random.normal(ks[1], (IN, SH1), jnp.float32) * s, 'sb1': jnp.zeros((SH1,), jnp.float32), 'sW2': jax.random.normal(ks[2], (SH1, SH2), jnp.float32) * s, 'sb2': jnp.zeros((SH2,), jnp.float32), 'sW3': jax.random.normal(ks[3], (SH2, OUT), jnp.float32) * s, 'sb3': jnp.zeros((OUT,), jnp.float32), 'eW1': jax.random.normal(ks[4], (E, IN, EH1), jnp.float32) * s, 'eb1': jnp.zeros((E, EH1), jnp.float32), 'eW2': jax.random.normal(ks[5], (E, EH1, EH2), jnp.float32) * s, 'eb2': jnp.zeros((E, EH2), jnp.float32), 'eW3': jax.random.normal(ks[6], (E, EH2, OUT), jnp.float32) * s, 'eb3': jnp.zeros((E, OUT), jnp.float32), 'gW': jax.random.normal(ks[7], (IN, E), jnp.float32) * s, 'gb': jnp.zeros((E,), jnp.float32)}
    _L0_ffn_all = _L0_ffn_setup()
    _L0_ffn_in = {k: v for k, v in _L0_ffn_all.items() if k in ('sW1', 'sb1', 'sW2', 'sb2', 'sW3', 'sb3', 'eW1', 'eb1', 'eW2', 'eb2', 'eW3', 'eb3', 'gW', 'gb')}
    del _L0_ffn_all

    def _L1_attn_setup():
        import jax, jax.numpy as jnp
        import numpy as np
        GROUPS = 64
        EPS = 1e-05
        DIM = 64
        SEQ = 256
        BATCH = 1

        def _group_norm(y, weight, bias):
            g = y.reshape(y.shape[:-1] + (GROUPS, -1))
            mean = g.mean(axis=-1, keepdims=True)
            var = g.var(axis=-1, keepdims=True)
            g = (g - mean) * jax.lax.rsqrt(var + EPS)
            return g.reshape(y.shape) * weight + bias

        def gate_loop_operator(k, v, q, a):
            kv = (k[..., :, None] * v[..., None, :]).astype(a.dtype)
            aa = a[..., :, None]

            def binop(e_i, e_j):
                a_i, kv_i = e_i
                a_j, kv_j = e_j
                return (a_j * a_i, a_j * kv_i + kv_j)
            _, y = jax.lax.associative_scan(binop, (aa, kv), axis=1)
            y = jnp.real(y).astype(k.dtype)
            return jnp.einsum('bld,blde->ble', q, y)
        key = jax.random.key(seed)
        ks = jax.random.split(key, 7)
        ortho = jax.nn.initializers.orthogonal()
        return {'x': jax.random.normal(ks[0], (BATCH, SEQ, DIM), jnp.float32), 'wq': ortho(ks[1], (DIM, DIM), jnp.float32), 'wk': ortho(ks[2], (DIM, DIM), jnp.float32), 'wv': ortho(ks[3], (DIM, DIM), jnp.float32), 'wa': ortho(ks[4], (DIM, 2 * DIM), jnp.float32), 'wg': ortho(ks[5], (DIM, DIM), jnp.float32), 'wo': ortho(ks[6], (DIM, DIM), jnp.float32), 'gn_weight': jnp.ones((DIM,), jnp.float32), 'gn_bias': jnp.zeros((DIM,), jnp.float32), 'bias': jnp.zeros((DIM,), jnp.float32)}
    _L1_attn_all = _L1_attn_setup()
    _L1_attn_in = {k: v for k, v in _L1_attn_all.items() if k in ('wq', 'wk', 'wv', 'wa', 'wg', 'wo', 'gn_weight', 'gn_bias', 'bias')}
    del _L1_attn_all

    def _L1_ffn_setup():
        import jax, jax.numpy as jnp
        import numpy as np
        B, S, D, F, E, K = (8, 512, 64, 256, 8, 2)
        key = jax.random.key(seed)
        ks = jax.random.split(key, 10)
        s = 0.02
        return {'x': jax.random.normal(ks[0], (B, S, D), dtype=jnp.float32), 'Wr': jax.random.normal(ks[1], (D, E), dtype=jnp.float32) * s, 'W1s': jax.random.normal(ks[2], (D, F), dtype=jnp.float32) * s, 'b1s': jnp.zeros((F,), dtype=jnp.float32), 'W2s': jax.random.normal(ks[3], (F, D), dtype=jnp.float32) * s, 'b2s': jnp.zeros((D,), dtype=jnp.float32), 'W1p': jax.random.normal(ks[4], (E, D, F), dtype=jnp.float32) * s, 'b1p': jnp.zeros((E, F), dtype=jnp.float32), 'W2p': jax.random.normal(ks[5], (E, F, D), dtype=jnp.float32) * s, 'b2p': jnp.zeros((E, D), dtype=jnp.float32)}
    _L1_ffn_all = _L1_ffn_setup()
    _L1_ffn_in = {k: v for k, v in _L1_ffn_all.items() if k in ('Wr', 'W1s', 'b1s', 'W2s', 'b2s', 'W1p', 'b1p', 'W2p', 'b2p')}
    del _L1_ffn_all
    return {'x': x, 'txt': txt, 'L0_tok_ln_q_w': _L0_tok_in['ln_q_w'], 'L0_tok_ln_q_b': _L0_tok_in['ln_q_b'], 'L0_tok_Wq': _L0_tok_in['Wq'], 'L0_tok_ln_kv_w': _L0_tok_in['ln_kv_w'], 'L0_tok_ln_kv_b': _L0_tok_in['ln_kv_b'], 'L0_tok_Wkv': _L0_tok_in['Wkv'], 'L0_tok_proj_w': _L0_tok_in['proj_w'], 'L0_tok_proj_b': _L0_tok_in['proj_b'], 'L0_attn_Wq': _L0_attn_in['Wq'], 'L0_attn_Wkv': _L0_attn_in['Wkv'], 'L0_attn_Wout': _L0_attn_in['Wout'], 'L0_attn_bout': _L0_attn_in['bout'], 'L0_attn_Wg': _L0_attn_in['Wg'], 'L0_attn_bg': _L0_attn_in['bg'], 'L0_attn_lq1': _L0_attn_in['lq1'], 'L0_attn_lk1': _L0_attn_in['lk1'], 'L0_attn_lq2': _L0_attn_in['lq2'], 'L0_attn_lk2': _L0_attn_in['lk2'], 'L0_attn_ln_gamma': _L0_attn_in['ln_gamma'], 'L0_attn_ln_beta': _L0_attn_in['ln_beta'], 'L0_ffn_sW1': _L0_ffn_in['sW1'], 'L0_ffn_sb1': _L0_ffn_in['sb1'], 'L0_ffn_sW2': _L0_ffn_in['sW2'], 'L0_ffn_sb2': _L0_ffn_in['sb2'], 'L0_ffn_sW3': _L0_ffn_in['sW3'], 'L0_ffn_sb3': _L0_ffn_in['sb3'], 'L0_ffn_eW1': _L0_ffn_in['eW1'], 'L0_ffn_eb1': _L0_ffn_in['eb1'], 'L0_ffn_eW2': _L0_ffn_in['eW2'], 'L0_ffn_eb2': _L0_ffn_in['eb2'], 'L0_ffn_eW3': _L0_ffn_in['eW3'], 'L0_ffn_eb3': _L0_ffn_in['eb3'], 'L0_ffn_gW': _L0_ffn_in['gW'], 'L0_ffn_gb': _L0_ffn_in['gb'], 'L1_attn_wq': _L1_attn_in['wq'], 'L1_attn_wk': _L1_attn_in['wk'], 'L1_attn_wv': _L1_attn_in['wv'], 'L1_attn_wa': _L1_attn_in['wa'], 'L1_attn_wg': _L1_attn_in['wg'], 'L1_attn_wo': _L1_attn_in['wo'], 'L1_attn_gn_weight': _L1_attn_in['gn_weight'], 'L1_attn_gn_bias': _L1_attn_in['gn_bias'], 'L1_attn_bias': _L1_attn_in['bias'], 'L1_ffn_Wr': _L1_ffn_in['Wr'], 'L1_ffn_W1s': _L1_ffn_in['W1s'], 'L1_ffn_b1s': _L1_ffn_in['b1s'], 'L1_ffn_W2s': _L1_ffn_in['W2s'], 'L1_ffn_b2s': _L1_ffn_in['b2s'], 'L1_ffn_W1p': _L1_ffn_in['W1p'], 'L1_ffn_b1p': _L1_ffn_in['b1p'], 'L1_ffn_W2p': _L1_ffn_in['W2p'], 'L1_ffn_b2p': _L1_ffn_in['b2p']}

def reference(x, txt, L0_tok_ln_q_w, L0_tok_ln_q_b, L0_tok_Wq, L0_tok_ln_kv_w, L0_tok_ln_kv_b, L0_tok_Wkv, L0_tok_proj_w, L0_tok_proj_b, L0_attn_Wq, L0_attn_Wkv, L0_attn_Wout, L0_attn_bout, L0_attn_Wg, L0_attn_bg, L0_attn_lq1, L0_attn_lk1, L0_attn_lq2, L0_attn_lk2, L0_attn_ln_gamma, L0_attn_ln_beta, L0_ffn_sW1, L0_ffn_sb1, L0_ffn_sW2, L0_ffn_sb2, L0_ffn_sW3, L0_ffn_sb3, L0_ffn_eW1, L0_ffn_eb1, L0_ffn_eW2, L0_ffn_eb2, L0_ffn_eW3, L0_ffn_eb3, L0_ffn_gW, L0_ffn_gb, L1_attn_wq, L1_attn_wk, L1_attn_wv, L1_attn_wa, L1_attn_wg, L1_attn_wo, L1_attn_gn_weight, L1_attn_gn_bias, L1_attn_bias, L1_ffn_Wr, L1_ffn_W1s, L1_ffn_b1s, L1_ffn_W2s, L1_ffn_b2s, L1_ffn_W1p, L1_ffn_b1p, L1_ffn_W2p, L1_ffn_b2p):
    import jax
    import jax.numpy as jnp

    def _L0_tok_ref(features, ln_q_w, ln_q_b, Wq, ln_kv_w, ln_kv_b, Wkv, proj_w, proj_b, conv_stride, num_heads):
        import jax, jax.numpy as jnp
        import numpy as np
        B, C, H, W = (32, 64, 64, 64)
        STRIDE, HEADS = (4, 8)

        def _ln(x, w, b):
            mu = x.mean(-1, keepdims=True)
            var = ((x - mu) ** 2).mean(-1, keepdims=True)
            return (x - mu) * jax.lax.rsqrt(var + 1e-05) * w + b
        s = conv_stride
        b, c, hh, ww = features.shape
        h, w = (hh // s, ww // s)
        hw, n, d = (h * w, s * s, c // num_heads)
        scale = c ** (-0.5)
        x = features.reshape(b, c, h, s, w, s)
        reduce_feats = x.mean((3, 5)).reshape(b, c, hw).transpose(0, 2, 1)
        unf = x.transpose(0, 1, 2, 4, 3, 5).reshape(b, c, hw, n).transpose(0, 2, 3, 1)
        q = _ln(reduce_feats, ln_q_w, ln_q_b) @ Wq.T
        q = q.reshape(b, hw, num_heads, d).transpose(0, 2, 1, 3)
        kv = _ln(unf, ln_kv_w, ln_kv_b) @ Wkv.T
        kv = kv.reshape(b, hw, n, 2, num_heads, d).transpose(3, 0, 4, 1, 2, 5)
        k, v = (kv[0], kv[1])
        attn = jax.nn.softmax(jnp.einsum('bhpd,bhpnd->bhpn', q * scale, k), axis=-1)
        aggre = jnp.einsum('bhpn,bhpnd->bhpd', attn, v)
        aggre = aggre.transpose(0, 2, 1, 3).reshape(b, hw, c)
        return reduce_feats + aggre @ proj_w.T + proj_b

    def _L0_attn_ref(x, Wq, Wkv, Wout, bout, Wg, bg, lq1, lk1, lq2, lk2, ln_gamma, ln_beta):
        import jax, jax.numpy as jnp
        import numpy as np
        import math
        H = 8
        DH = 16
        DEPTH = 1
        LAMBDA_INIT = 0.8 - 0.6 * math.exp(-0.3 * DEPTH)
        LN_EPS = 1e-05
        b, n, dim = x.shape
        scale = DH ** (-0.5)
        q = x @ Wq
        kv = x @ Wkv
        k, v = jnp.split(kv, 2, axis=-1)
        q = q.reshape(b, n, 2 * H, DH).transpose(0, 2, 1, 3) * scale
        k = k.reshape(b, n, 2 * H, DH).transpose(0, 2, 1, 3)
        v = v.reshape(b, n, H, 2 * DH).transpose(0, 2, 1, 3)
        dots = jnp.einsum('bhid,bhjd->bhij', q, k)
        attn = jax.nn.softmax(dots, axis=-1)
        lam1 = jnp.exp(jnp.sum(lq1 * lk1))
        lam2 = jnp.exp(jnp.sum(lq2 * lk2))
        lam = lam1 - lam2 + LAMBDA_INIT
        attn = attn.reshape(b, H, 2, n, n)
        attn = attn[:, :, 0] - lam * attn[:, :, 1]
        out = jnp.einsum('bhij,bhjd->bhid', attn, v)
        mu = jnp.mean(out, axis=-1, keepdims=True)
        var = jnp.var(out, axis=-1, keepdims=True)
        out = (out - mu) * jax.lax.rsqrt(var + LN_EPS) * ln_gamma + ln_beta
        out = out * (1.0 - LAMBDA_INIT)
        out = out.transpose(0, 2, 1, 3).reshape(b, n, H * 2 * DH)
        gates = x @ Wg + bg
        out = out * jax.nn.sigmoid(gates)
        return out @ Wout + bout

    def _L0_ffn_ref(x, sW1, sb1, sW2, sb2, sW3, sb3, eW1, eb1, eW2, eb2, eW3, eb3, gW, gb):
        import jax, jax.numpy as jnp
        import numpy as np
        B, A = (1024, 8)
        IN, OUT = (64, 64)
        SH1, SH2 = (64, 128)
        EH1, EH2 = (128, 64)
        E, TOPK = (4, 2)

        def _shared_mlp(x, W1, b1, W2, b2, W3, b3):
            h = jax.nn.relu(x @ W1 + b1)
            h = jax.nn.relu(h @ W2 + b2)
            return h @ W3 + b3

        def _experts_mlp(x, eW1, eb1, eW2, eb2, eW3, eb3):
            h = jax.nn.relu(jnp.einsum('baf,efh->ebah', x, eW1) + eb1[:, None, None, :])
            h = jax.nn.relu(jnp.einsum('ebah,ehg->ebag', h, eW2) + eb2[:, None, None, :])
            o = jnp.einsum('ebag,ego->ebao', h, eW3) + eb3[:, None, None, :]
            return jnp.moveaxis(o, 0, -1)
        all_out = _experts_mlp(x, eW1, eb1, eW2, eb2, eW3, eb3)
        shared = _shared_mlp(x, sW1, sb1, sW2, sb2, sW3, sb3)
        gates = jax.nn.softmax(x @ gW + gb, axis=-1)
        topv, topi = jax.lax.top_k(gates, TOPK)
        topw = jax.nn.softmax(topv, axis=-1)
        sel = jnp.take_along_axis(all_out, topi[:, :, None, :], axis=-1)
        gated = jnp.sum(sel * topw[:, :, None, :], axis=-1)
        return shared + gated

    def _L1_attn_ref(x, wq, wk, wv, wa, wg, wo, gn_weight, gn_bias, bias):
        import jax, jax.numpy as jnp
        import numpy as np
        GROUPS = 64
        EPS = 1e-05
        DIM = 64
        SEQ = 256
        BATCH = 1

        def _group_norm(y, weight, bias):
            g = y.reshape(y.shape[:-1] + (GROUPS, -1))
            mean = g.mean(axis=-1, keepdims=True)
            var = g.var(axis=-1, keepdims=True)
            g = (g - mean) * jax.lax.rsqrt(var + EPS)
            return g.reshape(y.shape) * weight + bias

        def gate_loop_operator(k, v, q, a):
            kv = (k[..., :, None] * v[..., None, :]).astype(a.dtype)
            aa = a[..., :, None]

            def binop(e_i, e_j):
                a_i, kv_i = e_i
                a_j, kv_j = e_j
                return (a_j * a_i, a_j * kv_i + kv_j)
            _, y = jax.lax.associative_scan(binop, (aa, kv), axis=1)
            y = jnp.real(y).astype(k.dtype)
            return jnp.einsum('bld,blde->ble', q, y)
        q = x @ wq
        k = x @ wk
        v = x @ wv
        g = x @ wg
        a = (x @ wa).astype(jnp.float32)
        a_real, a_imag = jnp.split(a, 2, axis=-1)
        a_complex = jax.nn.sigmoid(a_real) * jnp.exp(1j * a_imag)
        y = gate_loop_operator(k, v, q, a_complex)
        y = _group_norm(y, gn_weight, gn_bias)
        y = y * jax.nn.silu(g)
        return y @ wo + bias

    def _L1_ffn_ref(x, Wr, W1s, b1s, W2s, b2s, W1p, b1p, W2p, b2p):
        import jax, jax.numpy as jnp
        import numpy as np
        B, S, D, F, E, K = (8, 512, 64, 256, 8, 2)
        gelu = lambda t: jax.nn.gelu(t, approximate=False)
        shared = gelu(x @ W1s + b1s) @ W2s + b2s
        rw = jax.nn.softmax(x @ Wr, axis=-1)
        topw, topi = jax.lax.top_k(rw, K)
        topw = topw / jnp.sum(topw, axis=-1, keepdims=True)
        mask = jnp.sum(jax.nn.one_hot(topi, E, dtype=topw.dtype) * topw[..., None], axis=-2)
        h = gelu(jnp.einsum('bsd,edf->bsef', x, W1p) + b1p)
        priv = jnp.einsum('bsef,efd->bsed', h, W2p) + b2p
        routed = jnp.einsum('bsed,bse->bsd', priv, mask)
        return shared + routed
    h = _L0_tok_ref(x, L0_tok_ln_q_w, L0_tok_ln_q_b, L0_tok_Wq, L0_tok_ln_kv_w, L0_tok_ln_kv_b, L0_tok_Wkv, L0_tok_proj_w, L0_tok_proj_b, 4, 8)
    h = jnp.concatenate([h, txt], axis=1)
    h = h + _L0_attn_ref(_layernorm(h, axis=-1), L0_attn_Wq, L0_attn_Wkv, L0_attn_Wout, L0_attn_bout, L0_attn_Wg, L0_attn_bg, L0_attn_lq1, L0_attn_lk1, L0_attn_lq2, L0_attn_lk2, L0_attn_ln_gamma, L0_attn_ln_beta)
    h = h + _L0_ffn_ref(_layernorm(h, axis=-1), L0_ffn_sW1, L0_ffn_sb1, L0_ffn_sW2, L0_ffn_sb2, L0_ffn_sW3, L0_ffn_sb3, L0_ffn_eW1, L0_ffn_eb1, L0_ffn_eW2, L0_ffn_eb2, L0_ffn_eW3, L0_ffn_eb3, L0_ffn_gW, L0_ffn_gb)
    h = h + _L1_attn_ref(_layernorm(h, axis=-1), L1_attn_wq, L1_attn_wk, L1_attn_wv, L1_attn_wa, L1_attn_wg, L1_attn_wo, L1_attn_gn_weight, L1_attn_gn_bias, L1_attn_bias)
    h = h + _L1_ffn_ref(_layernorm(h, axis=-1), L1_ffn_Wr, L1_ffn_W1s, L1_ffn_b1s, L1_ffn_W2s, L1_ffn_b2s, L1_ffn_W1p, L1_ffn_b1p, L1_ffn_W2p, L1_ffn_b2p)
    return h

_drawn_inputs = setup_inputs


def setup_inputs(seed=0):
    import zlib

    import numpy as np

    out = dict(_drawn_inputs(seed))
    spreads = {'L0_tok_ln_q_w': (1.0, 0.6),
     'L0_tok_ln_q_b': (0.0, 2.0),
     'L0_tok_ln_kv_w': (1.0, 0.6),
     'L0_tok_ln_kv_b': (0.0, 0.1),
     'L0_tok_proj_b': (0.0, 0.1),
     'L0_attn_bout': (0.0, 0.1),
     'L0_attn_bg': (1.0, 0.2),
     'L0_attn_ln_gamma': (1.0, 0.2),
     'L0_attn_ln_beta': (0.0, 0.1),
     'L0_ffn_sb1': (0.0, 0.384),
     'L0_ffn_sb2': (0.0, 0.1),
     'L0_ffn_sb3': (0.0, 0.1),
     'L0_ffn_eb1': (0.0, 0.517),
     'L0_ffn_eb2': (0.0, 0.271),
     'L0_ffn_eb3': (0.0, 0.1),
     'L0_ffn_gb': (0.0, 0.1),
     'L1_attn_gn_weight': (1.0, 0.2),
     'L1_attn_gn_bias': (0.0, 0.1),
     'L1_attn_bias': (0.0, 0.1),
     'L1_ffn_b1s': (0.0, 0.286),
     'L1_ffn_b2s': (0.0, 0.1),
     'L1_ffn_b1p': (0.0, 0.446),
     'L1_ffn_b2p': (0.0, 0.1)}
    factors = {'L0_tok_Wq': 28.599, 'L0_attn_lq1': 3.002}
    for name, (base, spread) in spreads.items():
        noise = np.random.default_rng([zlib.crc32(name.encode()), seed]).standard_normal(out[name].shape)
        drawn = base * np.exp(spread * noise) if base else spread * noise
        out[name] = jnp.asarray(drawn.astype(out[name].dtype))
    for name, factor in factors.items():
        out[name] = (out[name] * factor).astype(out[name].dtype)
    return out
```

```python
import math
from contextlib import ExitStack

import concourse.bass as bass
from concourse import mybir

B, C, IMG = 32, 64, 64
TXT = 128
STRIDE, TOK_HEADS = 4, 8
SIDE = IMG // STRIDE
PATCHES = SIDE * SIDE
L = PATCHES + TXT
NT = L // 128
TILES = B * NT
HEADS, DH = 8, 16
DV = 2 * DH
INNER = HEADS * DV
E0, E0_H1, E0_H2, S0_H1, S0_H2 = 4, 128, 64, 64, 128
E1, F1 = 8, 256
EPS = 1e-5
LAMBDA_INIT = 0.8 - 0.6 * math.exp(-0.3)

FIELDS = [
    ("ident", 128), ("sel", 1024), ("selT", 1024), ("center", 128), ("blk", 2),
    ("tq", 128), ("tk", 128), ("tv", 128), ("tproj", 128), ("kvw", 1), ("kvb", 1),
    ("lnqw", 64), ("lnqb", 64), ("projb", 64),
    ("aqk", 512), ("avg", 512), ("aout", 128), ("aoutb", 64), ("gam", 32), ("bet", 32), ("lqk", 64),
    ("sw1", 128), ("ew1", 512), ("gw", 4), ("sw2", 128), ("sb2", 1), ("sw3", 64), ("ew2", 256), ("eb2", 2),
    ("ew3", 256), ("b30", 320), ("tie0", 16),
    ("glg", 64), ("glo", 64), ("gnb", 1), ("glb", 64),
    ("wr", 8), ("w1", 9 * F1), ("w2", 9 * 128), ("b21", 9 * 64), ("tie1", 64),
]
AT = {}
_n = 0
for _name, _w in FIELDS:
    AT[_name] = (_n, _w)
    _n += _w
WCOLS = _n


F32 = mybir.dt.float32
BF16 = mybir.dt.bfloat16
ALU = mybir.AluOpType
ACT = mybir.ActivationFunctionType
AX_X, AX_XY = mybir.AxisListType.X, mybir.AxisListType.XY


def signals(nc, ctx, prefix, names):
    sems = {n: nc.alloc_semaphore(name=prefix + n) for n in names.split()}

    def clear():
        nc.clear_and_free_semaphores(list(sems.values()))
        nc.all_engine_barrier()

    ctx.callback(clear)
    return sems


def load_stage(nc, mem, pack, txt):
    with nc.semaphore("loaded") as loaded, nc.Block() as block:
        @block.sync
        def _(sp):
            sp.dma_start(mem["w"][:, :], pack).then_inc(loaded, 16)
            sp.dma_start(mem["h"][:, 2:TILES:NT, :], txt.rearrange("b l d -> l b d")).then_inc(loaded, 16)
            sp.wait_ge(loaded, 32)


def store_stage(nc, mem, out):
    with nc.semaphore("stored") as stored, nc.Block() as block:
        @block.sync
        def _(sp):
            sp.dma_start(out.rearrange("b (j p) c -> p (b j) c", p=128), mem["h"][:, :, :]).then_inc(stored, 16)
            sp.wait_ge(stored, 16)


def tok_stage(nc, mem, x):
    h_all, W = mem["h"], mem["W"]
    CH = 8
    with ExitStack() as ctx:
        sb = lambda n, s, d=F32: ctx.enter_context(nc.sbuf_tensor("t_" + n, s, d))
        ps = lambda n, s, d=F32: ctx.enter_context(nc.psum_tensor("t_" + n, s, d))
        xb = [sb(f"x{k}", [128, 4096]) for k in range(2)]
        sq = sb("sq", [128, 4096])
        wk, wv = sb("wk", [128, 128]), sb("wv", [128, 128])
        wk0, wv0 = sb("wk0", [128, 128]), sb("wv0", [128, 128])
        kb, vb = sb("kb", [128, 1]), sb("vb", [128, 1])
        half = sb("half", [128, 64])
        rf = sb("rf", [128, PATCHES])
        rt = sb("rt", [128, 4, 64])
        hc, hs, qn = sb("hc", [128, 4, 64]), sb("hs", [128, 4, 64]), sb("qn", [128, 4, 64])
        sm, nm, ve, rs = (sb(n, [128, 4]) for n in ("sm", "nm", "ve", "rs"))
        qnT = sb("qnT", [128, 256])
        qx = sb("qx", [128, 256, 4])
        t0 = sb("t0", [128, 256])
        tb = [sb(f"tb{k}", [128, 512]) for k in range(2)]
        st = sb("st", [128, 32, 4])
        m2, va, rr = (sb(n, [128, 32, 2]) for n in ("m2", "va", "rr"))
        rrep = sb("rrep", [128, 4, 8, 2, 8])
        rp = sb("rp", [128, 512])
        c0 = sb("c0", [128, 32, 4])
        s1, s2, s3, ex, p1, p2 = (sb(n, [128, 512]) for n in ("s1", "s2", "s3", "ex", "p1", "p2"))
        mx, z, rz = (sb(n, [128, 32]) for n in ("mx", "z", "rz"))
        mxx, rzx = sb("mxx", [128, 32, 4]), sb("rzx", [128, 32, 4])
        vs = [sb(f"vs{k}", [128, 512]) for k in range(2)]
        pv = [sb(f"pv{k}", [128, 512]) for k in range(2)]
        agg, agb = sb("agg", [128, 256]), sb("agb", [128, 256])
        po = sb("po", [128, 4, 64])
        misc = ps("misc", [128, 512])
        kps = [ps(f"k{k}", [128, 512]) for k in range(2)]
        sps = ps("s", [128, 512])
        vps = [ps(f"v{k}", [128, 512]) for k in range(2)]
        bps = [ps(f"b{k}", [128, 512]) for k in range(2)]
        s = signals(nc, ctx, "t_", """wfold wcent wready half x_in0 x_in1 x_used rf rfT rt sm nm hc hs ssq ve rs hn hnw qn qnT_ps qnT
            q_ps qx t0 sq stat_ps st m2 va vae rr rrep rr_ps rp k_ps tb  s_ps  c0_ps c0 s1 s2 mx mxx s3
            ex z rz rzx p1 p2 v_ps vs vs_used b_ps b_used pv agg agb o_ps po o_done""")

        grid = lambda ap: ap.rearrange("p (a s w t) -> p a w s t", s=4, w=16, t=4)
        strips = lambda ap: ap.rearrange("p (a s m) -> p a s m", s=4, m=64)
        over_rows = lambda ap, a: ap.rearrange("p (a o w) t -> p a o (w t)", a=a, o=1).broadcast_to([128, a, 4, 64])
        each = lambda ap, n, k: ap.unsqueeze(2).broadcast_to([128, n, k])

        with nc.Block() as block:
            @block.sync
            def _(sp):
                with sp.Fori(0, B // 4) as i:
                    for k in range(2):
                        n = 2 * i + k
                        sp.wait_ge(s["x_used"], n + 1)
                        sp.dma_start(xb[k][:, :], x[bass.ds(n, 1), :, :].rearrange("o p m -> (o p) m")).then_inc(s[f"x_in{k}"], 16)

            @block.gpsimd
            def _(pl):
                pl.memset(half[:, :], -0.5).then_inc(s["half"], 1)
                pl.wait_ge(s["half"], 1)
                with pl.Fori(0, B // 2) as n:
                    pl.wait_ge(s["ve"], n + 1)
                    pl.tensor_tensor(rs[:, :], ve[:, :], half[:, 0:4], ALU.pow).then_inc(s["rs"], 1)
                    pl.wait_ge(s["vae"], n + 1)
                    pl.tensor_tensor(rr[:, :, :].rearrange("p a b -> p (a b)"), va[:, :, :].rearrange("p a b -> p (a b)"),
                                     half[:, 0:64], ALU.pow).then_inc(s["rr"], 1)

            @block.tensor
            def _(pe):
                pe.sem_inc(s["x_used"], 2)
                pe.sem_inc(s["stat_ps"], 1)
                pe.sem_inc(s["s_ps"], 2)
                pe.wait_ge(s["wfold"], 2)
                pe.matmul(misc[:, 0:128], W("center"), wk0[:, :], start=True, stop=True)
                pe.matmul(misc[:, 128:256], W("center"), wv0[:, :], start=True, stop=True)
                pe.matmul(misc[:, 256:257], W("tk"), W("kvb"), start=True, stop=True)
                pe.matmul(misc[:, 257:258], W("tv"), W("kvb"), start=True, stop=True).then_inc(s["wcent"], 1)
                pe.wait_ge(s["wready"], 1)
                with pe.Fori(0, B // 4) as i:
                    for k in range(2):
                        n = 2 * i + k
                        xt = xb[k]
                        pe.wait_ge(s["rf"], n + 1)
                        for j in range(2):
                            mm = pe.transpose(misc[:, 128 * j:128 * j + 128], rf[:, 128 * j:128 * j + 128], W("ident"))
                        mm.then_inc(s["rfT"], 1)
                        pe.wait_ge(s["rt"], n + 1)
                        pe.wait_ge(s["sq"], 4 * n + 4)
                        for q in range(32):
                            pe.matmul(misc[:, 4 * q:4 * q + 2], xt[:, 128 * q:128 * q + 128], W("blk"), start=True, stop=True)
                            mm = pe.matmul(misc[:, 4 * q + 2:4 * q + 4], sq[:, 128 * q:128 * q + 128], W("blk"), start=True, stop=True)
                        mm.then_inc(s["stat_ps"], 1)
                        pe.wait_ge(s["qn"], n + 1)
                        pe.wait_ge(s["st"], n + 1)
                        for j in range(2):
                            mm = pe.transpose(misc[:, 128 * j:128 * j + 128],
                                              qn[:, 2 * j:2 * j + 2, :].rearrange("p a b -> p (a b)"), W("ident"))
                        mm.then_inc(s["qnT_ps"], 1)
                        pe.wait_ge(s["qnT"], n + 1)
                        pe.matmul(misc[:, 0:256], W("tq"), qnT[:, :], start=True, stop=True).then_inc(s["q_ps"], 1)
                        for c in range(CH + 1):
                            if c < CH:
                                pe.wait_ge(s["tb"], CH * n + c + 1)
                                pe.matmul(kps[c % 2][:, :], wk[:, :], xt[:, 512 * c:512 * c + 512], start=True, stop=True).then_inc(s["k_ps"], 1)
                            if c > 0:
                                pe.wait_ge(s["tb"], CH * n + c + 2)
                                if c == 1:
                                    pe.wait_ge(s["s1"], n + 1)
                                pe.matmul(sps[:, :], W("sel", 128 * (c - 1), 128), tb[(c - 1) % 2][:, :],
                                          start=(c == 1), stop=(c == CH)).then_inc(s["s_ps"], 1)
                        pe.wait_ge(s["qx"], n + 1)
                        pe.wait_ge(s["t0"], n + 1)
                        for c in range(CH):
                            mm = pe.matmul(misc[:, 0:32], W("sel", 128 * c, 128), t0[:, 32 * c:32 * c + 32],
                                           start=(c == 0), stop=(c == CH - 1))
                        mm.then_inc(s["c0_ps"], 1)
                        pe.wait_ge(s["c0"], n + 1)
                        pe.wait_ge(s["rrep"], n + 1)
                        for j in range(4):
                            mm = pe.transpose(misc[:, 128 * j:128 * j + 128], rrep[:, j].rearrange("p a b c -> p (a b c)"), W("ident"))
                        mm.then_inc(s["rr_ps"], 1)
                        for c in range(CH):
                            pe.wait_ge(s["vs"], CH * n + c + 1)
                            mm = pe.matmul(vps[c % 2][:, :], wv[:, :], xt[:, 512 * c:512 * c + 512], start=True, stop=True)
                            mm.then_inc(s["v_ps"], 1)
                            if c == 0:
                                pe.wait_ge(s["p2"], n + 1)
                            pe.wait_ge(s["b_used"], CH * n + c + 1)
                            pe.matmul(bps[c % 2][:, :], W("selT", 128 * c, 128), p2[:, :], start=True, stop=True).then_inc(s["b_ps"], 1)
                        pe.wait_ge(s["rp"], n + 1)
                        pe.wait_ge(s["agb"], n + 1)
                        for j in range(2):
                            mm = pe.matmul(misc[:, 128 * j:128 * j + 128], agb[:, 128 * j:128 * j + 128], W("tproj"), start=True, stop=True)
                            mm.then_inc(s["x_used" if j == 0 else "o_ps"], 1)
                        pe.wait_ge(s["po"], n + 1)

            @block.scalar
            def _(act):
                act.sem_inc(s["vs"], 2)
                with act.Fori(0, B // 4) as i:
                    for k in range(2):
                        n = 2 * i + k
                        act.wait_ge(s[f"x_in{k}"], 16 * i + 16)
                        act.wait_ge(s["stat_ps"], n + 1)
                        for q in range(4):
                            act.activation(sq[:, 1024 * q:1024 * q + 1024], xb[k][:, 1024 * q:1024 * q + 1024], ACT.Square).then_inc(s["sq"], 1)
                        act.wait_ge(s["rfT"], n + 1)
                        act.mul(rt[:, :, :].rearrange("p a b -> p (a b)"), misc[:, 0:256], 1 / 16).then_inc(s["rt"], 1)
                        act.wait_ge(s["qnT_ps"], n + 1)
                        act.copy(qnT[:, :], misc[:, 0:256]).then_inc(s["qnT"], 1)
                        act.wait_ge(s["q_ps"], n + 1)
                        act.mul(qx[:, :, :], each(misc[:, 0:256], 256, 4), 1 / 8).then_inc(s["qx"], 1)
                        act.wait_ge(s["rr"], n + 1)
                        for j in range(4):
                            cp = act.copy(rrep[:, j], rr[:, j:32:4, :].unsqueeze(3).broadcast_to([128, CH, 2, 8]))
                        cp.then_inc(s["rrep"], 1)
                        act.wait_ge(s["c0_ps"], n + 1)
                        act.copy(c0[:, :, :], each(misc[:, 0:32], 32, 4)).then_inc(s["c0"], 1)
                        act.wait_ge(s["rr_ps"], n + 1)
                        act.copy(rp[:, :], misc[:, :]).then_inc(s["rp"], 1)
                        act.wait_ge(s["s3"], n + 1)
                        act.activation(ex[:, :], s3[:, :], ACT.Exp).then_inc(s["ex"], 1)
                        for c in range(CH):
                            act.wait_ge(s["v_ps"], CH * n + c + 1)
                            act.wait_ge(s["b_used"], CH * n + c + 1)
                            act.copy(vs[c % 2][:, :], vps[c % 2][:, :]).then_inc(s["vs"], 1)

            @block.vector
            def _(v):
                v.sem_inc(s["tb"], 2)
                v.sem_inc(s["s1"], 1)
                v.sem_inc(s["b_used"], 2)
                v.sem_inc(s["agg"], 2)
                v.tensor_scalar(wk0[:, :], W("tk"), W("kvw"), None, ALU.mult).then_inc(s["wfold"], 1)
                v.tensor_scalar(wv0[:, :], W("tv"), W("kvw"), None, ALU.mult).then_inc(s["wfold"], 1)
                v.wait_ge(s["wcent"], 1)
                v.tensor_copy(wk[:, :], misc[:, 0:128])
                v.tensor_copy(wv[:, :], misc[:, 128:256])
                v.tensor_copy(kb[:, :], misc[:, 256:257])
                v.tensor_copy(vb[:, :], misc[:, 257:258]).then_inc(s["wready"], 1)
                v.wait_ge(s["wready"], 1)
                with v.Fori(0, B // 4) as i:
                    for k in range(2):
                        n = 2 * i + k
                        v.wait_ge(s[f"x_in{k}"], 16 * i + 16)
                        v.tensor_reduce(rf[:, :].rearrange("p (a w) -> p a w", w=16), grid(xb[k][:, :]), AX_XY, ALU.add).then_inc(s["rf"], 1)
                        v.wait_ge(s["rt"], n + 1)
                        v.tensor_reduce(sm[:, :], rt[:, :, :], AX_X, ALU.add).then_inc(s["sm"], 1)
                        v.wait_ge(s["sm"], n + 1)
                        v.tensor_scalar(nm[:, :], sm[:, :], -1 / C, None, ALU.mult).then_inc(s["nm"], 1)
                        v.wait_ge(s["nm"], n + 1)
                        v.tensor_tensor(hc[:, :, :], rt[:, :, :], each(nm[:, :], 4, 64), ALU.add).then_inc(s["hc"], 1)
                        v.wait_ge(s["hc"], n + 1)
                        v.tensor_tensor(hs[:, :, :], hc[:, :, :], hc[:, :, :], ALU.mult).then_inc(s["hs"], 1)
                        v.wait_ge(s["hs"], n + 1)
                        v.tensor_reduce(sm[:, :], hs[:, :, :], AX_X, ALU.add).then_inc(s["ssq"], 1)
                        v.wait_ge(s["ssq"], n + 1)
                        v.tensor_scalar(ve[:, :], sm[:, :], 1 / C, EPS, ALU.mult, ALU.add).then_inc(s["ve"], 1)
                        v.wait_ge(s["rs"], n + 1)
                        v.tensor_tensor(hs[:, :, :], hc[:, :, :], each(rs[:, :], 4, 64), ALU.mult).then_inc(s["hn"], 1)
                        v.wait_ge(s["hn"], n + 1)
                        lnqw, lnqb = (W(m).unsqueeze(1).broadcast_to([128, 4, 64]) for m in ("lnqw", "lnqb"))
                        v.tensor_tensor(hc[:, :, :], hs[:, :, :], lnqw, ALU.mult).then_inc(s["hnw"], 1)
                        v.wait_ge(s["hnw"], n + 1)
                        v.tensor_tensor(qn[:, :, :], hc[:, :, :], lnqb, ALU.add).then_inc(s["qn"], 1)
                        v.wait_ge(s["stat_ps"], n + 2)
                        v.tensor_copy(st[:, :, :], misc[:, 0:128].rearrange("p (a b) -> p a b", b=4)).then_inc(s["st"], 1)
                        v.wait_ge(s["st"], n + 1)
                        v.tensor_tensor(m2[:, :, :], st[:, :, 0:2], st[:, :, 0:2], ALU.mult).then_inc(s["m2"], 1)
                        v.wait_ge(s["m2"], n + 1)
                        v.tensor_tensor(m2[:, :, :], st[:, :, 2:4], m2[:, :, :], ALU.subtract).then_inc(s["va"], 1)
                        v.wait_ge(s["va"], n + 1)
                        v.tensor_scalar(va[:, :, :], m2[:, :, :], 0.0, EPS, ALU.max, ALU.add).then_inc(s["vae"], 1)
                        v.wait_ge(s["qx"], n + 1)
                        v.tensor_scalar(t0[:, :], qx[:, :, 0:1].rearrange("p a b -> p (a b)"), kb[:, :], None, ALU.mult).then_inc(s["t0"], 1)
                        for c in range(CH):
                            v.wait_ge(s["k_ps"], CH * n + c + 1)
                            v.wait_ge(s["s_ps"], CH * n + c + 1)
                            v.tensor_tensor(strips(tb[c % 2][:, :]), strips(kps[c % 2][:, :]), over_rows(qx[:, 32 * c:32 * c + 32, :], 2),
                                            ALU.mult).then_inc(s["tb"], 1)
                        v.wait_ge(s["s_ps"], CH * n + CH + 2)
                        v.wait_ge(s["rp"], n + 1)
                        v.tensor_tensor(s1[:, :], sps[:, :], rp[:, :], ALU.mult).then_inc(s["s1"], 1)
                        v.wait_ge(s["s1"], n + 2)
                        v.wait_ge(s["c0"], n + 1)
                        v.tensor_tensor(strips(s2[:, :]), strips(s1[:, :]), over_rows(c0[:, :, :], 2), ALU.add).then_inc(s["s2"], 1)
                        v.wait_ge(s["s2"], n + 1)
                        v.tensor_reduce(mx[:, :].rearrange("p (a w) -> p a w", w=16), grid(s2[:, :]), AX_XY, ALU.max).then_inc(s["mx"], 1)
                        v.wait_ge(s["mx"], n + 1)
                        v.tensor_copy(mxx[:, :, :], each(mx[:, :], 32, 4)).then_inc(s["mxx"], 1)
                        v.wait_ge(s["mxx"], n + 1)
                        v.tensor_tensor(strips(s3[:, :]), strips(s2[:, :]), over_rows(mxx[:, :, :], 2), ALU.subtract).then_inc(s["s3"], 1)
                        v.wait_ge(s["ex"], n + 1)
                        v.tensor_reduce(z[:, :].rearrange("p (a w) -> p a w", w=16), grid(ex[:, :]), AX_XY, ALU.add).then_inc(s["z"], 1)
                        v.wait_ge(s["z"], n + 1)
                        v.reciprocal(rz[:, :], z[:, :]).then_inc(s["rz"], 1)
                        v.wait_ge(s["rz"], n + 1)
                        v.tensor_copy(rzx[:, :, :], each(rz[:, :], 32, 4)).then_inc(s["rzx"], 1)
                        v.wait_ge(s["rzx"], n + 1)
                        v.tensor_tensor(strips(p1[:, :]), strips(ex[:, :]), over_rows(rzx[:, :, :], 2), ALU.mult).then_inc(s["p1"], 1)
                        v.wait_ge(s["p1"], n + 1)
                        v.tensor_tensor(p2[:, :], p1[:, :], rp[:, :], ALU.mult).then_inc(s["p2"], 1)
                        for c in range(CH):
                            v.wait_ge(s["b_ps"], CH * n + c + 1)
                            v.wait_ge(s["vs"], CH * n + c + 3)
                            v.wait_ge(s["agg"], CH * n + c + 1)
                            v.tensor_tensor(pv[c % 2][:, :], bps[c % 2][:, :], vs[c % 2][:, :], ALU.mult).then_inc(s["b_used"], 1)
                            v.wait_ge(s["b_used"], CH * n + c + 3)
                            v.tensor_reduce(agg[:, 32 * c:32 * c + 32].rearrange("p (a w) -> p a w", w=16), grid(pv[c % 2][:, :]), AX_XY, ALU.add).then_inc(s["agg"], 1)
                        v.wait_ge(s["agg"], CH * n + CH + 2)
                        v.tensor_scalar(agb[:, :], agg[:, :], vb[:, :], None, ALU.add).then_inc(s["agb"], 1)
                        v.wait_ge(s["o_ps"], n + 1)
                        v.tensor_tensor(po[:, :, :], misc[:, 0:256].rearrange("p (a b) -> p a b", b=64), rt[:, :, :], ALU.add).then_inc(s["po"], 1)
                        v.wait_ge(s["po"], n + 1)
                        v.tensor_tensor(h_all[:, bass.ds(6 * n, 6), :].rearrange("p (g j) c -> p j g c", g=2)[:, 0:2],
                                        po[:, :, :].rearrange("p (j g) c -> p j g c", j=2),
                                        W("projb").unsqueeze(1).unsqueeze(1).broadcast_to([128, 2, 2, 64]), ALU.add).then_inc(s["o_done"], 1)


def attention_stage(nc, mem):
    h_all, W = mem["h"], mem["W"]
    Q_PARTS, K_PARTS = (0, 0, 0, 1, 1, 2), (0, 1, 2, 0, 1, 0)
    U = NT * HEADS
    G = U // 4
    with ExitStack() as ctx:
        sb = lambda n, s, d=F32: ctx.enter_context(nc.sbuf_tensor("a_" + n, s, d))
        ps = lambda n, s, d=F32: ctx.enter_context(nc.psum_tensor("a_" + n, s, d))
        half = sb("half", [128, 24])
        lp, ls, le, neglam = sb("lp", [128, 2, 16]), sb("ls", [128, 2]), sb("le", [128, 2]), sb("neglam", [128, 1])
        ld = sb("ld", [128, 1])
        gam, bet = sb("gam", [128, 32]), sb("bet", [128, 32])
        sm, nm, ve, rs = (sb(n, [128, NT]) for n in ("sm", "nm", "ve", "rs"))
        hc, hs = (sb(n, [128, NT, C]) for n in ("hc", "hs"))
        hn = sb("hn", [128, NT + 1, C])
        zero = sb("zero", [128, 1])
        hT = sb("hT", [65, L])
        parts = sb("parts", [128, 4, 3, L], BF16)
        rest = [sb(f"rest{k}", [128, L]) for k in range(2)]
        qe = [sb(f"qe{k}", [96, 16, L], BF16) for k in range(2)]
        ke = [sb(f"ke{k}", [96, 16, L], BF16) for k in range(2)]
        val = [sb(f"val{k}", [128, NT, INNER]) for k in range(2)]
        eg = [sb(f"eg{k}", [128, NT, INNER]) for k in range(2)]
        nmx = sb("nmx", [128, 4, 2])
        E = [sb(f"e{k}", [128, 2, L]) for k in range(3)]
        Z = [sb(f"z{k}", [128, U, 2]) for k in range(2)]
        RZ = [sb(f"rz{k}", [128, U, 2]) for k in range(2)]
        mixc = sb("mixc", [128, 4])
        D = [sb(f"d{k}", [128, L]) for k in range(2)]
        DT = [sb(f"dt{k}", [128, 4, NT, 128]) for k in range(2)]
        oT = [sb(f"oT{k}", [128, 128]) for k in range(2)]
        O = [sb(f"o{k}", [128, NT, HEADS, DV]) for k in range(2)]
        so, no, vo, ro = (sb(n, [128, 24]) for n in ("so", "no", "vo", "ro"))
        oc, o2, on, og, ob, eg1, sg, of = (sb(n, [128, 24, DV]) for n in ("oc", "o2", "on", "og", "ob", "egp", "sg", "of"))
        oF = sb("oF", [128, 2, L])
        hp = sb("hp", [128, NT, C])
        s_ps = [ps(f"s{k}", [128, 2, 512]) for k in range(2)]
        t_ps = [ps(f"t{k}", [128, 512]) for k in range(2)]
        av_ps = ps("av", [128, 512])
        misc = ps("misc", [128, 512])
        scratch = nc.dram_tensor("a_scratch", (3, 2, 16, 16, L), BF16, kind="Internal").ap()
        s = signals(nc, ctx, "a_", """half lp ls le ld neglam gb ones
            sm nm hc hs ssq ve rs hn ht_ps ht qk_ps hi rest mid lo scr qe vg_ps val
            s_ps mx ex rz mixc df t_ps dt av_ps av ot_ps ot
            so no oc o2 sso vo ro on og ob eg1 sg of ft_ps ft op_ps hp h""")
        each = lambda ap, n, k: ap.unsqueeze(2).broadcast_to([128, n, k])
        per_group = lambda ap: ap.unsqueeze(1).broadcast_to([128, 24, DV])
        flat = lambda ap: ap.rearrange("p a b -> p (a b)")
        tiles = lambda n: h_all[:, bass.ds(NT * n, NT), :]

        MISC = {1: ("ot", 5), 4: ("ht", 0), 5: ("ot", 0), 6: ("qk", 0), 7: ("qk", 1), 8: ("qk", 2), 9: ("ot", 1),
                10: ("qk", 3), 11: ("vg", 0), 12: ("vg", 1), 13: ("ot", 2), 14: ("vg", 2), 17: ("ot", 3),
                18: ("ft", 0), 19: ("ft", 1), 20: ("op", 0), 21: ("ot", 4)}

        def bodies(eng, body, prologue, epilogue):
            prologue()
            body(0, 0, True, False)
            with eng.Fori(0, (B - 2) // 2) as i:
                body(2 * i + 1, 1, False, False)
                body(2 * i + 2, 0, False, False)
            body(B - 1, 1, False, True)
            epilogue()

        def tasks(u, first, last):
            if u not in MISC:
                return None
            name, c = MISC[u]
            ahead = 1 if name in ("ht", "qk", "vg") else -1 if name in ("ft", "op") or (name, c) == ("ot", 5) else 0
            if (ahead == 1 and last) or (ahead == -1 and first):
                return None
            return name, c, ahead

        with nc.Block() as block:
            @block.sync
            def _(sp):
                def spread(n, k):
                    sp.wait_ge(s["lo"], 4 * n + 6)
                    for t in range(4):
                        sp.dma_start(scratch[:, t // 2, 8 * (t % 2):8 * (t % 2) + 8].rearrange("q m d n -> (m d) q n"),
                                     parts[:, t]).then_inc(s["scr"], 16)
                    sp.wait_ge(s["scr"], 64 * n + 64)
                    for g in range(6):
                        sp.dma_start(qe[k][16 * g:16 * g + 16, :, :],
                                     scratch[Q_PARTS[g], 0].rearrange("m d n -> d m n")).then_inc(s["qe"], 16)
                        sp.dma_start(ke[k][16 * g:16 * g + 16, :, :],
                                     scratch[K_PARTS[g], 1].rearrange("m d n -> d m n")).then_inc(s["qe"], 16)

                spread(0, 0)
                spread(1, 1)
                with sp.Fori(0, (B - 2) // 2) as i:
                    for k in range(2):
                        spread(2 * i + 2 + k, k)

            @block.gpsimd
            def _(pl):
                def deviation(m):
                    pl.wait_ge(s["ve"], m + 1)
                    pl.tensor_tensor(rs[:, :], ve[:, :], half[:, 0:NT], ALU.pow).then_inc(s["rs"], 1)

                def split(m, c):
                    pl.wait_ge(s["rest"], 4 * m + c + 1)
                    pl.tensor_tensor(parts[:, c, 1, :], rest[c % 2][:, :], zero[:, :].broadcast_to([128, L]), ALU.add).then_inc(s["mid"], 1)
                    pl.wait_ge(s["mid"], 4 * m + c + 1)
                    pl.tensor_tensor(parts[:, c, 2, :], rest[c % 2][:, :], parts[:, c, 1, :], ALU.subtract).then_inc(s["lo"], 1)

                def centre(m, k):
                    pl.wait_ge(s["no"], m + 1)
                    pl.tensor_tensor(oc[:, :, :], O[k][:, :, :, :].rearrange("p a b c -> p (a b) c"), each(no[:, :], 24, DV), ALU.add)\
                        .then_inc(s["oc"], 1)
                    pl.wait_ge(s["oc"], m + 1)
                    pl.tensor_tensor(o2[:, :, :], oc[:, :, :], oc[:, :, :], ALU.mult).then_inc(s["o2"], 1)

                def normed(m):
                    pl.wait_ge(s["vo"], m + 1)
                    pl.tensor_tensor(ro[:, :], vo[:, :], half[:, :], ALU.pow).then_inc(s["ro"], 1)
                    pl.wait_ge(s["ro"], m + 1)
                    pl.tensor_tensor(on[:, :, :], oc[:, :, :], each(ro[:, :], 24, DV), ALU.mult).then_inc(s["on"], 1)

                def gated(m):
                    pl.wait_ge(s["on"], m + 1)
                    pl.tensor_tensor(og[:, :, :], on[:, :, :], per_group(gam[:, :]), ALU.mult).then_inc(s["og"], 1)
                    pl.wait_ge(s["og"], m + 1)
                    pl.tensor_tensor(ob[:, :, :], og[:, :, :], per_group(bet[:, :]), ALU.add).then_inc(s["ob"], 1)
                    pl.wait_ge(s["ob"], m + 1)
                    pl.wait_ge(s["sg"], m + 1)
                    pl.tensor_tensor(of[:, :, :], ob[:, :, :], sg[:, :, :], ALU.mult).then_inc(s["of"], 1)

                def prologue():
                    pl.sem_inc(s["lo"], 2)
                    pl.memset(zero[:, :], 0.0)
                    pl.memset(half[:, :], -0.5).then_inc(s["half"], 1)
                    pl.wait_ge(s["half"], 1)
                    pl.wait_ge(s["gb"], 1)
                    deviation(0)
                    for c in range(4):
                        split(0, c)

                def body(n, k, first, last):
                    if not first:
                        centre(n - 1, 1 - k)
                    if not last:
                        deviation(n + 1)
                        split(n + 1, 0)
                        split(n + 1, 1)
                    if not first:
                        normed(n - 1)
                    if not last:
                        split(n + 1, 2)
                        split(n + 1, 3)
                    if not first:
                        gated(n - 1)

                def epilogue():
                    centre(B - 1, 1)
                    normed(B - 1)
                    gated(B - 1)

                bodies(pl, body, prologue, epilogue)

            @block.tensor
            def _(pe):
                def scores(n, k, u):
                    ic, hd = u // HEADS, u % HEADS
                    pe.wait_ge(s["ex"], U * n + u + 1)
                    for m in range(2):
                        mm = pe.matmul(s_ps[u % 2][:, m, 0:L], qe[k][:, 2 * hd + m, 128 * ic:128 * ic + 128], ke[k][:, 2 * hd + m, :],
                                       start=True, stop=True)
                    mm.then_inc(s["s_ps"], 1)

                def free_misc(name, c, m):
                    total = {"ot": G, "ht": 1, "qk": 4, "vg": NT, "ft": 2, "op": 1}[name]
                    sem = {"ot": "ot", "ht": "ht", "qk": "rest", "vg": "val", "ft": "ft", "op": "hp"}[name]
                    pe.wait_ge(s[sem], total * m + c + 1)

                def task(name, c, m, k):
                    if name == "ht":
                        pe.wait_ge(s["hn"], m + 1)
                        for j in range(NT):
                            mm = pe.transpose(misc[:, 128 * j:128 * j + 128], hn[:, j:j + 2, :].rearrange("p a b -> p (a b)"), W("ident"))
                        mm.then_inc(s["ht_ps"], 1)
                    if name == "qk":
                        if c == 0:
                            pe.wait_ge(s["ht"], m + 1)
                        pe.matmul(misc[:, 0:L], W("aqk", 128 * c, 128, 65), hT[:, :], start=True, stop=True).then_inc(s["qk_ps"], 1)
                    if name == "vg":
                        pe.matmul(misc[:, :], hT[:, 128 * c:128 * c + 128], W("avg", rows=65), start=True, stop=True).then_inc(s["vg_ps"], 1)
                    if name == "ot":
                        pe.wait_ge(s["av"], G * m + c + 2)
                        pe.transpose(misc[:, 0:128], oT[c % 2][:, :], W("ident")).then_inc(s["ot_ps"], 1)
                    if name == "ft":
                        pe.wait_ge(s["of"], m + 1)
                        for j in range(NT):
                            mm = pe.transpose(misc[:, 128 * j:128 * j + 128],
                                              of[:, 8 * j + 4 * c:8 * j + 4 * c + 4, :].rearrange("p a b -> p (a b)"), W("ident"))
                        mm.then_inc(s["ft_ps"], 1)
                    if name == "op":
                        pe.wait_ge(s["ft"], 2 * m + 2)
                        for j in range(NT):
                            for c in range(2):
                                mm = pe.matmul(misc[:, 64 * j:64 * j + 64], oF[:, c, 128 * j:128 * j + 128], W("aout", 64 * c, 64),
                                               start=(c == 0), stop=(c == 1))
                        mm.then_inc(s["op_ps"], 1)

                def prologue():
                    chain = [("ht", 0)] + [("qk", c) for c in range(4)] + [("vg", c) for c in range(NT)]
                    pe.sem_inc(s["t_ps"], 2)
                    pe.sem_inc(s["av_ps"], 2)
                    pe.sem_inc(s["ot_ps"], 2)
                    pe.wait_ge(s["ones"], 1)
                    for j, (name, c) in enumerate(chain):
                        if j:
                            free_misc(*chain[j - 1], 0)
                        task(name, c, 0, 0)
                    free_misc("vg", NT - 1, 0)
                    pe.wait_ge(s["qe"], 192)
                    scores(0, 0, 0)
                    scores(0, 0, 1)

                def body(n, k, first, last):
                    before = ("vg", NT - 1, 0) if first else ("ot", 4, -1)
                    for u in range(U):
                        ic, hd = u // HEADS, u % HEADS
                        if u + 2 < U:
                            scores(n, k, u + 2)
                        elif not last:
                            if u + 2 == U:
                                pe.wait_ge(s["qe"], 192 * n + 384)
                            scores(n + 1, 1 - k, u + 2 - U)
                        pe.wait_ge(s["df"], U * n + u + 4)
                        pe.wait_ge(s["dt"], U * n + u + 1)
                        for j in range(NT):
                            mm = pe.transpose(t_ps[u % 2][:, 128 * j:128 * j + 128], D[u % 2][:, 128 * j:128 * j + 128], W("ident"))
                        mm.then_inc(s["t_ps"], 1)
                        if u % 4 == 3:
                            g = u // 4
                            pe.wait_ge(s["dt"], U * n + u + 3)
                            pe.wait_ge(s["av"], G * n + g + 1)
                            for j in range(NT):
                                for q in range(4):
                                    mm = pe.matmul(av_ps[32 * q:32 * q + 32, 0:128], val[k][:, j, DV * (hd - 3 + q):DV * (hd - 2 + q)],
                                                   DT[g % 2][:, q, j, :], start=(j == 0), stop=(j == NT - 1))
                            mm.then_inc(s["av_ps"], 1)
                        t = tasks(u, first, last)
                        if t:
                            name, c, ahead = t
                            free_misc(before[0], before[1], n + before[2])
                            task(name, c, n + ahead, k)
                            before = (name, c, ahead)

                def epilogue():
                    n, chain = B - 1, [("ot", 5), ("ft", 0), ("ft", 1), ("op", 0)]
                    free_misc("ot", 4, n)
                    for j, (name, c) in enumerate(chain):
                        if j:
                            free_misc(*chain[j - 1], n)
                        task(name, c, n, 1)

                bodies(pe, body, prologue, epilogue)

            @block.scalar
            def _(act):
                def exps(n, k, u):
                    act.wait_ge(s["mx"], U * n + u + 1)
                    act.wait_ge(s["df"], U * n + u + 1)
                    for m in range(2):
                        a = act.activation(E[u % 3][:, m, :], s_ps[u % 2][:, m, 0:L], ACT.Exp, bias=nmx[:, u % 4, m:m + 1],
                                           accum_out=Z[k][:, u, m:m + 1])
                    a.then_inc(s["ex"], 1)

                def output(g, buf):
                    act.wait_ge(s["av_ps"], g + 3)
                    act.wait_ge(s["ot_ps"], g + 1)
                    act.copy(oT[buf][:, :], av_ps[:, 0:128]).then_inc(s["av"], 1)

                def evac(name, c, m, k, ahead=True):
                    if name == "ht":
                        act.wait_ge(s["ht_ps"], m + 1)
                        act.copy(hT[0:64, :], misc[0:64, 0:L]).then_inc(s["ht"], 1)
                    if name == "qk":
                        act.wait_ge(s["qk_ps"], 4 * m + c + 1)
                        if c == 0 and ahead:
                            act.wait_ge(s["scr"], 64 * m)
                        act.mul(parts[:, c, 0, :], misc[:, 0:L], DH ** -0.5 if c < 2 else 1.0).then_inc(s["hi"], 1)
                    if name == "vg":
                        act.wait_ge(s["vg_ps"], NT * m + c + 1)
                        act.copy(val[k][:, c, :], misc[:, 0:INNER])
                        act.activation(eg[k][:, c, :], misc[:, INNER:2 * INNER], ACT.Exp, scale=-1.0).then_inc(s["val"], 1)
                    if name == "ft":
                        act.wait_ge(s["ft_ps"], 2 * m + c + 1)
                        act.copy(oF[:, c, :], misc[:, 0:L]).then_inc(s["ft"], 1)

                def prologue():
                    act.sem_inc(s["ex"], 2)
                    act.sem_inc(s["dt"], 2)
                    act.sem_inc(s["av"], 1)
                    act.wait_ge(s["ls"], 1)
                    act.activation(le[:, :], ls[:, :], ACT.Exp).then_inc(s["le"], 1)
                    for name, c in [("ht", 0)] + [("qk", c) for c in range(4)] + [("vg", c) for c in range(NT)]:
                        evac(name, c, 0, 0, False)
                    exps(0, 0, 0)

                def body(n, k, first, last):
                    for u in range(U):
                        if u == 0 and not first:
                            output(G * n - 1, 1)
                        if u + 1 < U:
                            exps(n, k, u + 1)
                        elif not last:
                            exps(n + 1, 1 - k, 0)
                        act.wait_ge(s["t_ps"], U * n + u + 3)
                        if u % 4 == 0:
                            act.wait_ge(s["av_ps"], G * n + u // 4 + 1)
                        act.copy(DT[(u // 4) % 2][:, u % 4], t_ps[u % 2][:, 0:L].rearrange("p (a b) -> p a b", b=128)).then_inc(s["dt"], 1)
                        if u % 4 == 0 and u:
                            output(G * n + u // 4 - 1, (u // 4 - 1) % 2)
                        t = tasks(u, first, last)
                        if t:
                            name, c, ahead = t
                            evac(name, c, n + ahead, (k + ahead) % 2)

                def epilogue():
                    output(G * B - 1, 1)
                    evac("ft", 0, B - 1, 1)
                    evac("ft", 1, B - 1, 1)

                bodies(act, body, prologue, epilogue)

            @block.vector
            def _(v):
                def maxima(n, u):
                    v.wait_ge(s["s_ps"], U * n + u + 1)
                    v.tensor_reduce(nmx[:, u % 4, :], s_ps[u % 2][:, :, 0:L], AX_X, ALU.max, negate=True).then_inc(s["mx"], 1)

                def norm_a(m):
                    v.tensor_reduce(sm[:, :], tiles(m), AX_X, ALU.add).then_inc(s["sm"], 1)
                    v.wait_ge(s["sm"], m + 1)
                    v.tensor_scalar(nm[:, :], sm[:, :], -1 / C, None, ALU.mult).then_inc(s["nm"], 1)
                    v.wait_ge(s["nm"], m + 1)
                    v.tensor_tensor(hc[:, :, :], tiles(m), each(nm[:, :], NT, C), ALU.add).then_inc(s["hc"], 1)
                    v.wait_ge(s["hc"], m + 1)
                    v.tensor_tensor(hs[:, :, :], hc[:, :, :], hc[:, :, :], ALU.mult).then_inc(s["hs"], 1)
                    v.wait_ge(s["hs"], m + 1)
                    v.tensor_reduce(sm[:, :], hs[:, :, :], AX_X, ALU.add).then_inc(s["ssq"], 1)
                    v.wait_ge(s["ssq"], m + 1)
                    v.tensor_scalar(ve[:, :], sm[:, :], 1 / C, EPS, ALU.mult, ALU.add).then_inc(s["ve"], 1)

                def norm_b(m):
                    v.wait_ge(s["rs"], m + 1)
                    v.tensor_tensor(hn[:, 0:NT, :], hc[:, :, :], each(rs[:, :], NT, C), ALU.mult).then_inc(s["hn"], 1)

                def heads_a(m, k):
                    o = O[k][:, :, :, :].rearrange("p a b c -> p (a b) c")
                    v.wait_ge(s["ot"], G * m + G)
                    v.tensor_reduce(so[:, :], o, AX_X, ALU.add).then_inc(s["so"], 1)
                    v.wait_ge(s["so"], m + 1)
                    v.tensor_scalar(no[:, :], so[:, :], -1 / DV, None, ALU.mult).then_inc(s["no"], 1)
                    e = eg[k][:, :, :].rearrange("p a (b c) -> p (a b) c", c=DV)
                    v.wait_ge(s["val"], NT * m + NT)
                    v.tensor_scalar(eg1[:, :, :], e, 1.0, None, ALU.add).then_inc(s["eg1"], 1)
                    v.wait_ge(s["eg1"], m + 1)
                    v.reciprocal(sg[:, :, :], eg1[:, :, :]).then_inc(s["sg"], 1)

                def heads_b(m):
                    v.wait_ge(s["o2"], m + 1)
                    v.tensor_reduce(so[:, :], o2[:, :, :], AX_X, ALU.add).then_inc(s["sso"], 1)
                    v.wait_ge(s["sso"], m + 1)
                    v.tensor_scalar(vo[:, :], so[:, :], 1 / DV, EPS, ALU.mult, ALU.add).then_inc(s["vo"], 1)

                def evac(name, c, m, k):
                    if name == "qk":
                        v.wait_ge(s["hi"], 4 * m + c + 1)
                        v.wait_ge(s["lo"], 4 * m + c + 1)
                        v.scalar_tensor_tensor(rest[c % 2][:, :], misc[:, 0:L], DH ** -0.5 if c < 2 else 1.0, parts[:, c, 0, :],
                                               ALU.mult, ALU.subtract).then_inc(s["rest"], 1)
                    if name == "ot":
                        ic, hg = c // 2, c % 2
                        v.wait_ge(s["ot_ps"], G * m + c + 3)
                        rz1 = RZ[k][:, 8 * ic + 4 * hg:8 * ic + 4 * hg + 4, 0:1].broadcast_to([128, 4, DV])
                        v.tensor_tensor(O[k][:, ic, 4 * hg:4 * hg + 4, :], misc[:, 0:128].rearrange("p (a b) -> p a b", b=DV), rz1,
                                        ALU.mult).then_inc(s["ot"], 1)
                    if name == "op":
                        v.wait_ge(s["op_ps"], m + 1)
                        v.tensor_tensor(hp[:, :, :], misc[:, 0:NT * C].rearrange("p (a b) -> p a b", b=C), tiles(m), ALU.add).then_inc(s["hp"], 1)
                        v.wait_ge(s["hp"], m + 1)
                        v.tensor_tensor(tiles(m), hp[:, :, :], W("aoutb").unsqueeze(1).broadcast_to([128, NT, C]), ALU.add).then_inc(s["h"], 1)

                def prologue():
                    v.sem_inc(s["df"], 3)
                    v.memset(hn[:, NT, :], 0.0)
                    v.memset(hT[64:65, :], 1.0).then_inc(s["ones"], 1)
                    for j in range(2):
                        v.tensor_tensor(lp[:, j], W("lqk", 32 * j, 16), W("lqk", 32 * j + 16, 16), ALU.mult).then_inc(s["lp"], 1)
                    v.wait_ge(s["lp"], 2)
                    v.tensor_reduce(ls[:, :], lp[:, :, :], AX_X, ALU.add).then_inc(s["ls"], 1)
                    v.tensor_scalar(gam[:, :], W("gam"), 1.0 - LAMBDA_INIT, None, ALU.mult)
                    v.tensor_scalar(bet[:, :], W("bet"), 1.0 - LAMBDA_INIT, None, ALU.mult).then_inc(s["gb"], 1)
                    v.wait_ge(s["le"], 1)
                    v.tensor_tensor(ld[:, :], le[:, 1:2], le[:, 0:1], ALU.subtract).then_inc(s["ld"], 1)
                    v.wait_ge(s["ld"], 1)
                    v.tensor_scalar(neglam[:, :], ld[:, :], -LAMBDA_INIT, None, ALU.add).then_inc(s["neglam"], 1)
                    v.wait_ge(s["neglam"], 1)
                    norm_a(0)
                    norm_b(0)
                    for c in range(4):
                        evac("qk", c, 0, 0)
                    maxima(0, 0)
                    maxima(0, 1)

                def body(n, k, first, last):
                    for u in range(U):
                        N = U * n + u
                        v.wait_ge(s["ex"], N + 3)
                        v.reciprocal(RZ[k][:, u, :], Z[k][:, u, :]).then_inc(s["rz"], 1)
                        v.wait_ge(s["rz"], N + 1)
                        v.scalar_tensor_tensor(mixc[:, u % 4:u % 4 + 1], Z[k][:, u, 0:1], neglam[:, :], RZ[k][:, u, 1:2], ALU.mult, ALU.mult)\
                            .then_inc(s["mixc"], 1)
                        v.wait_ge(s["mixc"], N + 1)
                        v.wait_ge(s["t_ps"], N + 1)
                        v.scalar_tensor_tensor(D[u % 2][:, :], E[u % 3][:, 1, :], mixc[:, u % 4:u % 4 + 1], E[u % 3][:, 0, :], ALU.mult, ALU.add)\
                            .then_inc(s["df"], 1)
                        if u + 2 < U:
                            maxima(n, u + 2)
                        elif not last:
                            maxima(n + 1, u + 2 - U)
                        if u == 1 and not last:
                            norm_a(n + 1)
                        if u == 3 and not last:
                            norm_b(n + 1)
                        t = tasks(u, first, last)
                        if t:
                            name, c, ahead = t
                            evac(name, c, n + ahead, (k + ahead) % 2)
                        if u == 2 and not first:
                            heads_a(n - 1, 1 - k)
                        if u == 6 and not first:
                            heads_b(n - 1)

                def epilogue():
                    evac("ot", 5, B - 1, 1)
                    heads_a(B - 1, 1)
                    heads_b(B - 1)
                    evac("op", 0, B - 1, 1)

                bodies(v, body, prologue, epilogue)


GT = 12


def norm_names():
    return "sm nm hc hs ssq ve rs hn"


def layer_norm(v, s, m, h, t, bufs):
    sm, nm, ve, hc, hs = bufs
    each = lambda ap: ap.unsqueeze(2).broadcast_to([128, t, C])
    v.tensor_reduce(sm[:, :], h, AX_X, ALU.add).then_inc(s["sm"], 1)
    v.wait_ge(s["sm"], m + 1)
    v.tensor_scalar(nm[:, :], sm[:, :], -1 / C, None, ALU.mult).then_inc(s["nm"], 1)
    v.wait_ge(s["nm"], m + 1)
    v.tensor_tensor(hc[:, :, :], h, each(nm[:, :]), ALU.add).then_inc(s["hc"], 1)
    v.wait_ge(s["hc"], m + 1)
    v.tensor_tensor(hs[:, :, :], hc[:, :, :], hc[:, :, :], ALU.mult).then_inc(s["hs"], 1)
    v.wait_ge(s["hs"], m + 1)
    v.tensor_reduce(sm[:, :], hs[:, :, :], AX_X, ALU.add).then_inc(s["ssq"], 1)
    v.wait_ge(s["ssq"], m + 1)
    v.tensor_scalar(ve[:, :], sm[:, :], 1 / C, EPS, ALU.mult, ALU.add).then_inc(s["ve"], 1)


def layer_norm_scale(v, s, m, rs, hc, hn, t):
    v.wait_ge(s["rs"], m + 1)
    v.tensor_tensor(hn, hc[:, :, :], rs[:, :].unsqueeze(2).broadcast_to([128, t, C]), ALU.mult).then_inc(s["hn"], 1)


def gate_buffers(sb, e):
    small = {n: sb("g" + n, [128, GT]) for n in ("m", "z", "rz", "gm", "zs", "rzs")}
    wide = {n: sb("g" + n, [128, GT, e]) for n in ("d", "e", "p", "rank", "sel", "dd", "ee", "es")}
    square = {n: sb("g" + n, [128, GT, e, e]) for n in ("gt", "eq", "el", "rk")}
    return {**small, **wide, **square}


GATE_NAMES = "gm gd ge gz grz gp ggt geq gel grk grank gsel ggm gdd gee ges gzs grzs gw"


def top_two(v, s, m, b, logits, e, tie, w, again):
    each = lambda ap: ap.unsqueeze(2).broadcast_to([128, GT, e])
    v.tensor_reduce(b["m"][:, :], logits, AX_X, ALU.max).then_inc(s["gm"], 1)
    v.wait_ge(s["gm"], m + 1)
    v.tensor_tensor(b["d"][:, :, :], logits, each(b["m"][:, :]), ALU.subtract).then_inc(s["gd"], 1)
    v.wait_ge(s["ge"], m + 1)
    v.tensor_reduce(b["z"][:, :], b["e"][:, :, :], AX_X, ALU.add).then_inc(s["gz"], 1)
    v.wait_ge(s["gz"], m + 1)
    v.reciprocal(b["rz"][:, :], b["z"][:, :]).then_inc(s["grz"], 1)
    v.wait_ge(s["grz"], m + 1)
    p = b["p"]
    v.tensor_tensor(p[:, :, :], b["e"][:, :, :], each(b["rz"][:, :]), ALU.mult).then_inc(s["gp"], 1)
    v.wait_ge(s["gp"], m + 1)
    other = p[:, :, :].unsqueeze(2).broadcast_to([128, GT, e, e])
    own = p[:, :, :].unsqueeze(3).broadcast_to([128, GT, e, e])
    v.tensor_tensor(b["gt"][:, :, :, :], other, own, ALU.is_gt).then_inc(s["ggt"], 1)
    v.tensor_tensor(b["eq"][:, :, :, :], other, own, ALU.is_equal).then_inc(s["geq"], 1)
    v.wait_ge(s["geq"], m + 1)
    v.tensor_tensor(b["el"][:, :, :, :].rearrange("p a b c -> p a (b c)"), b["eq"][:, :, :, :].rearrange("p a b c -> p a (b c)"),
                    tie.unsqueeze(1).broadcast_to([128, GT, e * e]), ALU.mult).then_inc(s["gel"], 1)
    v.wait_ge(s["gel"], m + 1)
    v.tensor_tensor(b["rk"][:, :, :, :], b["el"][:, :, :, :], b["gt"][:, :, :, :], ALU.add).then_inc(s["grk"], 1)
    v.wait_ge(s["grk"], m + 1)
    v.tensor_reduce(b["rank"][:, :, :], b["rk"][:, :, :, :], AX_X, ALU.add).then_inc(s["grank"], 1)
    v.wait_ge(s["grank"], m + 1)
    v.tensor_scalar(b["sel"][:, :, :], b["rank"][:, :, :], 2.0, None, ALU.is_lt).then_inc(s["gsel"], 1)
    if again:
        v.tensor_reduce(b["gm"][:, :], p[:, :, :], AX_X, ALU.max).then_inc(s["ggm"], 1)
        v.wait_ge(s["ggm"], m + 1)
        v.tensor_tensor(b["dd"][:, :, :], p[:, :, :], each(b["gm"][:, :]), ALU.subtract).then_inc(s["gdd"], 1)
        v.wait_ge(s["gee"], m + 1)
        p = b["ee"]
    v.wait_ge(s["gsel"], m + 1)
    v.tensor_tensor(b["es"][:, :, :], p[:, :, :], b["sel"][:, :, :], ALU.mult).then_inc(s["ges"], 1)
    v.wait_ge(s["ges"], m + 1)
    v.tensor_reduce(b["zs"][:, :], b["es"][:, :, :], AX_X, ALU.add).then_inc(s["gzs"], 1)
    v.wait_ge(s["gzs"], m + 1)
    v.reciprocal(b["rzs"][:, :], b["zs"][:, :]).then_inc(s["grzs"], 1)
    v.wait_ge(s["grzs"], m + 1)
    v.tensor_tensor(w, b["es"][:, :, :], each(b["rzs"][:, :]), ALU.mult).then_inc(s["gw"], 1)


def norm_buffers(sb):
    b = {n: sb("n" + n, [128, GT]) for n in ("sm", "nm", "ve", "rs")}
    b["hc"], b["hs"] = sb("nhc", [128, GT, C]), sb("nhs", [128, GT, C])
    b["hn"] = sb("nhn", [128, GT + 1, C])
    b["half"] = sb("nhalf", [128, GT])
    return b


def routing_stage(nc, mem, e, gate_w, tie, again):
    h_all, W, hT_all, w_all = mem["h"], mem["W"], mem["hT"], mem["wts"]
    with ExitStack() as ctx:
        pre = f"r{e}_"
        sb = lambda n, s, d=F32: ctx.enter_context(nc.sbuf_tensor(pre + n, s, d))
        ps = lambda n, s, d=F32: ctx.enter_context(nc.psum_tensor(pre + n, s, d))
        nb, gb = norm_buffers(sb), gate_buffers(sb, e)
        hTg = sb("hTg", [65, GT * 128])
        t_ps, g_ps = ps("t", [128, GT // 4, 512]), ps("g", [128, GT, e])
        s = signals(nc, ctx, pre, "half ones ht_ps ht g_ps kept " + norm_names() + " " + GATE_NAMES)
        bufs = [nb[n] for n in ("sm", "nm", "ve", "hc", "hs")]
        with nc.Block() as block:
            @block.gpsimd
            def _(pl):
                pl.memset(nb["half"][:, :], -0.5).then_inc(s["half"], 1)
                pl.wait_ge(s["half"], 1)
                with pl.Fori(0, TILES // GT) as g:
                    pl.wait_ge(s["ve"], g + 1)
                    pl.tensor_tensor(nb["rs"][:, :], nb["ve"][:, :], nb["half"][:, :], ALU.pow).then_inc(s["rs"], 1)
                    pl.wait_ge(s["ht"], 3 * g + 3)
                    pl.tensor_copy(hT_all[:, bass.ds(GT * 128 * g, GT * 128)], hTg[:, :]).then_inc(s["kept"], 1)

            @block.tensor
            def _(pe):
                pe.wait_ge(s["ones"], 1)
                with pe.Fori(0, TILES // GT) as g:
                    pe.wait_ge(s["hn"], g + 1)
                    for j in range(GT):
                        mm = pe.transpose(t_ps[:, j // 4, 128 * (j % 4):128 * (j % 4) + 128],
                                          nb["hn"][:, j:j + 2, :].rearrange("p a b -> p (a b)"), W("ident"))
                        if j % 4 == 3:
                            mm.then_inc(s["ht_ps"], 1)
                    pe.wait_ge(s["ht"], 3 * g + 3)
                    for j in range(GT):
                        mm = pe.matmul(g_ps[:, j, :], hTg[:, 128 * j:128 * j + 128], W(gate_w, rows=65), start=True, stop=True)
                    mm.then_inc(s["g_ps"], 1)

            @block.scalar
            def _(act):
                
                with act.Fori(0, TILES // GT) as g:
                    for q in range(GT // 4):
                        act.wait_ge(s["ht_ps"], 3 * g + q + 1)
                        act.copy(hTg[0:64, 512 * q:512 * q + 512], t_ps[0:64, q, :]).then_inc(s["ht"], 1)
                    act.wait_ge(s["gd"], g + 1)
                    act.activation(gb["e"][:, :, :], gb["d"][:, :, :], ACT.Exp).then_inc(s["ge"], 1)
                    if again:
                        act.wait_ge(s["gdd"], g + 1)
                        act.activation(gb["ee"][:, :, :], gb["dd"][:, :, :], ACT.Exp).then_inc(s["gee"], 1)
                    act.wait_ge(s["kept"], g + 1)

            @block.vector
            def _(v):
                v.memset(nb["hn"][:, GT, :], 0.0)
                v.memset(hTg[64:65, :], 1.0).then_inc(s["ones"], 1)
                v.wait_ge(s["ones"], 1)
                with v.Fori(0, TILES // GT) as g:
                    layer_norm(v, s, g, h_all[:, bass.ds(GT * g, GT), :], GT, bufs)
                    layer_norm_scale(v, s, g, nb["rs"], nb["hc"], nb["hn"][:, 0:GT, :], GT)
                    v.wait_ge(s["g_ps"], g + 1)
                    top_two(v, s, g, gb, g_ps[:, :, :], e, W(tie), w_all[:, bass.ds(GT * g, GT), 0:e], again)


def batches(eng, body, epilogue):
    body(0, 0, True)
    with eng.Fori(0, (B - 2) // 2) as i:
        body(2 * i + 1, 1, False)
        body(2 * i + 2, 0, False)
    body(B - 1, 1, False)
    epilogue()


def experts_stage(nc, mem):
    h_all, W, hT_all, w_all = mem["h"], mem["W"], mem["hT"], mem["wts"]
    with ExitStack() as ctx:
        sb = lambda n, s, d=F32: ctx.enter_context(nc.sbuf_tensor("f_" + n, s, d))
        ps = lambda n, s, d=F32: ctx.enter_context(nc.psum_tensor("f_" + n, s, d))
        h1 = [sb(f"h1{k}", [128, L]) for k in range(2)]
        sh1, sh2 = sb("sh1", [128, L]), sb("sh2", [128, L])
        h2 = [sb(f"h2{k}", [128, L]) for k in range(2)]
        ob, ow = sb("ob", [128, NT, 320]), sb("ow", [128, NT, E0, C])
        osum, hp = sb("osum", [128, NT, C]), sb("hp", [128, NT, C])
        l1 = [ps(f"l1{k}", [128, 512]) for k in range(2)]
        l2 = ps("l2", [128, 512])
        ops = [ps(f"o{k}", [128, 512]) for k in range(NT)]
        s = signals(nc, ctx, "f_", "l1_ps h1 l2_ps h2 o_ps ob ow osum hp h")
        tiles = lambda ap, n: ap[:, bass.ds(NT * n, NT), :]

        with nc.Block() as block:
            @block.gpsimd
            def _(pl):
                def weigh(n):
                    pl.wait_ge(s["ob"], n + 2)
                    pl.tensor_tensor(ow[:, :, :, :], ob[:, :, 0:256].rearrange("p a (e c) -> p a e c", c=C),
                                     tiles(w_all, n)[:, :, 0:E0].unsqueeze(3).broadcast_to([128, NT, E0, C]), ALU.mult).then_inc(s["ow"], 1)
                batches(pl, lambda n, k, first: None if first else weigh(n - 1), lambda: weigh(B - 1))

            @block.tensor
            def _(pe):
                def body(n, k, first):
                    x = hT_all[:, bass.ds(L * n, L)]
                    for e in range(6):
                        if e < 5:
                            pe.wait_ge(s["h1"], 5 * n + (2 if e == 0 else e + 1))
                            w1 = W("ew1", 128 * e, 128, 65) if e < 4 else W("sw1", rows=65)
                            pe.matmul(l1[e % 2][:, 0:L], w1, x, start=True, stop=True).then_inc(s["l1_ps"], 1)
                        if e > 0:
                            q = e - 1
                            pe.wait_ge(s["h1"], 5 * n + q + 3)
                            if q % 2 == 0:
                                pe.wait_ge(s["h2"], 3 * n + q // 2 + 1)
                            if q < 4:
                                mm = pe.matmul(l2[64 * (q % 2):64 * (q % 2) + 64, 0:L], W("ew2", 64 * q, 64), h1[q % 2][:, :], start=True, stop=True)
                            else:
                                mm = pe.matmul(l2[:, 0:L], W("sw2"), sh1[:, :], start=True, stop=True)
                            mm.then_inc(s["l2_ps"], 1)
                    pe.wait_ge(s["h2"], 3 * n + 4)
                    pe.wait_ge(s["ob"], n + 1)
                    for j in range(NT):
                        t = slice(128 * j, 128 * j + 128)
                        for q in range(2):
                            pe.matmul(ops[j][:, 128 * q:128 * q + 128], h2[q][:, t], W("ew3", 128 * q, 128), start=True, stop=True)
                        mm = pe.matmul(ops[j][:, 256:320], sh2[:, t], W("sw3"), start=True, stop=True)
                    mm.then_inc(s["o_ps"], 1)
                batches(pe, body, lambda: None)

            @block.scalar
            def _(act):
                act.sem_inc(s["h1"], 2)
                act.sem_inc(s["h2"], 1)

                def first_layer(n, e):
                    act.wait_ge(s["l1_ps"], 5 * n + e + 1)
                    if e in (2, 3):
                        act.wait_ge(s["l2_ps"], 5 * n + e - 1)
                    dst = sh1 if e == 4 else h1[e % 2]
                    act.activation(dst[:, :], l1[e % 2][:, 0:L], ACT.Relu).then_inc(s["h1"], 1)

                def second_layer(n, q):
                    act.wait_ge(s["l2_ps"], 5 * n + (2, 4, 5)[q])
                    dst, bias = (sh2, W("sb2")) if q == 2 else (h2[q], W("eb2", q, 1))
                    act.activation(dst[:, :], l2[:, 0:L], ACT.Relu, bias=bias).then_inc(s["h2"], 1)

                def body(n, k, first):
                    for e in range(3):
                        first_layer(n, e)
                    second_layer(n, 0)
                    first_layer(n, 3)
                    first_layer(n, 4)
                    second_layer(n, 1)
                    second_layer(n, 2)
                batches(act, body, lambda: None)

            @block.vector
            def _(v):
                v.sem_inc(s["ob"], 1)

                def combine(n):
                    v.wait_ge(s["o_ps"], n + 1)
                    for j in range(NT):
                        o = v.tensor_tensor(ob[:, j, :], ops[j][:, 0:320], W("b30"), ALU.add)
                    o.then_inc(s["ob"], 1)
                    v.wait_ge(s["ow"], n + 1)
                    v.tensor_reduce(osum[:, :, :], ow[:, :, :, :].rearrange("p a e c -> p a c e"), AX_X, ALU.add).then_inc(s["osum"], 1)
                    v.wait_ge(s["osum"], n + 1)
                    v.tensor_tensor(hp[:, :, :], osum[:, :, :], ob[:, :, 256:320], ALU.add).then_inc(s["hp"], 1)
                    v.wait_ge(s["hp"], n + 1)
                    v.tensor_tensor(tiles(h_all, n), tiles(h_all, n), hp[:, :, :], ALU.add).then_inc(s["h"], 1)
                batches(v, lambda n, k, first: None if first else combine(n - 1), lambda: combine(B - 1))


def gate_stage(nc, mem):
    h_all, W = mem["h"], mem["W"]
    with ExitStack() as ctx:
        sb = lambda n, s, d=F32: ctx.enter_context(nc.sbuf_tensor("g_" + n, s, d))
        ps = lambda n, s, d=F32: ctx.enter_context(nc.psum_tensor("g_" + n, s, d))
        nb = norm_buffers(sb)
        hTg = sb("hTg", [64, GT * 128])
        eg, e1, sg, y = (sb(n, [64, GT // 4, 512]) for n in ("eg", "e1", "sg", "y"))
        hp = sb("hp", [128, GT, C])
        t_ps, g_ps = ps("t", [128, GT // 4, 512]), ps("g", [128, GT // 4, 512])
        o_ps = ps("o", [128, 2, 512])
        s = signals(nc, ctx, "g_", "half zeroed ht_ps ht g_ps eg e1 sg y o_ps hp h " + norm_names())
        bufs = [nb[n] for n in ("sm", "nm", "ve", "hc", "hs")]
        with nc.Block() as block:
            @block.gpsimd
            def _(pl):
                pl.memset(nb["half"][:, :], -0.5).then_inc(s["half"], 1)
                pl.wait_ge(s["half"], 1)
                with pl.Fori(0, TILES // GT) as g:
                    pl.wait_ge(s["ve"], g + 1)
                    pl.tensor_tensor(nb["rs"][:, :], nb["ve"][:, :], nb["half"][:, :], ALU.pow).then_inc(s["rs"], 1)

            @block.tensor
            def _(pe):
                pe.wait_ge(s["zeroed"], 1)
                with pe.Fori(0, TILES // GT) as g:
                    pe.wait_ge(s["hn"], g + 1)
                    for j in range(GT):
                        mm = pe.transpose(t_ps[:, j // 4, 128 * (j % 4):128 * (j % 4) + 128],
                                          nb["hn"][:, j:j + 2, :].rearrange("p a b -> p (a b)"), W("ident"))
                        if j % 4 == 3:
                            mm.then_inc(s["ht_ps"], 1)
                    for q in range(GT // 4):
                        pe.wait_ge(s["ht"], 3 * g + q + 1)
                        pe.matmul(g_ps[:, q, :], W("glg", 0, 128, 64), hTg[:, 512 * q:512 * q + 512], start=True, stop=True).then_inc(s["g_ps"], 1)
                    pe.wait_ge(s["y"], g + 1)
                    for j in range(GT):
                        mm = pe.matmul(o_ps[:, j // 6, 64 * (j % 6):64 * (j % 6) + 64], y[:, j // 4, 128 * (j % 4):128 * (j % 4) + 128],
                                       W("glo", rows=64), start=True, stop=True)
                    mm.then_inc(s["o_ps"], 1)

            @block.scalar
            def _(act):
                with act.Fori(0, TILES // GT) as g:
                    for q in range(GT // 4):
                        act.wait_ge(s["ht_ps"], 3 * g + q + 1)
                        act.copy(hTg[:, 512 * q:512 * q + 512], t_ps[0:64, q, :]).then_inc(s["ht"], 1)
                    for q in range(GT // 4):
                        act.wait_ge(s["g_ps"], 3 * g + q + 1)
                        act.activation(eg[:, q, :], g_ps[0:64, q, :], ACT.Exp, scale=-1.0).then_inc(s["eg"], 1)

            @block.vector
            def _(v):
                v.memset(nb["hn"][:, GT, :], 0.0).then_inc(s["zeroed"], 1)
                v.wait_ge(s["zeroed"], 1)
                with v.Fori(0, TILES // GT) as g:
                    h = h_all[:, bass.ds(GT * g, GT), :]
                    layer_norm(v, s, g, h, GT, bufs)
                    layer_norm_scale(v, s, g, nb["rs"], nb["hc"], nb["hn"][:, 0:GT, :], GT)
                    v.wait_ge(s["eg"], 3 * g + 3)
                    v.tensor_scalar(e1[:, :, :], eg[:, :, :], 1.0, None, ALU.add).then_inc(s["e1"], 1)
                    v.wait_ge(s["e1"], g + 1)
                    v.reciprocal(sg[:, :, :], e1[:, :, :]).then_inc(s["sg"], 1)
                    v.wait_ge(s["sg"], g + 1)
                    v.scalar_tensor_tensor(y[:, :, :], g_ps[0:64, :, :], W("gnb", rows=64), sg[:, :, :], ALU.mult, ALU.mult).then_inc(s["y"], 1)
                    v.wait_ge(s["o_ps"], g + 1)
                    v.tensor_tensor(hp[:, :, :].rearrange("p (a b) c -> p a (b c)", a=2), o_ps[:, :, 0:384],
                                    h.rearrange("p (a b) c -> p a (b c)", a=2), ALU.add).then_inc(s["hp"], 1)
                    v.wait_ge(s["hp"], g + 1)
                    v.tensor_tensor(h, hp[:, :, :], W("glb").unsqueeze(1).broadcast_to([128, GT, C]), ALU.add).then_inc(s["h"], 1)


def gelu_experts_stage(nc, mem):
    h_all, W, hT_all, w_all = mem["h"], mem["W"], mem["hT"], mem["wts"]
    NE = E1 + 1
    with ExitStack() as ctx:
        sb = lambda n, s, d=F32: ctx.enter_context(nc.sbuf_tensor("x_" + n, s, d))
        ps = lambda n, s, d=F32: ctx.enter_context(nc.psum_tensor("x_" + n, s, d))
        act1 = [sb(f"act{k}", [128, 2, L]) for k in range(3)]
        ob, ow = sb("ob", [128, NT, NE * C]), sb("ow", [128, NT, E1, C])
        osum, hp = sb("osum", [128, NT, C]), sb("hp", [128, NT, C])
        l1 = [ps(f"l1{k}", [128, 2, 512]) for k in range(2)]
        ops = [ps(f"o{k}", [128, 512]) for k in range(NT)]
        shared = ps("shared", [128, NT, C])
        s = signals(nc, ctx, "x_", "l1_ps act l2_ps ob ow osum hp h")
        tiles = lambda ap, n: ap[:, bass.ds(NT * n, NT), :]

        with nc.Block() as block:
            @block.gpsimd
            def _(pl):
                def weigh(n):
                    pl.wait_ge(s["ob"], n + 2)
                    pl.tensor_tensor(ow[:, :, :, :], ob[:, :, 0:E1 * C].rearrange("p a (e c) -> p a e c", c=C),
                                     tiles(w_all, n)[:, :, 0:E1].unsqueeze(3).broadcast_to([128, NT, E1, C]), ALU.mult).then_inc(s["ow"], 1)
                batches(pl, lambda n, k, first: None if first else weigh(n - 1), lambda: weigh(B - 1))

            @block.tensor
            def _(pe):
                pe.sem_inc(s["l2_ps"], 3)

                def body(n, k, first):
                    x = hT_all[:, bass.ds(L * n, L)]
                    for e in range(NE + 1):
                        if e < NE:
                            pe.wait_ge(s["act"], NE * n + (2 if e == 0 else e + 1))
                            for f in range(2):
                                mm = pe.matmul(l1[e % 2][:, f, 0:L], W("w1", F1 * e + 128 * f, 128, 65), x, start=True, stop=True)
                            mm.then_inc(s["l1_ps"], 1)
                        if e > 0:
                            q = e - 1
                            pe.wait_ge(s["act"], NE * n + q + 3)
                            if q == 0:
                                pe.wait_ge(s["ob"], n + 1)
                            for j in range(NT):
                                dst = ops[j][:, C * q:C * q + C] if q < E1 else shared[:, j, :]
                                for f in range(2):
                                    mm = pe.matmul(dst, act1[q % 3][:, f, 128 * j:128 * j + 128], W("w2", 128 * q + C * f, C),
                                                   start=(f == 0), stop=(f == 1))
                            mm.then_inc(s["l2_ps"], 1)
                batches(pe, body, lambda: None)

            @block.scalar
            def _(act):
                act.sem_inc(s["act"], 2)

                def body(n, k, first):
                    for e in range(NE):
                        act.wait_ge(s["l1_ps"], NE * n + e + 1)
                        act.wait_ge(s["l2_ps"], NE * n + e + 1)
                        act.activation(act1[e % 3][:, :, :], l1[e % 2][:, :, 0:L], ACT.Gelu).then_inc(s["act"], 1)
                batches(act, body, lambda: None)

            @block.vector
            def _(v):
                v.sem_inc(s["ob"], 1)

                def combine(n):
                    v.wait_ge(s["l2_ps"], NE * n + NE + 3)
                    for j in range(NT):
                        v.tensor_tensor(ob[:, j, 0:E1 * C], ops[j][:, :], W("b21", 0, E1 * C), ALU.add)
                    v.tensor_tensor(ob[:, :, E1 * C:NE * C], shared[:, :, :], W("b21", E1 * C, C).unsqueeze(1).broadcast_to([128, NT, C]), ALU.add)\
                        .then_inc(s["ob"], 1)
                    v.wait_ge(s["ow"], n + 1)
                    v.tensor_reduce(osum[:, :, :], ow[:, :, :, :].rearrange("p a e c -> p a c e"), AX_X, ALU.add).then_inc(s["osum"], 1)
                    v.wait_ge(s["osum"], n + 1)
                    v.tensor_tensor(hp[:, :, :], osum[:, :, :], ob[:, :, E1 * C:NE * C], ALU.add).then_inc(s["hp"], 1)
                    v.wait_ge(s["hp"], n + 1)
                    v.tensor_tensor(tiles(h_all, n), tiles(h_all, n), hp[:, :, :], ALU.add).then_inc(s["h"], 1)
                batches(v, lambda n, k, first: None if first else combine(n - 1), lambda: combine(B - 1))


def early_fusion_program(nc, x, txt, pack, out):
    with ExitStack() as ctx:
        w = ctx.enter_context(nc.sbuf_tensor("w", [128, WCOLS], F32))
        h = ctx.enter_context(nc.sbuf_tensor("h", [128, TILES, C], F32))

        def W(name, col=0, cols=None, rows=128):
            at, width = AT[name]
            return w[0:rows, at + col:at + col + (width if cols is None else cols)]

        mem = {"w": w, "h": h, "W": W}
        load_stage(nc, mem, pack, txt)
        tok_stage(nc, mem, x)
        attention_stage(nc, mem)
        with (nc.sbuf_tensor("hT", [65, B * L], F32) as hT, nc.sbuf_tensor("wts", [128, TILES, E1], F32) as wts):
            mem["hT"], mem["wts"] = hT, wts
            routing_stage(nc, mem, E0, "gw", "tie0", True)
            experts_stage(nc, mem)
            gate_stage(nc, mem)
            routing_stage(nc, mem, E1, "wr", "tie1", False)
            gelu_experts_stage(nc, mem)
        store_stage(nc, mem, out)


def kernel(**inputs):
    import numpy as np
    import concourse.bacc as _bacc
    from concourse import mybir as _mybir
    from concourse.bass_utils import run_bass_kernel_spmd as _run

    f32 = np.float32
    w = {k: np.ascontiguousarray(v) for k, v in inputs.items()}
    pack = np.zeros((128, WCOLS), f32)

    def put(name, value, row=0, col=0):
        at, _ = AT[name]
        value = value.reshape(value.shape[0], -1)
        pack[row:row + value.shape[0], at + col:at + col + value.shape[1]] = value

    def rows(name, vector, col=0):
        put(name, np.broadcast_to(vector.reshape(1, -1), (128, vector.size)), 0, col)

    def twice(name, block):
        put(name, block)
        put(name, block, 64, 64)

    put("ident", np.eye(128, dtype=f32))
    head_of = np.repeat(np.eye(16, dtype=f32), 8, axis=0)
    full = np.zeros((128, 8, 8, 16), f32)
    for c in range(8):
        full[:, c, c, :] = head_of
    put("sel", full)
    put("selT", full.reshape(128, 8, 128).transpose(2, 1, 0))
    center = np.eye(64, dtype=f32) - np.full((64, 64), 1 / 64, f32)
    twice("center", center)
    put("blk", np.full((64, 1), 1 / 64, f32), 0, 0)
    put("blk", np.full((64, 1), 1 / 64, f32), 64, 1)
    lower = lambda n: np.array([[1.0 if j < i else 0.0 for j in range(n)] for i in range(n)], f32)
    rows("tie0", lower(E0))
    rows("tie1", lower(E1))
    twice("tq", w["L0_tok_Wq"].T)
    twice("tk", w["L0_tok_Wkv"][:64].T)
    twice("tv", w["L0_tok_Wkv"][64:].T)
    twice("tproj", w["L0_tok_proj_w"].T)
    for r in (0, 64):
        put("kvw", w["L0_tok_ln_kv_w"][:, None], r)
        put("kvb", w["L0_tok_ln_kv_b"][:, None], r)
    rows("lnqw", w["L0_tok_ln_q_w"])
    rows("lnqb", w["L0_tok_ln_q_b"])
    rows("projb", w["L0_tok_proj_b"])
    put("aqk", w["L0_attn_Wq"])
    put("aqk", w["L0_attn_Wkv"][:, :INNER], 0, INNER)
    put("avg", w["L0_attn_Wkv"][:, INNER:])
    put("avg", w["L0_attn_Wg"], 0, INNER)
    put("avg", w["L0_attn_bg"][None], 64, INNER)
    put("aout", w["L0_attn_Wout"][:128])
    put("aout", w["L0_attn_Wout"][128:], 0, 64)
    rows("aoutb", w["L0_attn_bout"])
    rows("gam", w["L0_attn_ln_gamma"])
    rows("bet", w["L0_attn_ln_beta"])
    for i, n in enumerate(("lq1", "lk1", "lq2", "lk2")):
        rows("lqk", w["L0_attn_" + n], 16 * i)
    put("sw1", w["L0_ffn_sW1"])
    put("sw1", w["L0_ffn_sb1"][None], 64)
    put("ew1", w["L0_ffn_eW1"].transpose(1, 0, 2))
    put("ew1", w["L0_ffn_eb1"].reshape(1, -1), 64)
    put("gw", w["L0_ffn_gW"])
    put("gw", w["L0_ffn_gb"][None], 64)
    put("sw2", w["L0_ffn_sW2"])
    put("sb2", w["L0_ffn_sb2"][:, None])
    put("sw3", w["L0_ffn_sW3"])
    put("ew2", w["L0_ffn_eW2"].transpose(1, 0, 2))
    put("eb2", w["L0_ffn_eb2"].reshape(2, 128).T)
    for p in range(2):
        put("ew3", w["L0_ffn_eW3"][2 * p], 0, 128 * p)
        put("ew3", w["L0_ffn_eW3"][2 * p + 1], 64, 128 * p + 64)
    rows("b30", w["L0_ffn_eb3"].reshape(-1))
    rows("b30", w["L0_ffn_sb3"], 256)
    put("glg", w["L1_attn_wg"])
    put("glo", w["L1_attn_wo"])
    put("gnb", w["L1_attn_gn_bias"][:, None])
    rows("glb", w["L1_attn_bias"])
    put("wr", w["L1_ffn_Wr"])
    put("w1", w["L1_ffn_W1p"].transpose(1, 0, 2))
    put("w1", w["L1_ffn_b1p"].reshape(1, -1), 64)
    put("w1", w["L1_ffn_W1s"], 0, 8 * F1)
    put("w1", w["L1_ffn_b1s"][None], 64, 8 * F1)
    put("w2", w["L1_ffn_W2p"].reshape(8, 2, 128, 64).transpose(2, 0, 1, 3))
    put("w2", w["L1_ffn_W2s"].reshape(2, 128, 64).transpose(1, 0, 2), 0, 8 * 128)
    rows("b21", w["L1_ffn_b2p"].reshape(-1))
    rows("b21", w["L1_ffn_b2s"], 512)

    arrays = {"x": w["x"].reshape(B // 2, 128, IMG * IMG), "txt": w["txt"], "pack": pack}
    nc = _bacc.Bacc("TRN2", target_bir_lowering=False, num_devices=1)
    args = [nc.dram_tensor(f"{k}_dram", a.shape, _mybir.dt.from_np(a.dtype), kind="ExternalInput").ap()
            for k, a in arrays.items()]
    args.append(nc.dram_tensor("out_dram", (B, L, C), _mybir.dt.float32, kind="ExternalOutput").ap())
    early_fusion_program(nc, *args)
    r = _run(nc, [{f"{k}_dram": a for k, a in arrays.items()}], core_ids=[0])
    return r.results[0]["out_dram"]
```

```python
import math
from contextlib import ExitStack

import concourse.bass as bass
from concourse import mybir

B, C, IMG = 32, 64, 64
TXT = 128
STRIDE, TOK_HEADS = 4, 8
SIDE = IMG // STRIDE
PATCHES = SIDE * SIDE
L = PATCHES + TXT
NT = L // 128
TILES = B * NT
HEADS, DH = 8, 16
DV = 2 * DH
INNER = HEADS * DV
E0, E0_H1, E0_H2, S0_H1, S0_H2 = 4, 128, 64, 64, 128
E1, F1 = 8, 256
EPS = 1e-5
LAMBDA_INIT = 0.8 - 0.6 * math.exp(-0.3)

FIELDS = [
    ("ident", 128), ("sel", 1024), ("selT", 1024), ("center", 128), ("blk", 128),
    ("tq", 128), ("tk", 128), ("tv", 128), ("tproj", 128), ("kvw", 1), ("kvb", 1),
    ("lnqw", 64), ("lnqb", 64), ("projb", 64),
    ("aqk", 512), ("avg", 512), ("aout", 128), ("aoutb", 64), ("gam", 32), ("bet", 32), ("lqk", 64),
    ("sw1", 128), ("ew1", 512), ("gw", 4), ("sw2", 128), ("sb2", 1), ("sw3", 64), ("ew2", 256), ("eb2", 2),
    ("ew3", 128), ("bias0", 64), ("pick0", 256), ("both", 64), ("tie0", 16),
    ("glg", 64), ("glo", 64), ("gnb", 1),
    ("wr", 8), ("w1", 9 * F1), ("w2", 9 * 128), ("bias1", 64), ("pick1", 1024), ("tie1", 64),
]
AT = {}
_n = 0
for _name, _w in FIELDS:
    AT[_name] = (_n, _w)
    _n += _w
WCOLS = _n


F32 = mybir.dt.float32
BF16 = mybir.dt.bfloat16
ALU = mybir.AluOpType
ACT = mybir.ActivationFunctionType
AX_X, AX_XY = mybir.AxisListType.X, mybir.AxisListType.XY


def signals(nc, ctx, prefix, names):
    sems = {n: nc.alloc_semaphore(name=prefix + n) for n in names.split()}

    def clear():
        nc.clear_and_free_semaphores(list(sems.values()))
        nc.all_engine_barrier()

    ctx.callback(clear)
    return sems


def load_stage(nc, mem, pack, txt):
    with nc.semaphore("loaded") as loaded, nc.Block() as block:
        @block.sync
        def _(sp):
            sp.dma_start(mem["w"][:, :], pack).then_inc(loaded, 16)
            sp.dma_start(mem["h"][:, 2:TILES:NT, :], txt.rearrange("b l d -> l b d")).then_inc(loaded, 16)
            sp.wait_ge(loaded, 32)


def store_stage(nc, mem, out):
    with nc.semaphore("stored") as stored, nc.Block() as block:
        @block.sync
        def _(sp):
            sp.dma_start(out.rearrange("b (j p) c -> p (b j) c", p=128), mem["h"][:, :, :]).then_inc(stored, 16)
            sp.wait_ge(stored, 16)


def tok_stage(nc, mem, x):
    h_all, W = mem["h"], mem["W"]
    CH = 8
    with ExitStack() as ctx:
        sb = lambda n, s, d=F32: ctx.enter_context(nc.sbuf_tensor("t_" + n, s, d))
        ps = lambda n, s, d=F32: ctx.enter_context(nc.psum_tensor("t_" + n, s, d))
        xb = [sb(f"x{k}", [128, 4096]) for k in range(2)]
        sq = sb("sq", [128, 4096])
        wk, wv = sb("wk", [128, 128]), sb("wv", [128, 128])
        wk0, wv0 = sb("wk0", [128, 128]), sb("wv0", [128, 128])
        kb, vb = sb("kb", [128, 1]), sb("vb", [128, 1])
        half = sb("half", [128, 64])
        rf = sb("rf", [128, PATCHES])
        rt = sb("rt", [128, 4, 64])
        hc, hs, qn = sb("hc", [128, 4, 64]), sb("hs", [128, 4, 64]), sb("qn", [128, 4, 64])
        sm, nm, ve, rs = (sb(n, [128, 4]) for n in ("sm", "nm", "ve", "rs"))
        qnT = sb("qnT", [128, 256])
        qx = sb("qx", [128, 256, 4])
        t0 = sb("t0", [128, 256])
        tb = [sb(f"tb{k}", [128, 512]) for k in range(2)]
        stT = sb("stT", [128, 512])
        st = sb("st", [128, 4, 4, 8])
        m2, va, rr = (sb(n, [128, 4, 2, 8]) for n in ("m2", "va", "rr"))
        rrep = sb("rrep", [128, 4, 8, 2, 8])
        rp = sb("rp", [128, 512])
        c0 = sb("c0", [128, 32, 4])
        s1, s2, s3, ex, p1, p2 = (sb(n, [128, 512]) for n in ("s1", "s2", "s3", "ex", "p1", "p2"))
        mx, z, rz = (sb(n, [128, 32]) for n in ("mx", "z", "rz"))
        mxx, rzx = sb("mxx", [128, 32, 4]), sb("rzx", [128, 32, 4])
        vs = [sb(f"vs{k}", [128, 512]) for k in range(2)]
        pv = [sb(f"pv{k}", [128, 512]) for k in range(2)]
        agg, agb = sb("agg", [128, 256]), sb("agb", [128, 256])
        po = sb("po", [128, 4, 64])
        misc = ps("misc", [128, 512])
        kps = [ps(f"k{k}", [128, 512]) for k in range(2)]
        sps = ps("s", [128, 512])
        vps = [ps(f"v{k}", [128, 512]) for k in range(2)]
        bps = [ps(f"b{k}", [128, 512]) for k in range(2)]
        s = signals(nc, ctx, "t_", """wfold wcent wready half x_in0 x_in1 x_used rf rfT rt sm nm hc hs ssq ve rs hn hnw qn qnT_ps qnT
            q_ps qx t0 sq stat_mm stT stat_ps st m2 va vae rr rrep rr_ps rp k_ps tb  s_ps  c0_ps c0 s1 s2 mx mxx s3
            ex z rz rzx p1 p2 v_ps vs vs_used b_ps b_used pv agg agb o_ps po o_done""")

        grid = lambda ap: ap.rearrange("p (a s w t) -> p a w s t", s=4, w=16, t=4)
        strips = lambda ap: ap.rearrange("p (a s m) -> p a s m", s=4, m=64)
        over_rows = lambda ap, a: ap.rearrange("p (a o w) t -> p a o (w t)", a=a, o=1).broadcast_to([128, a, 4, 64])
        each = lambda ap, n, k: ap.unsqueeze(2).broadcast_to([128, n, k])

        with nc.Block() as block:
            @block.sync
            def _(sp):
                with sp.Fori(0, B // 4) as i:
                    for k in range(2):
                        n = 2 * i + k
                        sp.wait_ge(s["x_used"], n + 1)
                        sp.dma_start(xb[k][:, :], x[bass.ds(n, 1), :, :].rearrange("o p m -> (o p) m")).then_inc(s[f"x_in{k}"], 16)

            @block.gpsimd
            def _(pl):
                pl.memset(half[:, :], -0.5).then_inc(s["half"], 1)
                pl.wait_ge(s["half"], 1)
                with pl.Fori(0, B // 2) as n:
                    pl.wait_ge(s["ve"], n + 1)
                    pl.tensor_tensor(rs[:, :], ve[:, :], half[:, 0:4], ALU.pow).then_inc(s["rs"], 1)
                    pl.wait_ge(s["vae"], n + 1)
                    pl.tensor_tensor(rr[:, :, :, :].rearrange("p a b c -> p (a b c)"), va[:, :, :, :].rearrange("p a b c -> p (a b c)"),
                                     half[:, 0:64], ALU.pow).then_inc(s["rr"], 1)

            @block.tensor
            def _(pe):
                pe.sem_inc(s["x_used"], 2)
                pe.sem_inc(s["stat_mm"], 1)
                pe.sem_inc(s["s_ps"], 2)
                pe.wait_ge(s["wfold"], 2)
                pe.matmul(misc[:, 0:128], W("center"), wk0[:, :], start=True, stop=True)
                pe.matmul(misc[:, 128:256], W("center"), wv0[:, :], start=True, stop=True)
                pe.matmul(misc[:, 256:257], W("tk"), W("kvb"), start=True, stop=True)
                pe.matmul(misc[:, 257:258], W("tv"), W("kvb"), start=True, stop=True).then_inc(s["wcent"], 1)
                pe.wait_ge(s["wready"], 1)
                with pe.Fori(0, B // 4) as i:
                    for k in range(2):
                        n = 2 * i + k
                        xt = xb[k]
                        pe.wait_ge(s["rf"], n + 1)
                        for j in range(2):
                            mm = pe.transpose(misc[:, 128 * j:128 * j + 128], rf[:, 128 * j:128 * j + 128], W("ident"))
                        mm.then_inc(s["rfT"], 1)
                        pe.wait_ge(s["tb"], CH * n + 2)
                        pe.wait_ge(s["sq"], 4 * n + 4)
                        for c in range(4):
                            for g in range(4):
                                at = 512 * (4 * (g % 2) + c)
                                mm = pe.matmul(kps[0][32 * g:32 * g + 32, :], W("blk", 32 * c, 32), (xt if g < 2 else sq)[:, at:at + 512],
                                               start=(c == 0), stop=(c == 3))
                        mm.then_inc(s["stat_mm"], 1)
                        pe.wait_ge(s["rt"], n + 1)
                        pe.wait_ge(s["stT"], n + 1)
                        for j in range(4):
                            mm = pe.transpose(misc[:, 128 * j:128 * j + 128], stT[:, 128 * j:128 * j + 128], W("ident"))
                        mm.then_inc(s["stat_ps"], 1)
                        pe.wait_ge(s["qn"], n + 1)
                        pe.wait_ge(s["st"], n + 1)
                        for j in range(2):
                            mm = pe.transpose(misc[:, 128 * j:128 * j + 128],
                                              qn[:, 2 * j:2 * j + 2, :].rearrange("p a b -> p (a b)"), W("ident"))
                        mm.then_inc(s["qnT_ps"], 1)
                        pe.wait_ge(s["qnT"], n + 1)
                        pe.matmul(misc[:, 0:256], W("tq"), qnT[:, :], start=True, stop=True).then_inc(s["q_ps"], 1)
                        for c in range(CH + 1):
                            if c < CH:
                                pe.wait_ge(s["tb"], CH * n + c + 1)
                                pe.matmul(kps[c % 2][:, :], wk[:, :], xt[:, 512 * c:512 * c + 512], start=True, stop=True).then_inc(s["k_ps"], 1)
                            if c > 0:
                                pe.wait_ge(s["tb"], CH * n + c + 2)
                                if c == 1:
                                    pe.wait_ge(s["s1"], n + 1)
                                pe.matmul(sps[:, :], W("sel", 128 * (c - 1), 128), tb[(c - 1) % 2][:, :],
                                          start=(c == 1), stop=(c == CH)).then_inc(s["s_ps"], 1)
                        pe.wait_ge(s["qx"], n + 1)
                        pe.wait_ge(s["t0"], n + 1)
                        for c in range(CH):
                            mm = pe.matmul(misc[:, 0:32], W("sel", 128 * c, 128), t0[:, 32 * c:32 * c + 32],
                                           start=(c == 0), stop=(c == CH - 1))
                        mm.then_inc(s["c0_ps"], 1)
                        pe.wait_ge(s["c0"], n + 1)
                        pe.wait_ge(s["rrep"], n + 1)
                        for j in range(4):
                            mm = pe.transpose(misc[:, 128 * j:128 * j + 128], rrep[:, j].rearrange("p a b c -> p (a b c)"), W("ident"))
                        mm.then_inc(s["rr_ps"], 1)
                        for c in range(CH):
                            pe.wait_ge(s["vs"], CH * n + c + 1)
                            mm = pe.matmul(vps[c % 2][:, :], wv[:, :], xt[:, 512 * c:512 * c + 512], start=True, stop=True)
                            mm.then_inc(s["v_ps"], 1)
                            if c == 0:
                                pe.wait_ge(s["p2"], n + 1)
                            pe.wait_ge(s["b_used"], CH * n + c + 1)
                            pe.matmul(bps[c % 2][:, :], W("selT", 128 * c, 128), p2[:, :], start=True, stop=True).then_inc(s["b_ps"], 1)
                        pe.wait_ge(s["rp"], n + 1)
                        pe.wait_ge(s["agb"], n + 1)
                        for j in range(2):
                            mm = pe.matmul(misc[:, 128 * j:128 * j + 128], agb[:, 128 * j:128 * j + 128], W("tproj"), start=True, stop=True)
                            mm.then_inc(s["x_used" if j == 0 else "o_ps"], 1)
                        pe.wait_ge(s["po"], n + 1)

            @block.scalar
            def _(act):
                act.sem_inc(s["vs"], 2)
                with act.Fori(0, B // 4) as i:
                    for k in range(2):
                        n = 2 * i + k
                        act.wait_ge(s[f"x_in{k}"], 16 * i + 16)
                        act.wait_ge(s["stat_mm"], n + 1)
                        for q in range(4):
                            act.activation(sq[:, 1024 * q:1024 * q + 1024], xb[k][:, 1024 * q:1024 * q + 1024], ACT.Square).then_inc(s["sq"], 1)
                        act.wait_ge(s["rfT"], n + 1)
                        act.mul(rt[:, :, :].rearrange("p a b -> p (a b)"), misc[:, 0:256], 1 / 16).then_inc(s["rt"], 1)
                        act.wait_ge(s["stat_mm"], n + 2)
                        act.copy(stT[:, :], kps[0][:, :]).then_inc(s["stT"], 1)
                        act.wait_ge(s["qnT_ps"], n + 1)
                        act.copy(qnT[:, :], misc[:, 0:256]).then_inc(s["qnT"], 1)
                        act.wait_ge(s["q_ps"], n + 1)
                        act.mul(qx[:, :, :], each(misc[:, 0:256], 256, 4), 1 / 8).then_inc(s["qx"], 1)
                        act.wait_ge(s["rr"], n + 1)
                        for j in range(4):
                            cp = act.copy(rrep[:, j].rearrange("p a b c -> p (a b) c"),
                                          rr[:, j].rearrange("p a b -> p (a b)").unsqueeze(2).broadcast_to([128, 2 * CH, 8]))
                        cp.then_inc(s["rrep"], 1)
                        act.wait_ge(s["c0_ps"], n + 1)
                        act.copy(c0[:, :, :], each(misc[:, 0:32], 32, 4)).then_inc(s["c0"], 1)
                        act.wait_ge(s["rr_ps"], n + 1)
                        act.copy(rp[:, :], misc[:, :]).then_inc(s["rp"], 1)
                        act.wait_ge(s["s3"], n + 1)
                        act.activation(ex[:, :], s3[:, :], ACT.Exp).then_inc(s["ex"], 1)
                        for c in range(CH):
                            act.wait_ge(s["v_ps"], CH * n + c + 1)
                            act.wait_ge(s["b_used"], CH * n + c + 1)
                            act.copy(vs[c % 2][:, :], vps[c % 2][:, :]).then_inc(s["vs"], 1)

            @block.vector
            def _(v):
                v.sem_inc(s["tb"], 2)
                v.sem_inc(s["s1"], 1)
                v.sem_inc(s["b_used"], 2)
                v.sem_inc(s["agg"], 2)
                v.tensor_scalar(wk0[:, :], W("tk"), W("kvw"), None, ALU.mult).then_inc(s["wfold"], 1)
                v.tensor_scalar(wv0[:, :], W("tv"), W("kvw"), None, ALU.mult).then_inc(s["wfold"], 1)
                v.wait_ge(s["wcent"], 1)
                v.tensor_copy(wk[:, :], misc[:, 0:128])
                v.tensor_copy(wv[:, :], misc[:, 128:256])
                v.tensor_copy(kb[:, :], misc[:, 256:257])
                v.tensor_copy(vb[:, :], misc[:, 257:258]).then_inc(s["wready"], 1)
                v.wait_ge(s["wready"], 1)
                with v.Fori(0, B // 4) as i:
                    for k in range(2):
                        n = 2 * i + k
                        v.wait_ge(s[f"x_in{k}"], 16 * i + 16)
                        v.tensor_reduce(rf[:, :].rearrange("p (a w) -> p a w", w=16), grid(xb[k][:, :]), AX_XY, ALU.add).then_inc(s["rf"], 1)
                        v.wait_ge(s["rt"], n + 1)
                        v.tensor_reduce(sm[:, :], rt[:, :, :], AX_X, ALU.add).then_inc(s["sm"], 1)
                        v.wait_ge(s["sm"], n + 1)
                        v.tensor_scalar(nm[:, :], sm[:, :], -1 / C, None, ALU.mult).then_inc(s["nm"], 1)
                        v.wait_ge(s["nm"], n + 1)
                        v.tensor_tensor(hc[:, :, :], rt[:, :, :], each(nm[:, :], 4, 64), ALU.add).then_inc(s["hc"], 1)
                        v.wait_ge(s["hc"], n + 1)
                        v.tensor_tensor(hs[:, :, :], hc[:, :, :], hc[:, :, :], ALU.mult).then_inc(s["hs"], 1)
                        v.wait_ge(s["hs"], n + 1)
                        v.tensor_reduce(sm[:, :], hs[:, :, :], AX_X, ALU.add).then_inc(s["ssq"], 1)
                        v.wait_ge(s["ssq"], n + 1)
                        v.tensor_scalar(ve[:, :], sm[:, :], 1 / C, EPS, ALU.mult, ALU.add).then_inc(s["ve"], 1)
                        v.wait_ge(s["rs"], n + 1)
                        v.tensor_tensor(hs[:, :, :], hc[:, :, :], each(rs[:, :], 4, 64), ALU.mult).then_inc(s["hn"], 1)
                        v.wait_ge(s["hn"], n + 1)
                        lnqw, lnqb = (W(m).unsqueeze(1).broadcast_to([128, 4, 64]) for m in ("lnqw", "lnqb"))
                        v.tensor_tensor(hc[:, :, :], hs[:, :, :], lnqw, ALU.mult).then_inc(s["hnw"], 1)
                        v.wait_ge(s["hnw"], n + 1)
                        v.tensor_tensor(qn[:, :, :], hc[:, :, :], lnqb, ALU.add).then_inc(s["qn"], 1)
                        v.wait_ge(s["stat_ps"], n + 1)
                        v.tensor_copy(st[:, :, :, :], misc[:, :].rearrange("p (j g r) -> p j g r", g=4, r=32)[:, :, :, 0:8]).then_inc(s["st"], 1)
                        v.wait_ge(s["st"], n + 1)
                        v.tensor_tensor(m2[:, :, :, :], st[:, :, 0:2], st[:, :, 0:2], ALU.mult).then_inc(s["m2"], 1)
                        v.wait_ge(s["m2"], n + 1)
                        v.tensor_tensor(m2[:, :, :, :], st[:, :, 2:4], m2[:, :, :, :], ALU.subtract).then_inc(s["va"], 1)
                        v.wait_ge(s["va"], n + 1)
                        v.tensor_scalar(va[:, :, :, :], m2[:, :, :, :], 0.0, EPS, ALU.max, ALU.add).then_inc(s["vae"], 1)
                        v.wait_ge(s["qx"], n + 1)
                        v.tensor_scalar(t0[:, :], qx[:, :, 0:1].rearrange("p a b -> p (a b)"), kb[:, :], None, ALU.mult).then_inc(s["t0"], 1)
                        for c in range(CH):
                            v.wait_ge(s["k_ps"], CH * n + c + 1)
                            v.wait_ge(s["s_ps"], CH * n + c + 1)
                            v.tensor_tensor(strips(tb[c % 2][:, :]), strips(kps[c % 2][:, :]), over_rows(qx[:, 32 * c:32 * c + 32, :], 2),
                                            ALU.mult).then_inc(s["tb"], 1)
                        v.wait_ge(s["s_ps"], CH * n + CH + 2)
                        v.wait_ge(s["rp"], n + 1)
                        v.tensor_tensor(s1[:, :], sps[:, :], rp[:, :], ALU.mult).then_inc(s["s1"], 1)
                        v.wait_ge(s["s1"], n + 2)
                        v.wait_ge(s["c0"], n + 1)
                        v.tensor_tensor(strips(s2[:, :]), strips(s1[:, :]), over_rows(c0[:, :, :], 2), ALU.add).then_inc(s["s2"], 1)
                        v.wait_ge(s["s2"], n + 1)
                        v.tensor_reduce(mx[:, :].rearrange("p (a w) -> p a w", w=16), grid(s2[:, :]), AX_XY, ALU.max).then_inc(s["mx"], 1)
                        v.wait_ge(s["mx"], n + 1)
                        v.tensor_copy(mxx[:, :, :], each(mx[:, :], 32, 4)).then_inc(s["mxx"], 1)
                        v.wait_ge(s["mxx"], n + 1)
                        v.tensor_tensor(strips(s3[:, :]), strips(s2[:, :]), over_rows(mxx[:, :, :], 2), ALU.subtract).then_inc(s["s3"], 1)
                        v.wait_ge(s["ex"], n + 1)
                        v.tensor_reduce(z[:, :].rearrange("p (a w) -> p a w", w=16), grid(ex[:, :]), AX_XY, ALU.add).then_inc(s["z"], 1)
                        v.wait_ge(s["z"], n + 1)
                        v.reciprocal(rz[:, :], z[:, :]).then_inc(s["rz"], 1)
                        v.wait_ge(s["rz"], n + 1)
                        v.tensor_copy(rzx[:, :, :], each(rz[:, :], 32, 4)).then_inc(s["rzx"], 1)
                        v.wait_ge(s["rzx"], n + 1)
                        v.tensor_tensor(strips(p1[:, :]), strips(ex[:, :]), over_rows(rzx[:, :, :], 2), ALU.mult).then_inc(s["p1"], 1)
                        v.wait_ge(s["p1"], n + 1)
                        v.tensor_tensor(p2[:, :], p1[:, :], rp[:, :], ALU.mult).then_inc(s["p2"], 1)
                        for c in range(CH):
                            v.wait_ge(s["b_ps"], CH * n + c + 1)
                            v.wait_ge(s["vs"], CH * n + c + 3)
                            v.wait_ge(s["agg"], CH * n + c + 1)
                            v.tensor_tensor(pv[c % 2][:, :], bps[c % 2][:, :], vs[c % 2][:, :], ALU.mult).then_inc(s["b_used"], 1)
                            v.wait_ge(s["b_used"], CH * n + c + 3)
                            v.tensor_reduce(agg[:, 32 * c:32 * c + 32].rearrange("p (a w) -> p a w", w=16), grid(pv[c % 2][:, :]), AX_XY, ALU.add).then_inc(s["agg"], 1)
                        v.wait_ge(s["agg"], CH * n + CH + 2)
                        v.tensor_scalar(agb[:, :], agg[:, :], vb[:, :], None, ALU.add).then_inc(s["agb"], 1)
                        v.wait_ge(s["o_ps"], n + 1)
                        v.tensor_tensor(po[:, :, :], misc[:, 0:256].rearrange("p (a b) -> p a b", b=64), rt[:, :, :], ALU.add).then_inc(s["po"], 1)
                        v.wait_ge(s["po"], n + 1)
                        v.tensor_tensor(h_all[:, bass.ds(6 * n, 6), :].rearrange("p (g j) c -> p j g c", g=2)[:, 0:2],
                                        po[:, :, :].rearrange("p (j g) c -> p j g c", j=2),
                                        W("projb").unsqueeze(1).unsqueeze(1).broadcast_to([128, 2, 2, 64]), ALU.add).then_inc(s["o_done"], 1)


def attention_stage(nc, mem):
    h_all, W = mem["h"], mem["W"]
    Q_PARTS, K_PARTS = (0, 0, 0, 1, 1, 2), (0, 1, 2, 0, 1, 0)
    U = NT * HEADS
    G = U // 4
    with ExitStack() as ctx:
        sb = lambda n, s, d=F32: ctx.enter_context(nc.sbuf_tensor("a_" + n, s, d))
        ps = lambda n, s, d=F32: ctx.enter_context(nc.psum_tensor("a_" + n, s, d))
        half = sb("half", [128, 24])
        lp, ls, le = sb("lp", [128, 2, 16]), sb("ls", [128, 2]), sb("le", [128, 2])
        ld, lamv = sb("ld", [128, 1]), sb("lamv", [128, 2])
        gam, bet = sb("gam", [128, 32]), sb("bet", [128, 32])
        sm, nm, ve, rs = (sb(n, [128, NT]) for n in ("sm", "nm", "ve", "rs"))
        hc, hs = (sb(n, [128, NT, C]) for n in ("hc", "hs"))
        hn = sb("hn", [128, NT + 1, C])
        zero, one = sb("zero", [128, 1]), sb("one", [128, 24])
        hT = sb("hT", [128, L])
        parts = sb("parts", [128, 4, 3, L], BF16)
        rest = [sb(f"rest{k}", [128, L]) for k in range(2)]
        qe = [sb(f"qe{k}", [96, 16, L], BF16) for k in range(2)]
        ke = [sb(f"ke{k}", [96, 16, L], BF16) for k in range(2)]
        val = [sb(f"val{k}", [128, NT, INNER]) for k in range(2)]
        th = [sb(f"th{k}", [128, NT, INNER]) for k in range(2)]
        nmx = sb("nmx", [128, 4, 2])
        E = [sb(f"e{k}", [128, 2, L]) for k in range(3)]
        Z = [sb(f"z{k}", [128, U, 2]) for k in range(2)]
        rz, rzl = sb("rz", [128, 4, 2]), sb("rzl", [128, 4, 2])
        DT = [sb(f"dt{k}", [128, 2, 4, NT, 128]) for k in range(2)]
        oT = [sb(f"oT{k}", [128, 256]) for k in range(2)]
        mixed = sb("mixed", [128, 2, 4, DV])
        O = [sb(f"o{k}", [128, NT, HEADS, DV]) for k in range(2)]
        so, no, vo, ro = (sb(n, [128, 24]) for n in ("so", "no", "vo", "ro"))
        oc, o2, sg, of = (sb(n, [128, 24, DV]) for n in ("oc", "o2", "sg", "of"))
        oF = sb("oF", [128, 2, L])
        hp = sb("hp", [128, NT, C])
        s_ps = [ps(f"s{k}", [128, 2, 512]) for k in range(2)]
        t_ps = [ps(f"t{k}", [128, 512]) for k in range(2)]
        av_ps = ps("av", [128, 512])
        misc = ps("misc", [128, 512])
        scratch = nc.dram_tensor("a_scratch", (3, 2, 16, 16, L), BF16, kind="Internal").ap()
        s = signals(nc, ctx, "a_", """half lp ls le ld neglam gb ones
            sm nm hc hs ssq ve rs hn ht_ps ht qk_ps hi rest mid lo scr qe vg_ps val
            s_ps mx ex t0_ps t1_ps dt0 dt1 av_ps av ot_ps rz rzl otm ot
            so no oc o2 sso vo ro on og ob sg of ft_ps ft op_ps hp h""")
        each = lambda ap, n, k: ap.unsqueeze(2).broadcast_to([128, n, k])
        per_group = lambda ap: ap.unsqueeze(1).broadcast_to([128, 24, DV])
        flat = lambda ap: ap.rearrange("p a b -> p (a b)")
        tiles = lambda n: h_all[:, bass.ds(NT * n, NT), :]

        MISC = {0: ("ot", 4), 2: ("ht", 0), 3: ("qk", 0), 4: ("ot", 5), 5: ("qk", 1), 6: ("qk", 2), 7: ("qk", 3), 8: ("ot", 0),
                9: ("vg", 0), 10: ("vg", 1), 11: ("vg", 2), 12: ("ot", 1), 16: ("ot", 2), 19: ("ft", 0), 20: ("ot", 3),
                21: ("ft", 1), 22: ("op", 0)}

        def bodies(eng, body, prologue, epilogue):
            prologue()
            body(0, 0, True, False)
            with eng.Fori(0, (B - 2) // 2) as i:
                body(2 * i + 1, 1, False, False)
                body(2 * i + 2, 0, False, False)
            body(B - 1, 1, False, True)
            epilogue()

        def tasks(u, first, last):
            if u not in MISC:
                return None
            name, c = MISC[u]
            ahead = 1 if name in ("ht", "qk", "vg") else -1 if name in ("ft", "op") or (name == "ot" and c >= 4) else 0
            if (ahead == 1 and last) or (ahead == -1 and first):
                return None
            return name, c, ahead

        def unit(n, k, u):
            return (n - 1, 1 - k, u + U) if u < 0 else (n, k, u) if u < U else (n + 1, 1 - k, u - U)

        def there(u, first, last):
            return not (u < 0 and first) and not (u >= U and last)

        with nc.Block() as block:
            @block.sync
            def _(sp):
                def spread(n, k):
                    sp.wait_ge(s["lo"], 4 * n + 6)
                    for t in range(4):
                        sp.dma_start(scratch[:, t // 2, 8 * (t % 2):8 * (t % 2) + 8].rearrange("q m d n -> (m d) q n"),
                                     parts[:, t]).then_inc(s["scr"], 16)
                    sp.wait_ge(s["scr"], 64 * n + 64)
                    for g in range(6):
                        sp.dma_start(qe[k][16 * g:16 * g + 16, :, :],
                                     scratch[Q_PARTS[g], 0].rearrange("m d n -> d m n")).then_inc(s["qe"], 16)
                        sp.dma_start(ke[k][16 * g:16 * g + 16, :, :],
                                     scratch[K_PARTS[g], 1].rearrange("m d n -> d m n")).then_inc(s["qe"], 16)

                spread(0, 0)
                spread(1, 1)
                with sp.Fori(0, (B - 2) // 2) as i:
                    for k in range(2):
                        spread(2 * i + 2 + k, k)

            @block.gpsimd
            def _(pl):
                def deviation(m):
                    pl.wait_ge(s["ve"], m + 1)
                    pl.tensor_tensor(rs[:, :], ve[:, :], half[:, 0:NT], ALU.pow).then_inc(s["rs"], 1)

                def split(m, c):
                    pl.wait_ge(s["rest"], 4 * m + c + 1)
                    pl.tensor_tensor(parts[:, c, 1, :], rest[c % 2][:, :], zero[:, :].broadcast_to([128, L]), ALU.add).then_inc(s["mid"], 1)
                    pl.wait_ge(s["mid"], 4 * m + c + 1)
                    pl.tensor_tensor(parts[:, c, 2, :], rest[c % 2][:, :], parts[:, c, 1, :], ALU.subtract).then_inc(s["lo"], 1)

                def gate_plus_one(m, k):
                    pl.wait_ge(s["of"], m + 1)
                    pl.wait_ge(s["val"], NT * m + NT)
                    pl.tensor_tensor(sg[:, :, :], th[k][:, :, :].rearrange("p a (b c) -> p (a b) c", c=DV),
                                     one[:, :].unsqueeze(2).broadcast_to([128, 24, DV]), ALU.add).then_inc(s["sg"], 1)

                def centre(m, k):
                    pl.wait_ge(s["no"], m + 1)
                    pl.tensor_tensor(oc[:, :, :], O[k][:, :, :, :].rearrange("p a b c -> p (a b) c"), each(no[:, :], 24, DV), ALU.add)\
                        .then_inc(s["oc"], 1)
                    pl.wait_ge(s["oc"], m + 1)
                    pl.tensor_tensor(o2[:, :, :], oc[:, :, :], oc[:, :, :], ALU.mult).then_inc(s["o2"], 1)

                def normed(m):
                    pl.wait_ge(s["vo"], m + 1)
                    pl.tensor_tensor(ro[:, :], vo[:, :], half[:, :], ALU.pow).then_inc(s["ro"], 1)
                    pl.wait_ge(s["ro"], m + 1)
                    pl.tensor_tensor(o2[:, :, :], oc[:, :, :], each(ro[:, :], 24, DV), ALU.mult).then_inc(s["on"], 1)

                def gated(m):
                    pl.wait_ge(s["on"], m + 1)
                    pl.tensor_tensor(oc[:, :, :], o2[:, :, :], per_group(gam[:, :]), ALU.mult).then_inc(s["og"], 1)
                    pl.wait_ge(s["og"], m + 1)
                    pl.tensor_tensor(o2[:, :, :], oc[:, :, :], per_group(bet[:, :]), ALU.add).then_inc(s["ob"], 1)
                    pl.wait_ge(s["ob"], m + 1)
                    pl.wait_ge(s["sg"], m + 1)
                    pl.tensor_tensor(of[:, :, :], o2[:, :, :], sg[:, :, :], ALU.mult).then_inc(s["of"], 1)

                def prologue():
                    pl.sem_inc(s["lo"], 2)
                    pl.sem_inc(s["of"], 1)
                    pl.memset(zero[:, :], 0.0)
                    pl.memset(one[:, :], 1.0)
                    pl.memset(half[:, :], -0.5).then_inc(s["half"], 1)
                    pl.wait_ge(s["half"], 1)
                    pl.wait_ge(s["gb"], 1)
                    deviation(0)
                    for c in range(4):
                        split(0, c)

                def body(n, k, first, last):
                    if not last:
                        deviation(n + 1)
                    if not first:
                        gate_plus_one(n - 1, 1 - k)
                    if not last:
                        for c in range(4):
                            split(n + 1, c)
                    if not first:
                        centre(n - 1, 1 - k)
                        normed(n - 1)
                        gated(n - 1)

                def epilogue():
                    gate_plus_one(B - 1, 1)
                    centre(B - 1, 1)
                    normed(B - 1)
                    gated(B - 1)

                bodies(pl, body, prologue, epilogue)

            @block.tensor
            def _(pe):
                def scores(n, k, u):
                    ic, hd = u // HEADS, u % HEADS
                    pe.wait_ge(s["ex"], U * n + u + 1)
                    for m in range(2):
                        mm = pe.matmul(s_ps[u % 2][:, m, 0:L], qe[k][:, 2 * hd + m, 128 * ic:128 * ic + 128], ke[k][:, 2 * hd + m, :],
                                       start=True, stop=True)
                    mm.then_inc(s["s_ps"], 1)

                def transposes(n, k, u):
                    for m in range(2):
                        if m == 0:
                            pe.wait_ge(s["ex"], U * n + u + 3)
                        pe.wait_ge(s[f"dt{m}"], U * n + u + 1)
                        for j in range(NT):
                            mm = pe.transpose(t_ps[m][:, 128 * j:128 * j + 128], E[u % 3][:, m, 128 * j:128 * j + 128], W("ident"))
                        mm.then_inc(s[f"t{m}_ps"], 1)

                def outputs(n, k, g, m):
                    pe.wait_ge(s[f"dt{m}"], U * n + 4 * g + 5)
                    if m == 0:
                        pe.wait_ge(s["av"], G * n + g + 1)
                    for j in range(NT):
                        for q in range(4):
                            mm = pe.matmul(av_ps[32 * q:32 * q + 32, 128 * m:128 * m + 128], val[k][:, j, DV * (4 * (g % 2) + q):DV * (4 * (g % 2) + q + 1)],
                                           DT[g % 2][:, m, q, j, :], start=(j == 0), stop=(j == NT - 1))
                    mm.then_inc(s["av_ps"], 1)

                def free_misc(name, c, m):
                    total = {"ot": G, "ht": 1, "qk": 4, "vg": NT, "ft": 2, "op": 1}[name]
                    sem = {"ot": "otm", "ht": "ht", "qk": "rest", "vg": "val", "ft": "ft", "op": "hp"}[name]
                    pe.wait_ge(s[sem], total * m + c + (2 if name == "op" else 1))

                def task(name, c, m, k):
                    if name == "ht":
                        pe.wait_ge(s["hn"], m + 1)
                        for j in range(NT):
                            mm = pe.transpose(misc[:, 128 * j:128 * j + 128], hn[:, j:j + 2, :].rearrange("p a b -> p (a b)"), W("ident"))
                        mm.then_inc(s["ht_ps"], 1)
                    if name == "qk":
                        if c == 0:
                            pe.wait_ge(s["ht"], m + 1)
                        pe.matmul(misc[:, 0:L], W("aqk", 128 * c, 128), hT[:, :], start=True, stop=True).then_inc(s["qk_ps"], 1)
                    if name == "vg":
                        pe.matmul(misc[:, :], hT[:, 128 * c:128 * c + 128], W("avg"), start=True, stop=True).then_inc(s["vg_ps"], 1)
                    if name == "ot":
                        pe.wait_ge(s["av"], G * m + c + 2)
                        for a in range(2):
                            mm = pe.transpose(misc[:, 128 * a:128 * a + 128], oT[c % 2][:, 128 * a:128 * a + 128], W("ident"))
                        mm.then_inc(s["ot_ps"], 1)
                    if name == "ft":
                        pe.wait_ge(s["of"], m + 2)
                        for j in range(NT):
                            mm = pe.transpose(misc[:, 128 * j:128 * j + 128],
                                              of[:, 8 * j + 4 * c:8 * j + 4 * c + 4, :].rearrange("p a b -> p (a b)"), W("ident"))
                        mm.then_inc(s["ft_ps"], 1)
                    if name == "op":
                        pe.wait_ge(s["ft"], 2 * m + 2)
                        for j in range(NT):
                            for c in range(2):
                                mm = pe.matmul(misc[:, 64 * j:64 * j + 64], oF[:, c, 128 * j:128 * j + 128], W("aout", 64 * c, 64),
                                               start=(c == 0), stop=(c == 1))
                        mm.then_inc(s["op_ps"], 1)

                def prologue():
                    chain = [("ht", 0)] + [("qk", c) for c in range(4)] + [("vg", c) for c in range(NT)]
                    pe.sem_inc(s["t1_ps"], 3)
                    pe.sem_inc(s["av_ps"], 4)
                    pe.sem_inc(s["ot_ps"], 2)
                    pe.wait_ge(s["ones"], 2)
                    for j, (name, c) in enumerate(chain):
                        if j:
                            free_misc(*chain[j - 1], 0)
                        task(name, c, 0, 0)
                    free_misc("vg", NT - 1, 0)
                    pe.wait_ge(s["qe"], 192)
                    scores(0, 0, 0)
                    scores(0, 0, 1)

                def body(n, k, first, last):
                    before = [("vg", NT - 1, 0)] if first else [("ot", 3, -1), ("op", 0, -2)]
                    for u in range(U):
                        if there(u + 2, first, last):
                            if u + 2 == U:
                                pe.wait_ge(s["qe"], 192 * n + 384)
                            scores(*unit(n, k, u + 2))
                        if there(u - 1, first, last):
                            transposes(*unit(n, k, u - 1))
                        if u % 4 in (1, 2) and there(u - 5, first, last):
                            b, kb, v = unit(n, k, u - 4 - u % 4)
                            outputs(b, kb, v // 4, u % 4 - 1)
                        t = tasks(u, first, last)
                        if t:
                            name, c, ahead = t
                            for b in before:
                                free_misc(b[0], b[1], n + b[2])
                            task(name, c, n + ahead, k)
                            before = [(name, c, ahead)]

                def epilogue():
                    n = B - 1
                    transposes(n, 1, U - 1)
                    free_misc("op", 0, n - 1)
                    task("ot", 4, n, 1)
                    outputs(n, 1, 5, 0)
                    outputs(n, 1, 5, 1)
                    chain = [("ot", 4), ("ot", 5), ("ft", 0), ("ft", 1), ("op", 0)]
                    for old, new in zip(chain, chain[1:]):
                        free_misc(*old, n)
                        task(*new, n, 1)

                bodies(pe, body, prologue, epilogue)

            @block.scalar
            def _(act):
                def exps(n, k, u):
                    act.wait_ge(s["mx"], U * n + u + 1)
                    act.wait_ge(s["t1_ps"], U * n + u + 1)
                    for m in range(2):
                        a = act.activation(E[u % 3][:, m, :], s_ps[u % 2][:, m, 0:L], ACT.Exp, bias=nmx[:, u % 4, m:m + 1],
                                           accum_out=Z[k][:, u, m:m + 1])
                    a.then_inc(s["ex"], 1)

                def first_map(n, u):
                    act.wait_ge(s["t0_ps"], U * n + u + 1)
                    if u % 4 == 0:
                        act.wait_ge(s["av_ps"], 2 * (G * n + u // 4) + 1)
                    act.copy(DT[(u // 4) % 2][:, 0, u % 4], t_ps[0][:, 0:L].rearrange("p (a b) -> p a b", b=128)).then_inc(s["dt0"], 1)

                def output(n, g):
                    act.wait_ge(s["av_ps"], 2 * (G * n + g) + 6)
                    act.wait_ge(s["ot_ps"], G * n + g + 1)
                    act.copy(oT[g % 2][:, :], av_ps[:, 0:256]).then_inc(s["av"], 1)

                def evac(name, c, m, k, ahead=True, guard=False):
                    if name == "ht":
                        act.wait_ge(s["ht_ps"], m + 1)
                        act.copy(hT[0:64, :], misc[0:64, 0:L]).then_inc(s["ht"], 1)
                    if name == "qk":
                        act.wait_ge(s["qk_ps"], 4 * m + c + 1)
                        if c == 0 and ahead:
                            act.wait_ge(s["scr"], 64 * m)
                        act.mul(parts[:, c, 0, :], misc[:, 0:L], DH ** -0.5 if c < 2 else 1.0).then_inc(s["hi"], 1)
                    if name == "vg":
                        act.wait_ge(s["vg_ps"], NT * m + c + 1)
                        if c == 0 and guard:
                            act.wait_ge(s["sg"], m - 1)
                        act.copy(val[k][:, c, :], misc[:, 0:INNER])
                        act.activation(th[k][:, c, :], misc[:, INNER:2 * INNER], ACT.Tanh, scale=0.5).then_inc(s["val"], 1)
                    if name == "ft":
                        act.wait_ge(s["ft_ps"], 2 * m + c + 1)
                        act.copy(oF[:, c, :], misc[:, 0:L]).then_inc(s["ft"], 1)

                def prologue():
                    act.sem_inc(s["ex"], 2)
                    act.sem_inc(s["dt0"], 1)
                    act.sem_inc(s["av"], 1)
                    act.wait_ge(s["ls"], 1)
                    act.activation(le[:, :], ls[:, :], ACT.Exp).then_inc(s["le"], 1)
                    for name, c in [("ht", 0)] + [("qk", c) for c in range(4)] + [("vg", c) for c in range(NT)]:
                        evac(name, c, 0, 0, False)
                    exps(0, 0, 0)

                def body(n, k, first, last):
                    for u in range(U):
                        if there(u + 1, first, last):
                            exps(*unit(n, k, u + 1))
                        if u % 4 == 3 and there(u - 7, first, last):
                            b, _, v = unit(n, k, u - 7)
                            output(b, v // 4)
                        if there(u - 1, first, last):
                            b, _, v = unit(n, k, u - 1)
                            first_map(b, v)
                        t = tasks(u, first, last)
                        if t:
                            name, c, ahead = t
                            evac(name, c, n + ahead, (k + ahead) % 2, guard=not first)

                def epilogue():
                    first_map(B - 1, U - 1)
                    output(B - 1, 5)
                    evac("ft", 0, B - 1, 1)
                    evac("ft", 1, B - 1, 1)

                bodies(act, body, prologue, epilogue)

            @block.vector
            def _(v):
                def maxima(n, u):
                    v.wait_ge(s["s_ps"], U * n + u + 1)
                    v.tensor_reduce(nmx[:, u % 4, :], s_ps[u % 2][:, :, 0:L], AX_X, ALU.max, negate=True).then_inc(s["mx"], 1)

                def norm(m, part):
                    if part == 0:
                        v.tensor_reduce(sm[:, :], tiles(m), AX_X, ALU.add).then_inc(s["sm"], 1)
                    if part == 1:
                        v.wait_ge(s["sm"], m + 1)
                        v.tensor_scalar(nm[:, :], sm[:, :], -1 / C, None, ALU.mult).then_inc(s["nm"], 1)
                    if part == 2:
                        v.wait_ge(s["nm"], m + 1)
                        v.tensor_tensor(hc[:, :, :], tiles(m), each(nm[:, :], NT, C), ALU.add).then_inc(s["hc"], 1)
                    if part == 3:
                        v.wait_ge(s["hc"], m + 1)
                        v.tensor_tensor(hs[:, :, :], hc[:, :, :], hc[:, :, :], ALU.mult).then_inc(s["hs"], 1)
                    if part == 4:
                        v.wait_ge(s["hs"], m + 1)
                        v.tensor_reduce(sm[:, :], hs[:, :, :], AX_X, ALU.add).then_inc(s["ssq"], 1)
                    if part == 5:
                        v.wait_ge(s["ssq"], m + 1)
                        v.tensor_scalar(ve[:, :], sm[:, :], 1 / C, EPS, ALU.mult, ALU.add).then_inc(s["ve"], 1)
                    if part == 6:
                        v.wait_ge(s["rs"], m + 1)
                        v.tensor_tensor(hn[:, 0:NT, :], hc[:, :, :], each(rs[:, :], NT, C), ALU.mult).then_inc(s["hn"], 1)

                def second_map(n, u):
                    v.wait_ge(s["t1_ps"], U * n + u + 4)
                    if u % 4 == 0:
                        v.wait_ge(s["av_ps"], 2 * (G * n + u // 4) + 2)
                    v.tensor_copy(DT[(u // 4) % 2][:, 1, u % 4], t_ps[1][:, 0:L].rearrange("p (a b) -> p a b", b=128)).then_inc(s["dt1"], 1)

                def heads_a(m, k):
                    v.wait_ge(s["ot"], G * m + G + 1)
                    v.tensor_reduce(so[:, :], O[k][:, :, :, :].rearrange("p a b c -> p (a b) c"), AX_X, ALU.add).then_inc(s["so"], 1)
                    v.wait_ge(s["so"], m + 1)
                    v.tensor_scalar(no[:, :], so[:, :], -1 / DV, None, ALU.mult).then_inc(s["no"], 1)

                def heads_b(m):
                    v.wait_ge(s["o2"], m + 1)
                    v.tensor_reduce(so[:, :], o2[:, :, :], AX_X, ALU.add).then_inc(s["sso"], 1)
                    v.wait_ge(s["sso"], m + 1)
                    v.tensor_scalar(vo[:, :], so[:, :], 1 / DV, EPS, ALU.mult, ALU.add).then_inc(s["vo"], 1)

                def mix(m, k, c, part):
                    N = G * m + c
                    if part == 0:
                        v.wait_ge(s["ex"], U * m + 4 * c + 6)
                        v.reciprocal(rz[:, :, :], Z[k][:, 4 * c:4 * c + 4, :]).then_inc(s["rz"], 1)
                    if part == 1:
                        v.wait_ge(s["rz"], N + 1)
                        v.wait_ge(s["ot"], N + 1)
                        v.tensor_tensor(rzl[:, :, :], rz[:, :, :], lamv[:, :].unsqueeze(1).broadcast_to([128, 4, 2]), ALU.mult).then_inc(s["rzl"], 1)
                    if part == 2:
                        v.wait_ge(s["rzl"], N + 1)
                        v.wait_ge(s["ot_ps"], N + 3)
                        v.tensor_tensor(mixed[:, :, :, :], misc[:, 0:256].rearrange("p (m h c) -> p m h c", m=2, h=4),
                                        rzl[:, :, :].rearrange("p h m -> p m h").unsqueeze(3).broadcast_to([128, 2, 4, DV]), ALU.mult).then_inc(s["otm"], 1)
                    if part == 3:
                        v.wait_ge(s["otm"], N + 1)
                        v.tensor_tensor(O[k][:, c // 2, 4 * (c % 2):4 * (c % 2) + 4, :], mixed[:, 0], mixed[:, 1], ALU.add).then_inc(s["ot"], 1)

                def evac(name, c, m, k):
                    if name == "qk":
                        v.wait_ge(s["hi"], 4 * m + c + 1)
                        v.wait_ge(s["lo"], 4 * m + c + 1)
                        v.scalar_tensor_tensor(rest[c % 2][:, :], misc[:, 0:L], DH ** -0.5 if c < 2 else 1.0, parts[:, c, 0, :],
                                               ALU.mult, ALU.subtract).then_inc(s["rest"], 1)
                    if name == "op":
                        v.wait_ge(s["op_ps"], m + 1)
                        v.tensor_tensor(hp[:, :, :], misc[:, 0:NT * C].rearrange("p (a b) -> p a b", b=C), tiles(m), ALU.add).then_inc(s["hp"], 1)
                        v.wait_ge(s["hp"], m + 2)
                        v.tensor_tensor(tiles(m), hp[:, :, :], W("aoutb").unsqueeze(1).broadcast_to([128, NT, C]), ALU.add).then_inc(s["h"], 1)

                def prologue():
                    v.sem_inc(s["dt1"], 1)
                    v.sem_inc(s["ot"], 1)
                    v.sem_inc(s["hp"], 1)
                    v.memset(lamv[:, 0:1], 1.0)
                    v.memset(hn[:, NT, :], 0.0)
                    v.memset(hT[64:128, :], 0.0).then_inc(s["ones"], 1)
                    v.wait_ge(s["ones"], 1)
                    v.memset(hT[64:65, :], 1.0).then_inc(s["ones"], 1)
                    for j in range(2):
                        v.tensor_tensor(lp[:, j], W("lqk", 32 * j, 16), W("lqk", 32 * j + 16, 16), ALU.mult).then_inc(s["lp"], 1)
                    v.wait_ge(s["lp"], 2)
                    v.tensor_reduce(ls[:, :], lp[:, :, :], AX_X, ALU.add).then_inc(s["ls"], 1)
                    v.tensor_scalar(gam[:, :], W("gam"), 0.5 * (1.0 - LAMBDA_INIT), None, ALU.mult)
                    v.tensor_scalar(bet[:, :], W("bet"), 0.5 * (1.0 - LAMBDA_INIT), None, ALU.mult).then_inc(s["gb"], 1)
                    v.wait_ge(s["le"], 1)
                    v.tensor_tensor(ld[:, :], le[:, 1:2], le[:, 0:1], ALU.subtract).then_inc(s["ld"], 1)
                    v.wait_ge(s["ld"], 1)
                    v.tensor_scalar(lamv[:, 1:2], ld[:, :], -LAMBDA_INIT, None, ALU.add).then_inc(s["neglam"], 1)
                    v.wait_ge(s["neglam"], 1)
                    for part in range(7):
                        norm(0, part)
                    for c in range(4):
                        evac("qk", c, 0, 0)
                    maxima(0, 0)
                    maxima(0, 1)

                def body(n, k, first, last):
                    for u in range(U):
                        now, old = tasks(u, first, last), tasks(u - 1, first, last)
                        mixing = lambda t, part: t and t[0] == "ot" and mix(n + t[2], (k + t[2]) % 2, t[1], part)
                        mixing(old, 2)
                        if old and old[0] != "ot":
                            name, c, ahead = old
                            evac(name, c, n + ahead, (k + ahead) % 2)
                        if u < 3 and not last:
                            norm(n + 1, 3 * u)
                        if there(u + 2, first, last):
                            b, _, w = unit(n, k, u + 2)
                            maxima(b, w)
                        mixing(now, 0)
                        mixing(old, 3)
                        if u < 2 and not last:
                            norm(n + 1, 3 * u + 1)
                        if there(u - 1, first, last):
                            b, _, w = unit(n, k, u - 1)
                            second_map(b, w)
                        mixing(now, 1)
                        if u < 2 and not last:
                            norm(n + 1, 3 * u + 2)
                        if u == 5 and not first:
                            heads_a(n - 1, 1 - k)
                        if u == 12 and not first:
                            heads_b(n - 1)

                def epilogue():
                    second_map(B - 1, U - 1)
                    for c in (4, 5):
                        for part in range(4):
                            mix(B - 1, 1, c, part)
                    heads_a(B - 1, 1)
                    heads_b(B - 1)
                    evac("op", 0, B - 1, 1)

                bodies(v, body, prologue, epilogue)


GT = 12


def norm_names():
    return "sm nm hc hs ssq ve rs hn"


def layer_norm(v, s, m, h, t, bufs):
    sm, nm, ve, hc, hs = bufs
    each = lambda ap: ap.unsqueeze(2).broadcast_to([128, t, C])
    v.tensor_reduce(sm[:, :], h, AX_X, ALU.add).then_inc(s["sm"], 1)
    v.wait_ge(s["hn"], m + 1)
    v.wait_ge(s["sm"], m + 1)
    v.tensor_scalar(nm[:, :], sm[:, :], -1 / C, None, ALU.mult).then_inc(s["nm"], 1)
    v.wait_ge(s["nm"], m + 1)
    v.tensor_tensor(hc[:, :, :], h, each(nm[:, :]), ALU.add).then_inc(s["hc"], 1)
    v.wait_ge(s["hc"], m + 1)
    v.tensor_tensor(hs[:, :, :], hc[:, :, :], hc[:, :, :], ALU.mult).then_inc(s["hs"], 1)
    v.wait_ge(s["hs"], m + 1)
    v.tensor_reduce(sm[:, :], hs[:, :, :], AX_X, ALU.add).then_inc(s["ssq"], 1)
    v.wait_ge(s["ssq"], m + 1)
    v.tensor_scalar(ve[:, :], sm[:, :], 1 / C, EPS, ALU.mult, ALU.add).then_inc(s["ve"], 1)


def layer_norm_scale(v, s, m, rs, hc, hn, t):
    v.wait_ge(s["rs"], m + 1)
    v.tensor_tensor(hn, hc[:, :, :], rs[:, :].unsqueeze(2).broadcast_to([128, t, C]), ALU.mult).then_inc(s["hn"], 1)


def gate_buffers(sb, e):
    small = {n: sb("g" + n, [128, GT]) for n in ("m", "z", "rz", "gm", "zs", "rzs")}
    wide = {n: sb("g" + n, [128, GT, e]) for n in ("d", "e", "p", "rank", "sel", "dd", "ee", "es")}
    square = {n: sb("g" + n, [128, GT, e, e]) for n in ("gt", "eq", "el", "rk")}
    return {**small, **wide, **square}


GATE_NAMES = "gm gd ge gz grz gp ggt geq gel grk grank gsel ggm gdd gee ges gzs grzs gw"


def shifted(v, s, m, b, logits, e):
    v.tensor_reduce(b["m"][:, :], logits, AX_X, ALU.max).then_inc(s["gm"], 1)
    v.wait_ge(s["gm"], m + 1)
    v.tensor_tensor(b["d"][:, :, :], logits, b["m"][:, :].unsqueeze(2).broadcast_to([128, GT, e]), ALU.subtract).then_inc(s["gd"], 1)


def top_two(v, s, m, b, e, tie, w, again):
    each = lambda ap: ap.unsqueeze(2).broadcast_to([128, GT, e])
    v.wait_ge(s["ge"], m + 1)
    v.tensor_reduce(b["z"][:, :], b["e"][:, :, :], AX_X, ALU.add).then_inc(s["gz"], 1)
    v.wait_ge(s["gz"], m + 1)
    v.reciprocal(b["rz"][:, :], b["z"][:, :]).then_inc(s["grz"], 1)
    v.wait_ge(s["grz"], m + 1)
    p = b["p"]
    v.tensor_tensor(p[:, :, :], b["e"][:, :, :], each(b["rz"][:, :]), ALU.mult).then_inc(s["gp"], 1)
    v.wait_ge(s["gp"], m + 1)
    other = p[:, :, :].unsqueeze(2).broadcast_to([128, GT, e, e])
    own = p[:, :, :].unsqueeze(3).broadcast_to([128, GT, e, e])
    v.tensor_tensor(b["gt"][:, :, :, :], other, own, ALU.is_gt).then_inc(s["ggt"], 1)
    v.tensor_tensor(b["eq"][:, :, :, :], other, own, ALU.is_equal).then_inc(s["geq"], 1)
    v.wait_ge(s["geq"], m + 1)
    v.tensor_tensor(b["el"][:, :, :, :].rearrange("p a b c -> p a (b c)"), b["eq"][:, :, :, :].rearrange("p a b c -> p a (b c)"),
                    tie.unsqueeze(1).broadcast_to([128, GT, e * e]), ALU.mult).then_inc(s["gel"], 1)
    v.wait_ge(s["gel"], m + 1)
    v.tensor_tensor(b["rk"][:, :, :, :], b["el"][:, :, :, :], b["gt"][:, :, :, :], ALU.add).then_inc(s["grk"], 1)
    v.wait_ge(s["grk"], m + 1)
    v.tensor_reduce(b["rank"][:, :, :], b["rk"][:, :, :, :], AX_X, ALU.add).then_inc(s["grank"], 1)
    v.wait_ge(s["grank"], m + 1)
    v.tensor_scalar(b["sel"][:, :, :], b["rank"][:, :, :], 2.0, None, ALU.is_lt).then_inc(s["gsel"], 1)
    if again:
        v.tensor_reduce(b["gm"][:, :], p[:, :, :], AX_X, ALU.max).then_inc(s["ggm"], 1)
        v.wait_ge(s["ggm"], m + 1)
        v.tensor_tensor(b["dd"][:, :, :], p[:, :, :], each(b["gm"][:, :]), ALU.subtract).then_inc(s["gdd"], 1)
        v.wait_ge(s["gee"], m + 1)
        p = b["ee"]
    v.wait_ge(s["gsel"], m + 1)
    v.tensor_tensor(b["es"][:, :, :], p[:, :, :], b["sel"][:, :, :], ALU.mult).then_inc(s["ges"], 1)
    v.wait_ge(s["ges"], m + 1)
    v.tensor_reduce(b["zs"][:, :], b["es"][:, :, :], AX_X, ALU.add).then_inc(s["gzs"], 1)
    v.wait_ge(s["gzs"], m + 1)
    v.reciprocal(b["rzs"][:, :], b["zs"][:, :]).then_inc(s["grzs"], 1)
    v.wait_ge(s["grzs"], m + 1)
    v.tensor_tensor(w, b["es"][:, :, :], each(b["rzs"][:, :]), ALU.mult).then_inc(s["gw"], 1)


def groups(eng, prologue, body, epilogue):
    n = TILES // GT
    prologue()
    body(0, True, False)
    with eng.Fori(0, n - 2) as i:
        body(i + 1, False, False)
    body(n - 1, False, True)
    epilogue()


def norm_buffers(sb):
    b = {n: sb("n" + n, [128, GT]) for n in ("sm", "nm", "ve", "rs")}
    b["hc"], b["hs"] = sb("nhc", [128, GT, C]), sb("nhs", [128, GT, C])
    b["hn"] = sb("nhn", [128, GT + 1, C])
    b["half"] = sb("nhalf", [128, GT])
    return b


def routing_stage(nc, mem, e, gate_w, tie, bias, again):
    h_all, W, hT_all, wT_all = mem["h"], mem["W"], mem["hT"], mem["wT"]
    with ExitStack() as ctx:
        pre = f"r{e}_"
        sb = lambda n, s, d=F32: ctx.enter_context(nc.sbuf_tensor(pre + n, s, d))
        ps = lambda n, s, d=F32: ctx.enter_context(nc.psum_tensor(pre + n, s, d))
        nb, gb = norm_buffers(sb), gate_buffers(sb, e)
        hTg, wTg = sb("hTg", [128, GT * 128]), sb("wTg", [32, GT * 128])
        wg, rest = sb("wg", [128, GT, e]), sb("rest", [128, GT, e])
        pb = sb("pb", [128, GT, 2, e], BF16)
        wp = sb("wp", [128, GT, 32])
        t_ps, g_ps, b_ps = ps("t", [128, GT // 4, 512]), ps("g", [128, GT, e]), ps("b", [128, 2, 512])
        s = signals(nc, ctx, pre, "half ones ht_ps ht g_ps kept_h kept_w hi whi rest mid wp wt_ps wt b_ps biased " + norm_names() + " " + GATE_NAMES)
        bufs = [nb[n] for n in ("sm", "nm", "ve", "hc", "hs")]
        with nc.Block() as block:
            @block.gpsimd
            def _(pl):
                pl.memset(nb["half"][:, :], -0.5).then_inc(s["half"], 1)
                pl.wait_ge(s["half"], 1)

                def norm(g):
                    pl.wait_ge(s["ve"], g + 1)
                    pl.tensor_tensor(nb["rs"][:, :], nb["ve"][:, :], nb["half"][:, :], ALU.pow).then_inc(s["rs"], 1)
                    pl.wait_ge(s["ht"], 3 * g + 3)
                    pl.tensor_copy(hT_all[:, bass.ds(GT * 128 * g, GT * 128)], hTg[:, :]).then_inc(s["kept_h"], 1)

                def body(g, first, last):
                    if not last:
                        norm(g + 1)
                    pl.wait_ge(s["wt"], 3 * g + 3)
                    pl.tensor_copy(wT_all[:, bass.ds(GT * 128 * g, GT * 128)], wTg[:, :]).then_inc(s["kept_w"], 1)
                groups(pl, lambda: norm(0), body, lambda: None)

            @block.tensor
            def _(pe):
                pe.wait_ge(s["ones"], 2)

                def logits(g):
                    pe.wait_ge(s["hn"], g + 2)
                    for j in range(GT):
                        mm = pe.transpose(t_ps[:, j // 4, 128 * (j % 4):128 * (j % 4) + 128],
                                          nb["hn"][:, j:j + 2, :].rearrange("p a b -> p (a b)"), W("ident"))
                        if j % 4 == 3:
                            mm.then_inc(s["ht_ps"], 1)
                    pe.wait_ge(s["ht"], 3 * g + 3)
                    for j in range(GT):
                        mm = pe.matmul(g_ps[:, j, :], hTg[:, 128 * j:128 * j + 128], W(gate_w), start=True, stop=True)
                    mm.then_inc(s["g_ps"], 1)

                def body(g, first, last):
                    if not last:
                        logits(g + 1)
                    pe.wait_ge(s["wp"], g + 1)
                    for j in range(GT):
                        mm = pe.transpose(t_ps[0:32, j // 4, 128 * (j % 4):128 * (j % 4) + 128], wp[:, j, :], W("ident"))
                        if j % 4 == 3:
                            mm.then_inc(s["wt_ps"], 1)
                    pe.wait_ge(s["wt"], 3 * g + 3)
                    for j in range(GT):
                        mm = pe.matmul(b_ps[:, j // 6, 64 * (j % 6):64 * (j % 6) + 64], wTg[:, 128 * j:128 * j + 128], W(bias, rows=32),
                                       start=True, stop=True)
                    mm.then_inc(s["b_ps"], 1)
                groups(pe, lambda: logits(0), body, lambda: None)

            @block.scalar
            def _(act):
                def transposed(g, first):
                    if not first:
                        act.wait_ge(s["kept_h"], g)
                    for q in range(GT // 4):
                        act.wait_ge(s["ht_ps"], 3 * g + q + 1)
                        act.copy(hTg[0:64, 512 * q:512 * q + 512], t_ps[0:64, q, :]).then_inc(s["ht"], 1)

                def body(g, first, last):
                    act.wait_ge(s["gd"], g + 1)
                    act.activation(gb["e"][:, :, :], gb["d"][:, :, :], ACT.Exp).then_inc(s["ge"], 1)
                    if not last:
                        transposed(g + 1, False)
                    if again:
                        act.wait_ge(s["gdd"], g + 1)
                        act.activation(gb["ee"][:, :, :], gb["dd"][:, :, :], ACT.Exp).then_inc(s["gee"], 1)
                    if not first:
                        act.wait_ge(s["kept_w"], g)
                    for q in range(GT // 4):
                        act.wait_ge(s["wt_ps"], 3 * g + q + 1)
                        act.copy(wTg[:, 512 * q:512 * q + 512], t_ps[0:32, q, :]).then_inc(s["wt"], 1)
                groups(act, lambda: transposed(0, True), body, lambda: None)

            @block.vector
            def _(v):
                v.sem_inc(s["hn"], 1)
                v.memset(nb["hn"][:, GT, :], 0.0)
                v.memset(hTg[64:128, :], 0.0)
                v.memset(wp[:, :, :], 0.0).then_inc(s["ones"], 1)
                v.wait_ge(s["ones"], 1)
                v.memset(wp[:, :, 24:25], 1.0)
                v.memset(hTg[64:65, :], 1.0).then_inc(s["ones"], 1)
                v.wait_ge(s["ones"], 2)

                def tokens(g):
                    return h_all[:, bass.ds(GT * g, GT), :]

                def biased(g):
                    v.wait_ge(s["b_ps"], g + 1)
                    h = tokens(g).rearrange("p (a b) c -> p a (b c)", a=2)
                    v.tensor_tensor(h, h, b_ps[:, :, 0:384], ALU.add).then_inc(s["biased"], 1)

                def scaled(g):
                    layer_norm_scale(v, s, g, nb["rs"], nb["hc"], nb["hn"][:, 0:GT, :], GT)

                def prologue():
                    layer_norm(v, s, 0, tokens(0), GT, bufs)
                    scaled(0)

                def body(g, first, last):
                    if not last:
                        layer_norm(v, s, g + 1, tokens(g + 1), GT, bufs)
                    if not first:
                        biased(g - 1)
                    v.wait_ge(s["g_ps"], g + 1)
                    shifted(v, s, g, gb, g_ps[:, :, :], e)
                    if not last:
                        scaled(g + 1)
                    top_two(v, s, g, gb, e, W(tie), wg[:, :, :], again)
                    v.wait_ge(s["gw"], g + 1)
                    v.tensor_copy(pb[:, :, 0], wg[:, :, :]).then_inc(s["hi"], 1)
                    v.wait_ge(s["hi"], g + 1)
                    v.tensor_copy(wp[:, :, 0:e], pb[:, :, 0]).then_inc(s["whi"], 1)
                    v.tensor_tensor(rest[:, :, :], wg[:, :, :], pb[:, :, 0], ALU.subtract).then_inc(s["rest"], 1)
                    v.wait_ge(s["rest"], g + 1)
                    v.tensor_copy(pb[:, :, 1], rest[:, :, :]).then_inc(s["mid"], 1)
                    v.wait_ge(s["mid"], g + 1)
                    v.tensor_copy(wp[:, :, 8:8 + e], pb[:, :, 1]).then_inc(s["whi"], 1)
                    v.tensor_tensor(wp[:, :, 16:16 + e], rest[:, :, :], pb[:, :, 1], ALU.subtract).then_inc(s["wp"], 1)

                groups(v, prologue, body, lambda: biased(TILES // GT - 1))


def batches(eng, body, epilogue):
    body(0, 0, True)
    with eng.Fori(0, (B - 2) // 2) as i:
        body(2 * i + 1, 1, False)
        body(2 * i + 2, 0, False)
    body(B - 1, 1, False)
    epilogue()


def experts_stage(nc, mem):
    h_all, W, hT_all, wT_all = mem["h"], mem["W"], mem["hT"], mem["wT"]
    with ExitStack() as ctx:
        sb = lambda n, s, d=F32: ctx.enter_context(nc.sbuf_tensor("f_" + n, s, d))
        ps = lambda n, s, d=F32: ctx.enter_context(nc.psum_tensor("f_" + n, s, d))
        pick = sb("pick", [32, 2 * 128], BF16)
        h1 = [sb(f"h1{e}", [128, L]) for e in range(5)]
        h2 = [sb(f"h2{q}", [128, L]) for q in range(3)]
        h2w = [sb(f"h2w{q}", [128, L]) for q in range(2)]
        total = sb("total", [128, L])
        l1 = [ps(f"l1{k}", [128, 512]) for k in range(2)]
        l2 = [ps(f"l2{k}", [128, 512]) for k in range(2)]
        wb = [ps(f"wb{k}", [128, 512]) for k in range(2)]
        acc, o_ps = ps("acc", [128, 512]), ps("o", [128, NT, C])
        s = signals(nc, ctx, "f_", "pick l1_ps h1 wb_ps l2_ps h2 h2w l3_ps total o_ps h")

        with nc.Block() as block:
            @block.tensor
            def _(pe):
                pe.sem_inc(s["o_ps"], 1)
                pe.wait_ge(s["pick"], 1)

                def first_layer(n, k, e):
                    pe.wait_ge(s["h1"], 5 * n + e + 1)
                    w1 = W("ew1", 128 * e, 128) if e < 4 else W("sw1")
                    pe.matmul(l1[(k + e) % 2][:, 0:L], w1, hT_all[:, bass.ds(L * n, L)], start=True, stop=True).then_inc(s["l1_ps"], 1)

                def weights(n):
                    for q in range(2):
                        pe.matmul(wb[q][:, 0:L], pick[:, 128 * q:128 * q + 128], wT_all[:, bass.ds(L * n, L)], start=True, stop=True)\
                            .then_inc(s["wb_ps"], 1)

                def second_layer(n, k, q):
                    pe.wait_ge(s["h1"], 5 * n + (4, 6, 7)[q])
                    pe.wait_ge(s["h2"], 3 * n + q + 1)
                    bank = l2[(k + q) % 2]
                    if q < 2:
                        for half in range(2):
                            mm = pe.matmul(bank[64 * half:64 * half + 64, 0:L], W("ew2", 64 * (2 * q + half), 64), h1[2 * q + half][:, :],
                                           start=True, stop=True)
                    else:
                        mm = pe.matmul(bank[:, 0:L], W("sw2"), h1[4][:, :], start=True, stop=True)
                    mm.then_inc(s["l2_ps"], 1)

                def third_layer(n, q):
                    if q < 2:
                        pe.wait_ge(s["h2w"], 2 * n + q + 3)
                    else:
                        pe.wait_ge(s["h2"], 3 * n + 5)
                    if q == 0:
                        pe.wait_ge(s["total"], n + 1)
                    half = q % 2
                    pe.matmul(acc[64 * half:64 * half + 64, 0:L], W("sw3") if q == 2 else W("ew3", 64 * q, 64), (h2w + h2[2:])[q][:, :],
                              start=(q < 2), stop=(q > 0)).then_inc(s["l3_ps"], 1)

                def back(n):
                    pe.wait_ge(s["total"], n + 2)
                    pe.wait_ge(s["h"], n + 1)
                    for j in range(NT):
                        mm = pe.matmul(o_ps[:, j, :], total[:, 128 * j:128 * j + 128], W("both"), start=True, stop=True)
                    mm.then_inc(s["o_ps"], 1)

                def body(n, k, first):
                    first_layer(n, k, 0)
                    pe.wait_ge(s["h2w"], 2 * n + 2)
                    first_layer(n, k, 1)
                    weights(n)
                    if not first:
                        third_layer(n - 1, 0)
                        third_layer(n - 1, 1)
                    first_layer(n, k, 2)
                    second_layer(n, k, 0)
                    if not first:
                        third_layer(n - 1, 2)
                    first_layer(n, k, 3)
                    first_layer(n, k, 4)
                    second_layer(n, k, 1)
                    if not first:
                        back(n - 1)
                    second_layer(n, k, 2)

                def epilogue():
                    for q in range(3):
                        third_layer(B - 1, q)
                    back(B - 1)
                batches(pe, body, epilogue)

            @block.scalar
            def _(act):
                act.sem_inc(s["h1"], 2)
                act.sem_inc(s["h2"], 2)
                act.sem_inc(s["total"], 1)
                act.copy(pick[:, :], W("pick0", rows=32)).then_inc(s["pick"], 1)

                def first_relu(n, k, e, first):
                    act.wait_ge(s["l1_ps"], 5 * n + e + 1)
                    if not first:
                        act.wait_ge(s["l2_ps"], 3 * n - 2 + e // 2)
                    act.activation(h1[e][:, :], l1[(k + e) % 2][:, 0:L], ACT.Relu).then_inc(s["h1"], 1)

                def second_relu(n, k, q, first):
                    act.wait_ge(s["l2_ps"], 3 * n + q + 1)
                    if not first and q < 2:
                        act.wait_ge(s["h2w"], 2 * n + q + 1)
                    elif not first:
                        act.wait_ge(s["l3_ps"], 3 * n)
                    act.activation(h2[q][:, :], l2[(k + q) % 2][:, 0:L], ACT.Relu, bias=W("sb2") if q == 2 else W("eb2", q, 1)).then_inc(s["h2"], 1)

                def summed(n):
                    act.wait_ge(s["l3_ps"], 3 * n + 3)
                    act.wait_ge(s["o_ps"], n + 1)
                    act.copy(total[:, :], acc[:, 0:L]).then_inc(s["total"], 1)

                def body(n, k, first):
                    first_relu(n, k, 0, first)
                    first_relu(n, k, 1, first)
                    first_relu(n, k, 2, first)
                    second_relu(n, k, 0, first)
                    first_relu(n, k, 3, first)
                    if not first:
                        summed(n - 1)
                    first_relu(n, k, 4, first)
                    second_relu(n, k, 1, first)
                    second_relu(n, k, 2, first)
                batches(act, body, lambda: summed(B - 1))

            @block.vector
            def _(v):
                v.sem_inc(s["h2w"], 2)
                v.sem_inc(s["h"], 1)

                def weigh(n, q, first):
                    v.wait_ge(s["wb_ps"], 2 * n + q + 1)
                    v.wait_ge(s["h2"], 3 * n + q + 3)
                    if not first:
                        v.wait_ge(s["l3_ps"], 3 * n - 2 + q)
                    v.tensor_tensor(h2w[q][:, :], h2[q][:, :], wb[q][:, 0:L], ALU.mult).then_inc(s["h2w"], 1)

                def added(n):
                    v.wait_ge(s["o_ps"], n + 2)
                    h = h_all[:, bass.ds(NT * n, NT), :]
                    v.tensor_tensor(h, h, o_ps[:, :, :], ALU.add).then_inc(s["h"], 1)

                def body(n, k, first):
                    weigh(n, 0, first)
                    if not first:
                        added(n - 1)
                    weigh(n, 1, first)
                batches(v, body, lambda: added(B - 1))


def gate_stage(nc, mem):
    h_all, W = mem["h"], mem["W"]
    with ExitStack() as ctx:
        sb = lambda n, s, d=F32: ctx.enter_context(nc.sbuf_tensor("g_" + n, s, d))
        ps = lambda n, s, d=F32: ctx.enter_context(nc.psum_tensor("g_" + n, s, d))
        nb = norm_buffers(sb)
        hTg = sb("hTg", [128, GT * 128])
        one = sb("one", [64, 1])
        halfb = sb("halfb", [64, 1])
        th, sg = (sb(n, [64, GT // 4, 512]) for n in ("th", "sg"))
        y = sb("y", [128, GT // 4, 512])
        t_ps, g_ps = ps("t", [128, GT // 4, 512]), ps("g", [128, GT // 4, 512])
        o_ps = ps("o", [128, 2, 512])
        s = signals(nc, ctx, "g_", "half ones halfb ht_ps ht g_ps th sg y o_ps h " + norm_names())
        bufs = [nb[n] for n in ("sm", "nm", "ve", "hc", "hs")]
        with nc.Block() as block:
            @block.gpsimd
            def _(pl):
                pl.memset(one[:, :], 1.0)
                pl.memset(nb["half"][:, :], -0.5).then_inc(s["half"], 1)
                pl.wait_ge(s["half"], 1)

                def norm(g):
                    pl.wait_ge(s["ve"], g + 1)
                    pl.tensor_tensor(nb["rs"][:, :], nb["ve"][:, :], nb["half"][:, :], ALU.pow).then_inc(s["rs"], 1)

                def body(g, first, last):
                    if not last:
                        norm(g + 1)
                    pl.wait_ge(s["y"], g + 1)
                    for q in range(GT // 4):
                        pl.wait_ge(s["th"], 3 * g + q + 1)
                        pl.tensor_tensor(sg[:, q, :], th[:, q, :], one[:, :].broadcast_to([64, 512]), ALU.add).then_inc(s["sg"], 1)
                groups(pl, lambda: norm(0), body, lambda: None)

            @block.tensor
            def _(pe):
                pe.wait_ge(s["ones"], 2)

                def gates(g):
                    pe.wait_ge(s["hn"], g + 2)
                    for j in range(GT):
                        mm = pe.transpose(t_ps[:, j // 4, 128 * (j % 4):128 * (j % 4) + 128],
                                          nb["hn"][:, j:j + 2, :].rearrange("p a b -> p (a b)"), W("ident"))
                        if j % 4 == 3:
                            mm.then_inc(s["ht_ps"], 1)
                    for q in range(GT // 4):
                        pe.wait_ge(s["ht"], 3 * g + q + 1)
                        pe.matmul(g_ps[:, q, :], W("glg", 0, 128), hTg[:, 512 * q:512 * q + 512], start=True, stop=True).then_inc(s["g_ps"], 1)

                def outputs(g):
                    pe.wait_ge(s["y"], g + 2)
                    for j in range(GT):
                        mm = pe.matmul(o_ps[:, j // 6, 64 * (j % 6):64 * (j % 6) + 64], y[:, j // 4, 128 * (j % 4):128 * (j % 4) + 128],
                                       W("glo"), start=True, stop=True)
                    mm.then_inc(s["o_ps"], 1)

                def body(g, first, last):
                    outputs(g)
                    if not last:
                        gates(g + 1)
                groups(pe, lambda: gates(0), body, lambda: None)

            @block.scalar
            def _(act):
                def gates(g):
                    for q in range(GT // 4):
                        act.wait_ge(s["ht_ps"], 3 * g + q + 1)
                        act.copy(hTg[0:64, 512 * q:512 * q + 512], t_ps[0:64, q, :]).then_inc(s["ht"], 1)
                    for q in range(GT // 4):
                        act.wait_ge(s["g_ps"], 3 * g + q + 1)
                        act.activation(th[:, q, :], g_ps[0:64, q, :], ACT.Tanh, scale=0.5).then_inc(s["th"], 1)

                groups(act, lambda: gates(0), lambda g, first, last: None if last else gates(g + 1), lambda: None)

            @block.vector
            def _(v):
                v.sem_inc(s["hn"], 1)
                v.sem_inc(s["y"], 1)
                v.memset(nb["hn"][:, GT, :], 0.0)
                v.memset(hTg[64:128, :], 0.0)
                v.tensor_scalar(halfb[:, :], W("gnb", rows=64), 0.5, None, ALU.mult)
                v.memset(y[64:128, :, :], 0.0).then_inc(s["ones"], 1)
                v.wait_ge(s["ones"], 1)
                v.memset(y[64:65, :, :], 1.0).then_inc(s["ones"], 1)
                v.wait_ge(s["ones"], 2)

                def tokens(g):
                    return h_all[:, bass.ds(GT * g, GT), :]

                def norm(g):
                    layer_norm(v, s, g, tokens(g), GT, bufs)

                def scaled(g):
                    layer_norm_scale(v, s, g, nb["rs"], nb["hc"], nb["hn"][:, 0:GT, :], GT)

                def added(g):
                    v.wait_ge(s["o_ps"], g + 1)
                    h = tokens(g).rearrange("p (a b) c -> p a (b c)", a=2)
                    v.tensor_tensor(h, h, o_ps[:, :, 0:384], ALU.add).then_inc(s["h"], 1)

                def prologue():
                    norm(0)
                    scaled(0)

                def body(g, first, last):
                    if not last:
                        norm(g + 1)
                    v.wait_ge(s["sg"], 3 * g + 3)
                    v.scalar_tensor_tensor(y[0:64, :, :], g_ps[0:64, :, :], halfb[:, :], sg[:, :, :], ALU.mult, ALU.mult).then_inc(s["y"], 1)
                    if not last:
                        scaled(g + 1)
                    added(g)
                groups(v, prologue, body, lambda: None)


def gelu_experts_stage(nc, mem):
    h_all, W, hT_all, wT_all = mem["h"], mem["W"], mem["hT"], mem["wT"]
    NE, LAG = E1 + 1, 2
    with ExitStack() as ctx:
        sb = lambda n, s, d=F32: ctx.enter_context(nc.sbuf_tensor("x_" + n, s, d))
        ps = lambda n, s, d=F32: ctx.enter_context(nc.psum_tensor("x_" + n, s, d))
        pick = sb("pick", [32, E1 * 128], BF16)
        g = [sb(f"g{k}", [128, 2, L]) for k in range(3)]
        gw = [sb(f"gw{k}", [128, 2, L]) for k in range(2)]
        total = sb("total", [128, L])
        l1 = [ps(f"l1{k}", [128, 2, 512]) for k in range(2)]
        wb = [ps(f"wb{k}", [128, 512]) for k in range(2)]
        acc, o_ps = ps("acc", [128, 512]), ps("o", [128, NT, C])
        s = signals(nc, ctx, "x_", "pick l1_ps wb_ps g gw l2_ps total o_ps h")

        with nc.Block() as block:
            @block.tensor
            def _(pe):
                pe.sem_inc(s["o_ps"], 1)
                pe.wait_ge(s["pick"], 1)

                def second_layer(n, q):
                    if q < E1:
                        pe.wait_ge(s["gw"], E1 * n + q + 3)
                    else:
                        pe.wait_ge(s["g"], NE * n + q + 3)
                    if q == 0:
                        pe.wait_ge(s["total"], n + 1)
                    src = gw[q % 2] if q < E1 else g[q % 3]
                    for f in range(2):
                        mm = pe.matmul(acc[64 * f:64 * f + 64, 0:L], W("w2", 128 * q + C * f, C), src[:, f, :], start=(q == 0), stop=(q == NE - 1))
                    mm.then_inc(s["l2_ps"], 1)

                def back(n):
                    pe.wait_ge(s["total"], n + 2)
                    pe.wait_ge(s["h"], n + 1)
                    for j in range(NT):
                        mm = pe.matmul(o_ps[:, j, :], total[:, 128 * j:128 * j + 128], W("both"), start=True, stop=True)
                    mm.then_inc(s["o_ps"], 1)

                def body(n, k, first):
                    for e in range(NE):
                        pe.wait_ge(s["g"], NE * n + e + 1)
                        for f in range(2):
                            if f == 1 and e < E1:
                                pe.wait_ge(s["gw"], E1 * n + e + 1)
                            mm = pe.matmul(l1[(k + e) % 2][:, f, 0:L], W("w1", F1 * e + 128 * f, 128), hT_all[:, bass.ds(L * n, L)],
                                           start=True, stop=True)
                        mm.then_inc(s["l1_ps"], 1)
                        if e < E1:
                            pe.matmul(wb[e % 2][:, 0:L], pick[:, 128 * e:128 * e + 128], wT_all[:, bass.ds(L * n, L)], start=True, stop=True)\
                                .then_inc(s["wb_ps"], 1)
                        if e >= LAG:
                            second_layer(n, e - LAG)
                        elif not first:
                            second_layer(n - 1, e - LAG + NE)
                        if e == 3 and not first:
                            back(n - 1)

                def epilogue():
                    for q in range(NE - LAG, NE):
                        second_layer(B - 1, q)
                    back(B - 1)
                batches(pe, body, epilogue)

            @block.scalar
            def _(act):
                act.sem_inc(s["g"], 2)
                act.sem_inc(s["total"], 1)
                act.copy(pick[:, :], W("pick1", rows=32)).then_inc(s["pick"], 1)

                def summed(n):
                    act.wait_ge(s["l2_ps"], NE * n + NE)
                    act.wait_ge(s["o_ps"], n + 1)
                    act.copy(total[:, :], acc[:, 0:L]).then_inc(s["total"], 1)

                def body(n, k, first):
                    for e in range(NE):
                        act.wait_ge(s["l1_ps"], NE * n + e + 1)
                        if e >= 3:
                            act.wait_ge(s["gw"], E1 * n + e)
                        elif not first and e < 2:
                            act.wait_ge(s["gw"], E1 * n + e + 1)
                        elif not first:
                            act.wait_ge(s["l2_ps"], NE * n)
                        act.activation(g[e % 3][:, :, :], l1[(k + e) % 2][:, :, 0:L], ACT.Gelu).then_inc(s["g"], 1)
                        if e == 1 and not first:
                            summed(n - 1)
                batches(act, body, lambda: summed(B - 1))

            @block.vector
            def _(v):
                v.sem_inc(s["gw"], 2)
                v.sem_inc(s["h"], 1)

                def added(n):
                    v.wait_ge(s["o_ps"], n + 2)
                    h = h_all[:, bass.ds(NT * n, NT), :]
                    v.tensor_tensor(h, h, o_ps[:, :, :], ALU.add).then_inc(s["h"], 1)

                def body(n, k, first):
                    for e in range(E1):
                        v.wait_ge(s["g"], NE * n + e + 3)
                        v.wait_ge(s["wb_ps"], E1 * n + e + 1)
                        if e >= 2:
                            v.wait_ge(s["l2_ps"], NE * n + e - 1)
                        elif not first:
                            v.wait_ge(s["l2_ps"], NE * n - 2 + e)
                        v.tensor_tensor(gw[e % 2][:, :, :], g[e % 3][:, :, :], wb[e % 2][:, 0:L].unsqueeze(1).broadcast_to([128, 2, L]),
                                        ALU.mult).then_inc(s["gw"], 1)
                        if e == 4 and not first:
                            added(n - 1)
                batches(v, body, lambda: added(B - 1))


def early_fusion_program(nc, x, txt, pack, out):
    with ExitStack() as ctx:
        w = ctx.enter_context(nc.sbuf_tensor("w", [128, WCOLS], F32))
        h = ctx.enter_context(nc.sbuf_tensor("h", [128, TILES, C], F32))

        def W(name, col=0, cols=None, rows=128):
            at, width = AT[name]
            return w[0:rows, at + col:at + col + (width if cols is None else cols)]

        mem = {"w": w, "h": h, "W": W}
        load_stage(nc, mem, pack, txt)
        tok_stage(nc, mem, x)
        attention_stage(nc, mem)
        with (nc.sbuf_tensor("hT", [128, B * L], F32) as hT, nc.sbuf_tensor("wT", [32, B * L], BF16) as wT):
            mem["hT"], mem["wT"] = hT, wT
            routing_stage(nc, mem, E0, "gw", "tie0", "bias0", True)
            experts_stage(nc, mem)
            gate_stage(nc, mem)
            routing_stage(nc, mem, E1, "wr", "tie1", "bias1", False)
            gelu_experts_stage(nc, mem)
        store_stage(nc, mem, out)


def kernel(**inputs):
    import numpy as np
    import concourse.bacc as _bacc
    from concourse import mybir as _mybir
    from concourse.bass_utils import run_bass_kernel_spmd as _run

    f32 = np.float32
    w = {k: np.ascontiguousarray(v) for k, v in inputs.items()}
    pack = np.zeros((128, WCOLS), f32)

    def put(name, value, row=0, col=0):
        at, _ = AT[name]
        value = value.reshape(value.shape[0], -1)
        pack[row:row + value.shape[0], at + col:at + col + value.shape[1]] = value

    def rows(name, vector, col=0):
        put(name, np.broadcast_to(vector.reshape(1, -1), (128, vector.size)), 0, col)

    def twice(name, block):
        put(name, block)
        put(name, block, 64, 64)

    put("ident", np.eye(128, dtype=f32))
    head_of = np.repeat(np.eye(16, dtype=f32), 8, axis=0)
    full = np.zeros((128, 8, 8, 16), f32)
    for c in range(8):
        full[:, c, c, :] = head_of
    put("sel", full)
    put("selT", full.reshape(128, 8, 128).transpose(2, 1, 0))
    center = np.eye(64, dtype=f32) - np.full((64, 64), 1 / 64, f32)
    twice("center", center)
    for c in range(4):
        for image in range(2):
            put("blk", np.full((64, 1), 1 / 64, f32), 64 * image, 32 * c + 2 * c + image)
    lower = lambda n: np.array([[1.0 if j < i else 0.0 for j in range(n)] for i in range(n)], f32)
    rows("tie0", lower(E0))
    rows("tie1", lower(E1))
    twice("tq", w["L0_tok_Wq"].T)
    twice("tk", w["L0_tok_Wkv"][:64].T)
    twice("tv", w["L0_tok_Wkv"][64:].T)
    twice("tproj", w["L0_tok_proj_w"].T)
    for r in (0, 64):
        put("kvw", w["L0_tok_ln_kv_w"][:, None], r)
        put("kvb", w["L0_tok_ln_kv_b"][:, None], r)
    rows("lnqw", w["L0_tok_ln_q_w"])
    rows("lnqb", w["L0_tok_ln_q_b"])
    rows("projb", w["L0_tok_proj_b"])
    put("aqk", w["L0_attn_Wq"])
    put("aqk", w["L0_attn_Wkv"][:, :INNER], 0, INNER)
    put("avg", w["L0_attn_Wkv"][:, INNER:])
    put("avg", w["L0_attn_Wg"], 0, INNER)
    put("avg", w["L0_attn_bg"][None], 64, INNER)
    put("aout", w["L0_attn_Wout"][:128])
    put("aout", w["L0_attn_Wout"][128:], 0, 64)
    rows("aoutb", w["L0_attn_bout"])
    rows("gam", w["L0_attn_ln_gamma"])
    rows("bet", w["L0_attn_ln_beta"])
    for i, n in enumerate(("lq1", "lk1", "lq2", "lk2")):
        rows("lqk", w["L0_attn_" + n], 16 * i)
    put("sw1", w["L0_ffn_sW1"])
    put("sw1", w["L0_ffn_sb1"][None], 64)
    put("ew1", w["L0_ffn_eW1"].transpose(1, 0, 2))
    put("ew1", w["L0_ffn_eb1"].reshape(1, -1), 64)
    put("gw", w["L0_ffn_gW"])
    put("gw", w["L0_ffn_gb"][None], 64)
    put("sw2", w["L0_ffn_sW2"])
    put("sb2", w["L0_ffn_sb2"][:, None])
    put("sw3", w["L0_ffn_sW3"])
    put("ew2", w["L0_ffn_eW2"].transpose(1, 0, 2))
    put("eb2", w["L0_ffn_eb2"].reshape(2, 128).T)
    for e in range(E0):
        put("ew3", w["L0_ffn_eW3"][e], 64 * (e % 2), 64 * (e // 2))
    for part in range(3):
        put("bias0", w["L0_ffn_eb3"], 8 * part)
        put("bias1", w["L1_ffn_b2p"], 8 * part)
        put("pick0", np.repeat(np.eye(E0, dtype=f32), 64, axis=1), 8 * part)
        put("pick1", np.repeat(np.eye(E1, dtype=f32), 128, axis=1), 8 * part)
    put("bias0", w["L0_ffn_sb3"][None], 24)
    put("bias1", w["L1_ffn_b2s"][None], 24)
    put("both", np.tile(np.eye(64, dtype=f32), (2, 1)))
    put("glg", w["L1_attn_wg"])
    put("glo", w["L1_attn_wo"])
    put("gnb", w["L1_attn_gn_bias"][:, None])
    put("glo", w["L1_attn_bias"][None], 64)
    put("wr", w["L1_ffn_Wr"])
    put("w1", w["L1_ffn_W1p"].transpose(1, 0, 2))
    put("w1", w["L1_ffn_b1p"].reshape(1, -1), 64)
    put("w1", w["L1_ffn_W1s"], 0, 8 * F1)
    put("w1", w["L1_ffn_b1s"][None], 64, 8 * F1)
    put("w2", w["L1_ffn_W2p"].reshape(8, 2, 128, 64).transpose(2, 0, 1, 3))
    put("w2", w["L1_ffn_W2s"].reshape(2, 128, 64).transpose(1, 0, 2), 0, 8 * 128)

    arrays = {"x": w["x"].reshape(B // 2, 128, IMG * IMG), "txt": w["txt"], "pack": pack}
    nc = _bacc.Bacc("TRN2", target_bir_lowering=False, num_devices=1)
    args = [nc.dram_tensor(f"{k}_dram", a.shape, _mybir.dt.from_np(a.dtype), kind="ExternalInput").ap()
            for k, a in arrays.items()]
    args.append(nc.dram_tensor("out_dram", (B, L, C), _mybir.dt.float32, kind="ExternalOutput").ap())
    early_fusion_program(nc, *args)
    r = _run(nc, [{f"{k}_dram": a for k, a in arrays.items()}], core_ids=[0])
    return r.results[0]["out_dram"]
```

```python
import math
from contextlib import ExitStack

import concourse.bass as bass
from concourse import mybir

B, C, IMG = 32, 64, 64
TXT = 128
STRIDE, TOK_HEADS = 4, 8
SIDE = IMG // STRIDE
PATCHES = SIDE * SIDE
L = PATCHES + TXT
NT = L // 128
TILES = B * NT
HEADS, DH = 8, 16
DV = 2 * DH
INNER = HEADS * DV
E0, E0_H1, E0_H2, S0_H1, S0_H2 = 4, 128, 64, 64, 128
E1, F1 = 8, 256
EPS = 1e-5
LAMBDA_INIT = 0.8 - 0.6 * math.exp(-0.3)

FIELDS = [
    ("ident", 128), ("sel", 1024), ("selT", 1024), ("center", 128), ("blk", 128),
    ("tq", 128), ("tk", 128), ("tv", 128), ("tproj", 128), ("kvw", 1), ("kvb", 1),
    ("lnqw", 64), ("lnqb", 64), ("projb", 64),
    ("aqk", 512), ("avg", 512), ("aout", 128), ("aoutb", 64), ("gam", 32), ("bet", 32), ("lqk", 64),
    ("sw1", 128), ("ew1", 512), ("gw", 4), ("sw2", 128), ("sb2", 1), ("sw3", 64), ("ew2", 256), ("eb2", 2),
    ("ew3", 128), ("bias0", 64), ("pick0", 256), ("both", 64), ("tie0", 16),
    ("glg", 64), ("glo", 64), ("gnb", 1),
    ("wr", 8), ("w1", 9 * F1), ("w2", 9 * 128), ("bias1", 64), ("pick1", 1024), ("tie1", 64),
]
AT = {}
_n = 0
for _name, _w in FIELDS:
    AT[_name] = (_n, _w)
    _n += _w
WCOLS = _n


F32 = mybir.dt.float32
BF16 = mybir.dt.bfloat16
ALU = mybir.AluOpType
ACT = mybir.ActivationFunctionType
AX_X, AX_XY = mybir.AxisListType.X, mybir.AxisListType.XY


def signals(nc, ctx, prefix, names):
    sems = {n: nc.alloc_semaphore(name=prefix + n) for n in names.split()}

    def clear():
        nc.clear_and_free_semaphores(list(sems.values()))
        nc.all_engine_barrier()

    ctx.callback(clear)
    return sems


def load_stage(nc, mem, pack, txt):
    with nc.semaphore("loaded") as loaded, nc.Block() as block:
        @block.sync
        def _(sp):
            sp.dma_start(mem["w"][:, :], pack).then_inc(loaded, 16)
            sp.dma_start(mem["h"][:, 2:TILES:NT, :], txt.rearrange("b l d -> l b d")).then_inc(loaded, 16)
            sp.wait_ge(loaded, 32)


def store_stage(nc, mem, out):
    with nc.semaphore("stored") as stored, nc.Block() as block:
        @block.sync
        def _(sp):
            sp.dma_start(out.rearrange("b (j p) c -> p (b j) c", p=128), mem["h"][:, :, :]).then_inc(stored, 16)
            sp.wait_ge(stored, 16)


def tok_stage(nc, mem, x):
    h_all, W = mem["h"], mem["W"]
    CH, PAIRS = 8, B // 2
    with ExitStack() as ctx:
        sb = lambda n, s, d=F32: ctx.enter_context(nc.sbuf_tensor("t_" + n, s, d))
        ps = lambda n, s, d=F32: ctx.enter_context(nc.psum_tensor("t_" + n, s, d))
        xb = [sb(f"x{k}", [128, 4096]) for k in range(2)]
        sq = sb("sq", [128, 4096])
        wk, wv = sb("wk", [128, 128]), sb("wv", [128, 128])
        wk0, wv0 = sb("wk0", [128, 128]), sb("wv0", [128, 128])
        kb, vb = sb("kb", [128, 1]), sb("vb", [128, 1])
        half = sb("half", [128, 64])
        r1, r2, r3 = sb("r1", [128, 1024, 2]), sb("r2", [128, 16, 4, 16]), sb("r3", [128, 16, 2, 16])
        rf = sb("rf", [128, PATCHES])
        rt = [sb(f"rt{k}", [128, 4, 64]) for k in range(2)]
        hc, hs, qn = sb("hc", [128, 4, 64]), sb("hs", [128, 4, 64]), sb("qn", [128, 4, 64])
        sm, nm, ve, rs = (sb(n, [128, 4]) for n in ("sm", "nm", "ve", "rs"))
        qnT = sb("qnT", [128, 256])
        qx = sb("qx", [128, 256, 4])
        t0 = sb("t0", [128, 256])
        tb = [sb(f"tb{k}", [128, 512]) for k in range(2)]
        stT = sb("stT", [128, 512])
        st = sb("st", [128, 4, 4, 8])
        m2, va, rr = (sb(n, [128, 4, 2, 8]) for n in ("m2", "va", "rr"))
        rrep = sb("rrep", [128, 4, 8, 2, 8])
        rp = sb("rp", [128, 512])
        c0 = sb("c0", [128, 32, 4])
        s1, s2, s3, ex, p1, p2 = (sb(n, [128, 512]) for n in ("s1", "s2", "s3", "ex", "p1", "p2"))
        mx, z, rz = (sb(n, [128, 32]) for n in ("mx", "z", "rz"))
        mxx, rzx = sb("mxx", [128, 32, 4]), sb("rzx", [128, 32, 4])
        vs = [sb(f"vs{k}", [128, 512]) for k in range(2)]
        pv = [sb(f"pv{k}", [128, 512]) for k in range(2)]
        agg, agb = sb("agg", [128, 256]), sb("agb", [128, 256])
        po = sb("po", [128, 4, 64])
        ahead_ps, misc = ps("ahead", [128, 512]), ps("misc", [128, 512])
        stats_ps = ps("stats", [128, 512])
        kv_ps = [ps(f"kv{k}", [128, 512]) for k in range(2)]
        sps = ps("s", [128, 512])
        bps = [ps(f"b{k}", [128, 512]) for k in range(2)]
        s = signals(nc, ctx, "t_", """wfold wcent wready half x_in0 x_in1 r1 r2 r3 rf rfT rt sm nm hc hs ssq ve rs hn hnw qn qnT_ps qnT
            q_ps qx t0 sq stat_mm stT stat_ps st m2 va vae rr rrep rr_ps rp k_ps tb  s_ps  c0_ps c0 s1 s2 mx mxx s3
            ex z rz rzx p1 p2 v_ps vs b_ps b_used agg agb o_ps po o_done""")

        grid = lambda ap: ap.rearrange("p (a s w t) -> p a w s t", s=4, w=16, t=4)
        strips = lambda ap: ap.rearrange("p (a s m) -> p a s m", s=4, m=64)
        over_rows = lambda ap, a: ap.rearrange("p (a o w) t -> p a o (w t)", a=a, o=1).broadcast_to([128, a, 4, 64])
        each = lambda ap, n, k: ap.unsqueeze(2).broadcast_to([128, n, k])

        def bodies(eng, prologue, body, epilogue):
            prologue()
            body(0, 0, 0, True, False)
            body(1, 1, 0, False, False)
            with eng.Fori(0, PAIRS // 2 - 2) as i:
                body(2 * i + 2, 0, i + 1, False, False)
                body(2 * i + 3, 1, i + 1, False, False)
            body(PAIRS - 2, 0, PAIRS // 2 - 1, False, False)
            body(PAIRS - 1, 1, PAIRS // 2 - 1, False, True)
            epilogue()

        with nc.Block() as block:
            @block.sync
            def _(sp):
                def load(m, k):
                    sp.dma_start(xb[k][:, :], x[bass.ds(m, 1), :, :].rearrange("o p m -> (o p) m")).then_inc(s[f"x_in{k}"], 16)

                load(0, 0)
                load(1, 1)
                with sp.Fori(0, PAIRS // 2 - 1) as i:
                    for k in range(2):
                        m = 2 * i + 2 + k
                        sp.wait_ge(s["v_ps"], CH * m - CH)
                        load(m, k)

            @block.gpsimd
            def _(pl):
                pl.memset(half[:, :], -0.5).then_inc(s["half"], 1)
                pl.wait_ge(s["half"], 1)

                def ahead(m, k, i, first=False):
                    pl.wait_ge(s[f"x_in{k}"], 16 * i + 16)
                    pixels = xb[k][:, :].rearrange("p (a t) -> p a t", t=4)
                    pl.tensor_tensor(r1[:, :, :], pixels[:, :, 0:2], pixels[:, :, 2:4], ALU.add).then_inc(s["r1"], 1)
                    pl.wait_ge(s["r1"], m + 1)
                    pl.tensor_tensor(r2[:, :, :, :].rearrange("p a s w -> p (a s w)"), r1[:, :, 0], r1[:, :, 1], ALU.add).then_inc(s["r2"], 1)
                    pl.wait_ge(s["r2"], m + 1)
                    pl.tensor_tensor(r3[:, :, :, :], r2[:, :, 0:2], r2[:, :, 2:4], ALU.add).then_inc(s["r3"], 1)
                    pl.wait_ge(s["r3"], m + 1)
                    if not first:
                        pl.wait_ge(s["rfT"], m)
                    pl.tensor_tensor(rf[:, :].rearrange("p (a w) -> p a w", w=16), r3[:, :, 0], r3[:, :, 1], ALU.add).then_inc(s["rf"], 1)
                    pl.wait_ge(s["ve"], m + 1)
                    pl.tensor_tensor(rs[:, :], ve[:, :], half[:, 0:4], ALU.pow).then_inc(s["rs"], 1)
                    pl.wait_ge(s["vae"], m + 1)
                    pl.tensor_tensor(rr[:, :, :, :].rearrange("p a b c -> p (a b c)"), va[:, :, :, :].rearrange("p a b c -> p (a b c)"),
                                     half[:, 0:64], ALU.pow).then_inc(s["rr"], 1)

                bodies(pl, lambda: ahead(0, 0, 0, True), lambda n, k, i, first, last: None if last else ahead(n + 1, 1 - k, i + k), lambda: None)

            @block.tensor
            def _(pe):
                pe.sem_inc(s["s_ps"], 2)
                pe.sem_inc(s["stat_mm"], 1)
                pe.wait_ge(s["wfold"], 2)
                pe.matmul(misc[:, 0:128], W("center"), wk0[:, :], start=True, stop=True)
                pe.matmul(misc[:, 128:256], W("center"), wv0[:, :], start=True, stop=True)
                pe.matmul(misc[:, 256:257], W("tk"), W("kvb"), start=True, stop=True)
                pe.matmul(misc[:, 257:258], W("tv"), W("kvb"), start=True, stop=True).then_inc(s["wcent"], 1)
                pe.wait_ge(s["wready"], 1)

                def stats(m, k):
                    pe.wait_ge(s["stT"], m + 1)
                    pe.wait_ge(s["sq"], 4 * m + 4)
                    for c in range(4):
                        for g in range(4):
                            at = 512 * (4 * (g % 2) + c)
                            mm = pe.matmul(stats_ps[32 * g:32 * g + 32, :], W("blk", 32 * c, 32), (xb[k] if g < 2 else sq)[:, at:at + 512],
                                           start=(c == 0), stop=(c == 3))
                    mm.then_inc(s["stat_mm"], 1)

                def stats_back(m):
                    pe.wait_ge(s["qx"], m + 1)
                    pe.wait_ge(s["stT"], m + 2)
                    for j in range(4):
                        mm = pe.transpose(ahead_ps[:, 128 * j:128 * j + 128], stT[:, 128 * j:128 * j + 128], W("ident"))
                    mm.then_inc(s["stat_ps"], 1)

                def patches(m):
                    pe.wait_ge(s["rf"], m + 1)
                    pe.wait_ge(s["st"], m + 1)
                    for j in range(2):
                        mm = pe.transpose(ahead_ps[:, 128 * j:128 * j + 128], rf[:, 128 * j:128 * j + 128], W("ident"))
                    mm.then_inc(s["rfT"], 1)

                def queries(m):
                    pe.wait_ge(s["qn"], m + 1)
                    for j in range(2):
                        mm = pe.transpose(ahead_ps[:, 128 * j:128 * j + 128],
                                          qn[:, 2 * j:2 * j + 2, :].rearrange("p a b -> p (a b)"), W("ident"))
                    mm.then_inc(s["qnT_ps"], 1)
                    pe.wait_ge(s["qnT"], m + 1)
                    pe.matmul(ahead_ps[:, 0:256], W("tq"), qnT[:, :], start=True, stop=True).then_inc(s["q_ps"], 1)

                def output(n):
                    pe.wait_ge(s["rp"], n + 1)
                    pe.wait_ge(s["agb"], n + 1)
                    for j in range(2):
                        mm = pe.matmul(misc[:, 128 * j:128 * j + 128], agb[:, 128 * j:128 * j + 128], W("tproj"), start=True, stop=True)
                    mm.then_inc(s["o_ps"], 1)

                def prologue():
                    stats(0, 0)
                    stats_back(0)
                    patches(0)
                    queries(0)

                def body(n, k, i, first, last):
                    xt = xb[k]
                    for c in range(CH + 1):
                        if c < CH:
                            pe.wait_ge(s["vs" if c < 2 else "tb"], CH * n + c + 1)
                            pe.matmul(kv_ps[c % 2][:, :], wk[:, :], xt[:, 512 * c:512 * c + 512], start=True, stop=True).then_inc(s["k_ps"], 1)
                        if c > 0:
                            pe.wait_ge(s["tb"], CH * n + c + 2)
                            if c == 1:
                                pe.wait_ge(s["s1"], n + 1)
                            pe.matmul(sps[:, :], W("sel", 128 * (c - 1), 128), tb[(c - 1) % 2][:, :],
                                      start=(c == 1), stop=(c == CH)).then_inc(s["s_ps"], 1)
                        if c == 1 and not first:
                            output(n - 1)
                        if c == 4:
                            pe.wait_ge(s["po"], n + 1)
                            pe.wait_ge(s["t0"], n + 1)
                            for a in range(CH):
                                mm = pe.matmul(misc[:, 0:32], W("sel", 128 * a, 128), t0[:, 32 * a:32 * a + 32],
                                               start=(a == 0), stop=(a == CH - 1))
                            mm.then_inc(s["c0_ps"], 1)
                        if c == 6:
                            pe.wait_ge(s["c0"], n + 1)
                            pe.wait_ge(s["rrep"], n + 1)
                            for j in range(4):
                                mm = pe.transpose(misc[:, 128 * j:128 * j + 128], rrep[:, j].rearrange("p a b c -> p (a b c)"), W("ident"))
                            mm.then_inc(s["rr_ps"], 1)
                    if not last:
                        stats(n + 1, 1 - k)
                    for c in range(CH):
                        pe.wait_ge(s["tb" if c < 2 else "vs"], CH * n + c + (9 if c < 2 else 1))
                        pe.matmul(kv_ps[c % 2][:, :], wv[:, :], xt[:, 512 * c:512 * c + 512], start=True, stop=True).then_inc(s["v_ps"], 1)
                        if c == 0:
                            if not last:
                                stats_back(n + 1)
                            pe.wait_ge(s["p2"], n + 1)
                        pe.wait_ge(s["b_used"], CH * n + c + 1)
                        pe.matmul(bps[c % 2][:, :], W("selT", 128 * c, 128), p2[:, :], start=True, stop=True).then_inc(s["b_ps"], 1)
                        if c == 1 and not last:
                            patches(n + 1)
                    if not last:
                        queries(n + 1)

                bodies(pe, prologue, body, lambda: output(PAIRS - 1))

            @block.scalar
            def _(act):
                act.sem_inc(s["vs"], 2)
                act.sem_inc(s["stT"], 1)
                act.sem_inc(s["qx"], 1)

                def squares(m, k, i):
                    act.wait_ge(s[f"x_in{k}"], 16 * i + 16)
                    act.wait_ge(s["stat_mm"], m + 1)
                    for q in range(4):
                        act.activation(sq[:, 1024 * q:1024 * q + 1024], xb[k][:, 1024 * q:1024 * q + 1024], ACT.Square).then_inc(s["sq"], 1)

                def means(m):
                    act.wait_ge(s["stat_mm"], m + 2)
                    act.copy(stT[:, :], stats_ps[:, :]).then_inc(s["stT"], 1)

                def patches(m, k):
                    act.wait_ge(s["rfT"], m + 1)
                    act.mul(rt[k][:, :, :].rearrange("p a b -> p (a b)"), ahead_ps[:, 0:256], 1 / 16).then_inc(s["rt"], 1)

                def queries(m):
                    act.wait_ge(s["qnT_ps"], m + 1)
                    act.copy(qnT[:, :], ahead_ps[:, 0:256]).then_inc(s["qnT"], 1)
                    act.wait_ge(s["q_ps"], m + 1)
                    act.mul(qx[:, :, :], each(ahead_ps[:, 0:256], 256, 4), 1 / 8).then_inc(s["qx"], 1)

                def prologue():
                    squares(0, 0, 0)
                    means(0)
                    patches(0, 0)
                    queries(0)

                def body(n, k, i, first, last):
                    act.wait_ge(s["rr"], n + 1)
                    for j in range(4):
                        cp = act.copy(rrep[:, j].rearrange("p a b c -> p (a b) c"),
                                      rr[:, j].rearrange("p a b -> p (a b)").unsqueeze(2).broadcast_to([128, 2 * CH, 8]))
                    cp.then_inc(s["rrep"], 1)
                    act.wait_ge(s["c0_ps"], n + 1)
                    act.copy(c0[:, :, :], each(misc[:, 0:32], 32, 4)).then_inc(s["c0"], 1)
                    act.wait_ge(s["rr_ps"], n + 1)
                    act.copy(rp[:, :], misc[:, :]).then_inc(s["rp"], 1)
                    if not last:
                        squares(n + 1, 1 - k, i + k)
                    act.wait_ge(s["s3"], n + 1)
                    act.activation(ex[:, :], s3[:, :], ACT.Exp).then_inc(s["ex"], 1)
                    if not last:
                        means(n + 1)
                    for c in range(CH):
                        act.wait_ge(s["v_ps"], CH * n + c + 1)
                        act.wait_ge(s["b_used"], CH * n + c + 1)
                        act.copy(vs[c % 2][:, :], kv_ps[c % 2][:, :]).then_inc(s["vs"], 1)
                        if c == 1 and not last:
                            patches(n + 1, 1 - k)
                    if not last:
                        queries(n + 1)
                bodies(act, prologue, body, lambda: None)

            @block.vector
            def _(v):
                v.sem_inc(s["tb"], 2)
                v.sem_inc(s["s1"], 1)
                v.sem_inc(s["b_used"], 2)
                v.sem_inc(s["agg"], 2)
                v.sem_inc(s["po"], 1)
                v.tensor_scalar(wk0[:, :], W("tk"), W("kvw"), None, ALU.mult).then_inc(s["wfold"], 1)
                v.tensor_scalar(wv0[:, :], W("tv"), W("kvw"), None, ALU.mult).then_inc(s["wfold"], 1)
                v.wait_ge(s["wcent"], 1)
                v.tensor_copy(wk[:, :], misc[:, 0:128])
                v.tensor_copy(wv[:, :], misc[:, 128:256])
                v.tensor_copy(kb[:, :], misc[:, 256:257])
                v.tensor_copy(vb[:, :], misc[:, 257:258]).then_inc(s["wready"], 1)
                v.wait_ge(s["wready"], 1)

                def ahead(m, k, step):
                    if step == 0:
                        v.wait_ge(s["stat_ps"], m + 1)
                        v.tensor_copy(st[:, :, :, :], ahead_ps[:, :].rearrange("p (j g r) -> p j g r", g=4, r=32)[:, :, :, 0:8]).then_inc(s["st"], 1)
                        v.wait_ge(s["st"], m + 1)
                        v.tensor_tensor(m2[:, :, :, :], st[:, :, 0:2], st[:, :, 0:2], ALU.mult).then_inc(s["m2"], 1)
                    if step == 1:
                        v.wait_ge(s["m2"], m + 1)
                        v.tensor_tensor(m2[:, :, :, :], st[:, :, 2:4], m2[:, :, :, :], ALU.subtract).then_inc(s["va"], 1)
                        v.wait_ge(s["va"], m + 1)
                        v.tensor_scalar(va[:, :, :, :], m2[:, :, :, :], 0.0, EPS, ALU.max, ALU.add).then_inc(s["vae"], 1)
                    if step == 2:
                        v.wait_ge(s["rt"], m + 1)
                        v.tensor_reduce(sm[:, :], rt[k][:, :, :], AX_X, ALU.add).then_inc(s["sm"], 1)
                        v.wait_ge(s["sm"], m + 1)
                        v.tensor_scalar(nm[:, :], sm[:, :], -1 / C, None, ALU.mult).then_inc(s["nm"], 1)
                    if step == 3:
                        v.wait_ge(s["nm"], m + 1)
                        v.tensor_tensor(hc[:, :, :], rt[k][:, :, :], each(nm[:, :], 4, 64), ALU.add).then_inc(s["hc"], 1)
                        v.wait_ge(s["hc"], m + 1)
                        v.tensor_tensor(hs[:, :, :], hc[:, :, :], hc[:, :, :], ALU.mult).then_inc(s["hs"], 1)
                    if step == 4:
                        v.wait_ge(s["hs"], m + 1)
                        v.tensor_reduce(sm[:, :], hs[:, :, :], AX_X, ALU.add).then_inc(s["ssq"], 1)
                        v.wait_ge(s["ssq"], m + 1)
                        v.tensor_scalar(ve[:, :], sm[:, :], 1 / C, EPS, ALU.mult, ALU.add).then_inc(s["ve"], 1)
                    if step == 5:
                        v.wait_ge(s["rs"], m + 1)
                        v.tensor_tensor(hs[:, :, :], hc[:, :, :], each(rs[:, :], 4, 64), ALU.mult).then_inc(s["hn"], 1)
                    if step == 6:
                        v.wait_ge(s["hn"], m + 1)
                        lnqw, lnqb = (W(m_).unsqueeze(1).broadcast_to([128, 4, 64]) for m_ in ("lnqw", "lnqb"))
                        v.tensor_tensor(hc[:, :, :], hs[:, :, :], lnqw, ALU.mult).then_inc(s["hnw"], 1)
                        v.wait_ge(s["hnw"], m + 1)
                        v.tensor_tensor(qn[:, :, :], hc[:, :, :], lnqb, ALU.add).then_inc(s["qn"], 1)

                def output(n, k):
                    v.wait_ge(s["o_ps"], n + 1)
                    v.tensor_tensor(po[:, :, :], misc[:, 0:256].rearrange("p (a b) -> p a b", b=64), rt[k][:, :, :], ALU.add).then_inc(s["po"], 1)
                    v.wait_ge(s["po"], n + 2)
                    v.tensor_tensor(h_all[:, bass.ds(6 * n, 6), :].rearrange("p (g j) c -> p j g c", g=2)[:, 0:2],
                                    po[:, :, :].rearrange("p (j g) c -> p j g c", j=2),
                                    W("projb").unsqueeze(1).unsqueeze(1).broadcast_to([128, 2, 2, 64]), ALU.add).then_inc(s["o_done"], 1)

                def prologue():
                    for step in range(7):
                        ahead(0, 0, step)

                def body(n, k, i, first, last):
                    v.wait_ge(s["qx"], n + 2)
                    v.tensor_scalar(t0[:, :], qx[:, :, 0:1].rearrange("p a b -> p (a b)"), kb[:, :], None, ALU.mult).then_inc(s["t0"], 1)
                    for c in range(CH):
                        v.wait_ge(s["k_ps"], CH * n + c + 1)
                        v.wait_ge(s["s_ps"], CH * n + c + 1)
                        v.tensor_tensor(strips(tb[c % 2][:, :]), strips(kv_ps[c % 2][:, :]), over_rows(qx[:, 32 * c:32 * c + 32, :], 2),
                                        ALU.mult).then_inc(s["tb"], 1)
                        if c == 2 and not first:
                            output(n - 1, 1 - k)
                    v.wait_ge(s["s_ps"], CH * n + CH + 2)
                    v.wait_ge(s["rp"], n + 1)
                    v.tensor_tensor(s1[:, :], sps[:, :], rp[:, :], ALU.mult).then_inc(s["s1"], 1)
                    v.wait_ge(s["s1"], n + 2)
                    v.wait_ge(s["c0"], n + 1)
                    v.tensor_tensor(strips(s2[:, :]), strips(s1[:, :]), over_rows(c0[:, :, :], 2), ALU.add).then_inc(s["s2"], 1)
                    v.wait_ge(s["s2"], n + 1)
                    v.tensor_reduce(mx[:, :].rearrange("p (a w) -> p a w", w=16), grid(s2[:, :]), AX_XY, ALU.max).then_inc(s["mx"], 1)
                    v.wait_ge(s["mx"], n + 1)
                    v.tensor_copy(mxx[:, :, :], each(mx[:, :], 32, 4)).then_inc(s["mxx"], 1)
                    v.wait_ge(s["mxx"], n + 1)
                    v.tensor_tensor(strips(s3[:, :]), strips(s2[:, :]), over_rows(mxx[:, :, :], 2), ALU.subtract).then_inc(s["s3"], 1)
                    v.wait_ge(s["ex"], n + 1)
                    v.tensor_reduce(z[:, :].rearrange("p (a w) -> p a w", w=16), grid(ex[:, :]), AX_XY, ALU.add).then_inc(s["z"], 1)
                    v.wait_ge(s["z"], n + 1)
                    v.reciprocal(rz[:, :], z[:, :]).then_inc(s["rz"], 1)
                    v.wait_ge(s["rz"], n + 1)
                    v.tensor_copy(rzx[:, :, :], each(rz[:, :], 32, 4)).then_inc(s["rzx"], 1)
                    v.wait_ge(s["rzx"], n + 1)
                    v.tensor_tensor(strips(p1[:, :]), strips(ex[:, :]), over_rows(rzx[:, :, :], 2), ALU.mult).then_inc(s["p1"], 1)
                    v.wait_ge(s["p1"], n + 1)
                    v.tensor_tensor(p2[:, :], p1[:, :], rp[:, :], ALU.mult).then_inc(s["p2"], 1)
                    for c in range(CH):
                        v.wait_ge(s["b_ps"], CH * n + c + 1)
                        v.wait_ge(s["vs"], CH * n + c + 3)
                        v.wait_ge(s["agg"], CH * n + c + 1)
                        v.tensor_tensor(pv[c % 2][:, :], bps[c % 2][:, :], vs[c % 2][:, :], ALU.mult).then_inc(s["b_used"], 1)
                        v.wait_ge(s["b_used"], CH * n + c + 3)
                        v.tensor_reduce(agg[:, 32 * c:32 * c + 32].rearrange("p (a w) -> p a w", w=16), grid(pv[c % 2][:, :]), AX_XY, ALU.add).then_inc(s["agg"], 1)
                        if c < 7 and not last:
                            ahead(n + 1, 1 - k, c)
                    v.wait_ge(s["agg"], CH * n + CH + 2)
                    v.tensor_scalar(agb[:, :], agg[:, :], vb[:, :], None, ALU.add).then_inc(s["agb"], 1)

                bodies(v, prologue, body, lambda: output(PAIRS - 1, 1))


def attention_stage(nc, mem):
    h_all, W = mem["h"], mem["W"]
    Q_PARTS, K_PARTS = (0, 0, 0, 1, 1, 2), (0, 1, 2, 0, 1, 0)
    U = NT * HEADS
    G = U // 4
    with ExitStack() as ctx:
        sb = lambda n, s, d=F32: ctx.enter_context(nc.sbuf_tensor("a_" + n, s, d))
        ps = lambda n, s, d=F32: ctx.enter_context(nc.psum_tensor("a_" + n, s, d))
        half = sb("half", [128, 24])
        lp, ls, le = sb("lp", [128, 2, 16]), sb("ls", [128, 2]), sb("le", [128, 2])
        ld, lamv = sb("ld", [128, 1]), sb("lamv", [128, 2])
        gam, bet = sb("gam", [128, 32]), sb("bet", [128, 32])
        sm, nm, ve, rs = (sb(n, [128, NT]) for n in ("sm", "nm", "ve", "rs"))
        hc, hs = (sb(n, [128, NT, C]) for n in ("hc", "hs"))
        hn = sb("hn", [128, NT + 1, C])
        zero, one = sb("zero", [128, 1]), sb("one", [128, 24])
        hT = sb("hT", [128, L])
        parts = sb("parts", [128, 4, 3, L], BF16)
        rest = [sb(f"rest{k}", [128, L]) for k in range(2)]
        qe = [sb(f"qe{k}", [96, 16, L], BF16) for k in range(2)]
        ke = [sb(f"ke{k}", [96, 16, L], BF16) for k in range(2)]
        val = [sb(f"val{k}", [128, NT, INNER]) for k in range(2)]
        th = [sb(f"th{k}", [128, NT, INNER]) for k in range(2)]
        nmx = sb("nmx", [128, 4, 2])
        E = [sb(f"e{k}", [128, 2, L]) for k in range(3)]
        Z = [sb(f"z{k}", [128, U, 2]) for k in range(2)]
        rz, rzl = sb("rz", [128, 4, 2]), sb("rzl", [128, 4, 2])
        DT = [sb(f"dt{k}", [128, 2, 4, NT, 128]) for k in range(2)]
        oT = [sb(f"oT{k}", [128, 256]) for k in range(2)]
        mixed = sb("mixed", [128, 2, 4, DV])
        O = [sb(f"o{k}", [128, NT, HEADS, DV]) for k in range(2)]
        so, no, vo, ro = (sb(n, [128, 24]) for n in ("so", "no", "vo", "ro"))
        oc, o2, sg, of = (sb(n, [128, 24, DV]) for n in ("oc", "o2", "sg", "of"))
        oF = sb("oF", [128, 2, L])
        hp = sb("hp", [128, NT, C])
        s_ps = [ps(f"s{k}", [128, 2, 512]) for k in range(2)]
        t_ps = [ps(f"t{k}", [128, 512]) for k in range(2)]
        av_ps = ps("av", [128, 512])
        misc = ps("misc", [128, 512])
        scratch = nc.dram_tensor("a_scratch", (3, 2, 16, 16, L), BF16, kind="Internal").ap()
        s = signals(nc, ctx, "a_", """half lp ls le ld neglam gb ones
            sm nm hc hs ssq ve rs hn ht_ps ht qk_ps hi rest mid lo scr qe vg_ps val
            s_ps mx ex t0_ps t1_ps dt0 dt1 av_ps av ot_ps rz rzl otm ot
            so no oc o2 sso vo ro on og ob sg of ft_ps ft op_ps hp h""")
        each = lambda ap, n, k: ap.unsqueeze(2).broadcast_to([128, n, k])
        per_group = lambda ap: ap.unsqueeze(1).broadcast_to([128, 24, DV])
        flat = lambda ap: ap.rearrange("p a b -> p (a b)")
        tiles = lambda n: h_all[:, bass.ds(NT * n, NT), :]

        MISC = {1: ("ot", 4), 2: ("ht", 0), 3: ("qk", 0), 4: ("qk", 1), 5: ("ot", 5), 7: ("qk", 2), 8: ("qk", 3), 9: ("ot", 0),
                11: ("vg", 0), 12: ("vg", 1), 13: ("ot", 1), 15: ("vg", 2), 17: ("ot", 2), 19: ("ft", 0), 20: ("ft", 1),
                21: ("ot", 3), 22: ("op", 0)}

        def bodies(eng, body, prologue, epilogue):
            prologue()
            body(0, 0, True, False)
            with eng.Fori(0, (B - 2) // 2) as i:
                body(2 * i + 1, 1, False, False)
                body(2 * i + 2, 0, False, False)
            body(B - 1, 1, False, True)
            epilogue()

        def tasks(u, first, last):
            if u not in MISC:
                return None
            name, c = MISC[u]
            ahead = 1 if name in ("ht", "qk", "vg") else -1 if name in ("ft", "op") or (name == "ot" and c >= 4) else 0
            if (ahead == 1 and last) or (ahead == -1 and first):
                return None
            return name, c, ahead

        def unit(n, k, u):
            return (n - 1, 1 - k, u + U) if u < 0 else (n, k, u) if u < U else (n + 1, 1 - k, u - U)

        def there(u, first, last):
            return not (u < 0 and first) and not (u >= U and last)

        with nc.Block() as block:
            @block.sync
            def _(sp):
                def spread(n, k):
                    sp.wait_ge(s["lo"], 4 * n + 6)
                    for t in range(4):
                        sp.dma_start(scratch[:, t // 2, 8 * (t % 2):8 * (t % 2) + 8].rearrange("q m d n -> (m d) q n"),
                                     parts[:, t]).then_inc(s["scr"], 16)
                    sp.wait_ge(s["scr"], 64 * n + 64)
                    for g in range(6):
                        sp.dma_start(qe[k][16 * g:16 * g + 16, :, :],
                                     scratch[Q_PARTS[g], 0].rearrange("m d n -> d m n")).then_inc(s["qe"], 16)
                        sp.dma_start(ke[k][16 * g:16 * g + 16, :, :],
                                     scratch[K_PARTS[g], 1].rearrange("m d n -> d m n")).then_inc(s["qe"], 16)

                spread(0, 0)
                spread(1, 1)
                with sp.Fori(0, (B - 2) // 2) as i:
                    for k in range(2):
                        spread(2 * i + 2 + k, k)

            @block.gpsimd
            def _(pl):
                def deviation(m):
                    pl.wait_ge(s["ve"], m + 1)
                    pl.tensor_tensor(rs[:, :], ve[:, :], half[:, 0:NT], ALU.pow).then_inc(s["rs"], 1)

                def split(m, c):
                    pl.wait_ge(s["rest"], 4 * m + c + 1)
                    pl.tensor_tensor(parts[:, c, 1, :], rest[c % 2][:, :], zero[:, :].broadcast_to([128, L]), ALU.add).then_inc(s["mid"], 1)
                    pl.wait_ge(s["mid"], 4 * m + c + 1)
                    pl.tensor_tensor(parts[:, c, 2, :], rest[c % 2][:, :], parts[:, c, 1, :], ALU.subtract).then_inc(s["lo"], 1)

                def gate_plus_one(m, k):
                    pl.wait_ge(s["of"], m + 1)
                    pl.wait_ge(s["val"], NT * m + NT)
                    pl.tensor_tensor(sg[:, :, :], th[k][:, :, :].rearrange("p a (b c) -> p (a b) c", c=DV),
                                     one[:, :].unsqueeze(2).broadcast_to([128, 24, DV]), ALU.add).then_inc(s["sg"], 1)

                def centre(m, k):
                    pl.wait_ge(s["no"], m + 1)
                    pl.tensor_tensor(oc[:, :, :], O[k][:, :, :, :].rearrange("p a b c -> p (a b) c"), each(no[:, :], 24, DV), ALU.add)\
                        .then_inc(s["oc"], 1)
                    pl.wait_ge(s["oc"], m + 1)
                    pl.tensor_tensor(o2[:, :, :], oc[:, :, :], oc[:, :, :], ALU.mult).then_inc(s["o2"], 1)

                def normed(m):
                    pl.wait_ge(s["vo"], m + 1)
                    pl.tensor_tensor(ro[:, :], vo[:, :], half[:, :], ALU.pow).then_inc(s["ro"], 1)
                    pl.wait_ge(s["ro"], m + 1)
                    pl.tensor_tensor(o2[:, :, :], oc[:, :, :], each(ro[:, :], 24, DV), ALU.mult).then_inc(s["on"], 1)

                def gated(m):
                    pl.wait_ge(s["on"], m + 1)
                    pl.tensor_tensor(oc[:, :, :], o2[:, :, :], per_group(gam[:, :]), ALU.mult).then_inc(s["og"], 1)
                    pl.wait_ge(s["og"], m + 1)
                    pl.tensor_tensor(o2[:, :, :], oc[:, :, :], per_group(bet[:, :]), ALU.add).then_inc(s["ob"], 1)
                    pl.wait_ge(s["ob"], m + 1)
                    pl.wait_ge(s["sg"], m + 1)
                    pl.tensor_tensor(of[:, :, :], o2[:, :, :], sg[:, :, :], ALU.mult).then_inc(s["of"], 1)

                def prologue():
                    pl.sem_inc(s["lo"], 2)
                    pl.sem_inc(s["of"], 1)
                    pl.memset(zero[:, :], 0.0)
                    pl.memset(one[:, :], 1.0)
                    pl.memset(half[:, :], -0.5).then_inc(s["half"], 1)
                    pl.wait_ge(s["half"], 1)
                    pl.wait_ge(s["gb"], 1)
                    deviation(0)
                    for c in range(4):
                        split(0, c)

                def body(n, k, first, last):
                    if not last:
                        deviation(n + 1)
                    if not first:
                        gate_plus_one(n - 1, 1 - k)
                    if not last:
                        for c in range(4):
                            split(n + 1, c)
                    if not first:
                        centre(n - 1, 1 - k)
                        normed(n - 1)
                        gated(n - 1)

                def epilogue():
                    gate_plus_one(B - 1, 1)
                    centre(B - 1, 1)
                    normed(B - 1)
                    gated(B - 1)

                bodies(pl, body, prologue, epilogue)

            @block.tensor
            def _(pe):
                def scores(n, k, u):
                    ic, hd = u // HEADS, u % HEADS
                    pe.wait_ge(s["ex"], U * n + u + 1)
                    for m in range(2):
                        mm = pe.matmul(s_ps[u % 2][:, m, 0:L], qe[k][:, 2 * hd + m, 128 * ic:128 * ic + 128], ke[k][:, 2 * hd + m, :],
                                       start=True, stop=True)
                    mm.then_inc(s["s_ps"], 1)

                def transposes(n, k, u):
                    for m in range(2):
                        if m == 0:
                            pe.wait_ge(s["ex"], U * n + u + 3)
                        pe.wait_ge(s[f"dt{m}"], U * n + u + 1)
                        for j in range(NT):
                            mm = pe.transpose(t_ps[m][:, 128 * j:128 * j + 128], E[u % 3][:, m, 128 * j:128 * j + 128], W("ident"))
                        mm.then_inc(s[f"t{m}_ps"], 1)

                def outputs(n, k, g, m):
                    pe.wait_ge(s[f"dt{m}"], U * n + 4 * g + 5)
                    if m == 0:
                        pe.wait_ge(s["av"], G * n + g + 1)
                    for j in range(NT):
                        for q in range(4):
                            mm = pe.matmul(av_ps[32 * q:32 * q + 32, 128 * m:128 * m + 128], val[k][:, j, DV * (4 * (g % 2) + q):DV * (4 * (g % 2) + q + 1)],
                                           DT[g % 2][:, m, q, j, :], start=(j == 0), stop=(j == NT - 1))
                    mm.then_inc(s["av_ps"], 1)

                def free_misc(name, c, m):
                    total = {"ot": G, "ht": 1, "qk": 4, "vg": NT, "ft": 2, "op": 1}[name]
                    sem = {"ot": "otm", "ht": "ht", "qk": "rest", "vg": "val", "ft": "ft", "op": "hp"}[name]
                    pe.wait_ge(s[sem], total * m + c + (2 if name == "op" else 1))

                def task(name, c, m, k):
                    if name == "ht":
                        pe.wait_ge(s["hn"], m + 1)
                        for j in range(NT):
                            mm = pe.transpose(misc[:, 128 * j:128 * j + 128], hn[:, j:j + 2, :].rearrange("p a b -> p (a b)"), W("ident"))
                        mm.then_inc(s["ht_ps"], 1)
                    if name == "qk":
                        if c == 0:
                            pe.wait_ge(s["ht"], m + 1)
                        pe.matmul(misc[:, 0:L], W("aqk", 128 * c, 128), hT[:, :], start=True, stop=True).then_inc(s["qk_ps"], 1)
                    if name == "vg":
                        pe.matmul(misc[:, :], hT[:, 128 * c:128 * c + 128], W("avg"), start=True, stop=True).then_inc(s["vg_ps"], 1)
                    if name == "ot":
                        pe.wait_ge(s["av"], G * m + c + 2)
                        for a in range(2):
                            mm = pe.transpose(misc[:, 128 * a:128 * a + 128], oT[c % 2][:, 128 * a:128 * a + 128], W("ident"))
                        mm.then_inc(s["ot_ps"], 1)
                    if name == "ft":
                        pe.wait_ge(s["of"], m + 2)
                        for j in range(NT):
                            mm = pe.transpose(misc[:, 128 * j:128 * j + 128],
                                              of[:, 8 * j + 4 * c:8 * j + 4 * c + 4, :].rearrange("p a b -> p (a b)"), W("ident"))
                        mm.then_inc(s["ft_ps"], 1)
                    if name == "op":
                        pe.wait_ge(s["ft"], 2 * m + 2)
                        for j in range(NT):
                            for c in range(2):
                                mm = pe.matmul(misc[:, 64 * j:64 * j + 64], oF[:, c, 128 * j:128 * j + 128], W("aout", 64 * c, 64),
                                               start=(c == 0), stop=(c == 1))
                        mm.then_inc(s["op_ps"], 1)

                def prologue():
                    chain = [("ht", 0)] + [("qk", c) for c in range(4)] + [("vg", c) for c in range(NT)]
                    pe.sem_inc(s["t1_ps"], 3)
                    pe.sem_inc(s["av_ps"], 4)
                    pe.sem_inc(s["ot_ps"], 2)
                    pe.wait_ge(s["ones"], 2)
                    for j, (name, c) in enumerate(chain):
                        if j:
                            free_misc(*chain[j - 1], 0)
                        task(name, c, 0, 0)
                    free_misc("vg", NT - 1, 0)
                    pe.wait_ge(s["qe"], 192)
                    scores(0, 0, 0)
                    scores(0, 0, 1)

                def body(n, k, first, last):
                    before = [("vg", NT - 1, 0)] if first else [("ot", 3, -1), ("op", 0, -2)]
                    for u in range(U):
                        if there(u + 2, first, last):
                            if u + 2 == U:
                                pe.wait_ge(s["qe"], 192 * n + 384)
                            scores(*unit(n, k, u + 2))
                        if there(u - 1, first, last):
                            transposes(*unit(n, k, u - 1))
                        if u % 4 in (1, 2) and there(u - 5, first, last):
                            b, kb, v = unit(n, k, u - 4 - u % 4)
                            outputs(b, kb, v // 4, u % 4 - 1)
                        t = tasks(u, first, last)
                        if t:
                            name, c, ahead = t
                            for b in before:
                                free_misc(b[0], b[1], n + b[2])
                            task(name, c, n + ahead, k)
                            before = [(name, c, ahead)]

                def epilogue():
                    n = B - 1
                    transposes(n, 1, U - 1)
                    free_misc("op", 0, n - 1)
                    task("ot", 4, n, 1)
                    outputs(n, 1, 5, 0)
                    outputs(n, 1, 5, 1)
                    chain = [("ot", 4), ("ot", 5), ("ft", 0), ("ft", 1), ("op", 0)]
                    for old, new in zip(chain, chain[1:]):
                        free_misc(*old, n)
                        task(*new, n, 1)

                bodies(pe, body, prologue, epilogue)

            @block.scalar
            def _(act):
                def exps(n, k, u):
                    act.wait_ge(s["mx"], U * n + u + 1)
                    act.wait_ge(s["t1_ps"], U * n + u + 1)
                    for m in range(2):
                        a = act.activation(E[u % 3][:, m, :], s_ps[u % 2][:, m, 0:L], ACT.Exp, bias=nmx[:, u % 4, m:m + 1],
                                           accum_out=Z[k][:, u, m:m + 1])
                    a.then_inc(s["ex"], 1)

                def first_map(n, u):
                    act.wait_ge(s["t0_ps"], U * n + u + 1)
                    if u % 4 == 0:
                        act.wait_ge(s["av_ps"], 2 * (G * n + u // 4) + 1)
                    act.copy(DT[(u // 4) % 2][:, 0, u % 4], t_ps[0][:, 0:L].rearrange("p (a b) -> p a b", b=128)).then_inc(s["dt0"], 1)

                def output(n, g):
                    act.wait_ge(s["av_ps"], 2 * (G * n + g) + 6)
                    act.wait_ge(s["ot_ps"], G * n + g + 1)
                    act.copy(oT[g % 2][:, :], av_ps[:, 0:256]).then_inc(s["av"], 1)

                def evac(name, c, m, k, ahead=True, guard=False):
                    if name == "ht":
                        act.wait_ge(s["ht_ps"], m + 1)
                        act.copy(hT[0:64, :], misc[0:64, 0:L]).then_inc(s["ht"], 1)
                    if name == "qk":
                        act.wait_ge(s["qk_ps"], 4 * m + c + 1)
                        if c == 0 and ahead:
                            act.wait_ge(s["scr"], 64 * m)
                        act.mul(parts[:, c, 0, :], misc[:, 0:L], DH ** -0.5 if c < 2 else 1.0).then_inc(s["hi"], 1)
                    if name == "vg":
                        act.wait_ge(s["vg_ps"], NT * m + c + 1)
                        if c == 0 and guard:
                            act.wait_ge(s["sg"], m - 1)
                        act.copy(val[k][:, c, :], misc[:, 0:INNER])
                        act.activation(th[k][:, c, :], misc[:, INNER:2 * INNER], ACT.Tanh, scale=0.5).then_inc(s["val"], 1)
                    if name == "ft":
                        act.wait_ge(s["ft_ps"], 2 * m + c + 1)
                        act.copy(oF[:, c, :], misc[:, 0:L]).then_inc(s["ft"], 1)

                def prologue():
                    act.sem_inc(s["ex"], 2)
                    act.sem_inc(s["dt0"], 1)
                    act.sem_inc(s["av"], 1)
                    act.wait_ge(s["ls"], 1)
                    act.activation(le[:, :], ls[:, :], ACT.Exp).then_inc(s["le"], 1)
                    for name, c in [("ht", 0)] + [("qk", c) for c in range(4)] + [("vg", c) for c in range(NT)]:
                        evac(name, c, 0, 0, False)
                    exps(0, 0, 0)

                def body(n, k, first, last):
                    for u in range(U):
                        if there(u + 1, first, last):
                            exps(*unit(n, k, u + 1))
                        if u % 4 == 3 and there(u - 7, first, last):
                            b, _, v = unit(n, k, u - 7)
                            output(b, v // 4)
                        if there(u - 1, first, last):
                            b, _, v = unit(n, k, u - 1)
                            first_map(b, v)
                        t = tasks(u, first, last)
                        if t:
                            name, c, ahead = t
                            evac(name, c, n + ahead, (k + ahead) % 2, guard=not first)

                def epilogue():
                    first_map(B - 1, U - 1)
                    output(B - 1, 5)
                    evac("ft", 0, B - 1, 1)
                    evac("ft", 1, B - 1, 1)

                bodies(act, body, prologue, epilogue)

            @block.vector
            def _(v):
                def maxima(n, u):
                    v.wait_ge(s["s_ps"], U * n + u + 1)
                    v.tensor_reduce(nmx[:, u % 4, :], s_ps[u % 2][:, :, 0:L], AX_X, ALU.max, negate=True).then_inc(s["mx"], 1)

                def norm(m, part):
                    if part == 0:
                        v.tensor_reduce(sm[:, :], tiles(m), AX_X, ALU.add).then_inc(s["sm"], 1)
                    if part == 1:
                        v.wait_ge(s["sm"], m + 1)
                        v.tensor_scalar(nm[:, :], sm[:, :], -1 / C, None, ALU.mult).then_inc(s["nm"], 1)
                    if part == 2:
                        v.wait_ge(s["nm"], m + 1)
                        v.tensor_tensor(hc[:, :, :], tiles(m), each(nm[:, :], NT, C), ALU.add).then_inc(s["hc"], 1)
                    if part == 3:
                        v.wait_ge(s["hc"], m + 1)
                        v.tensor_tensor(hs[:, :, :], hc[:, :, :], hc[:, :, :], ALU.mult).then_inc(s["hs"], 1)
                    if part == 4:
                        v.wait_ge(s["hs"], m + 1)
                        v.tensor_reduce(sm[:, :], hs[:, :, :], AX_X, ALU.add).then_inc(s["ssq"], 1)
                    if part == 5:
                        v.wait_ge(s["ssq"], m + 1)
                        v.tensor_scalar(ve[:, :], sm[:, :], 1 / C, EPS, ALU.mult, ALU.add).then_inc(s["ve"], 1)
                    if part == 6:
                        v.wait_ge(s["rs"], m + 1)
                        v.tensor_tensor(hn[:, 0:NT, :], hc[:, :, :], each(rs[:, :], NT, C), ALU.mult).then_inc(s["hn"], 1)

                def second_map(n, u):
                    v.wait_ge(s["t1_ps"], U * n + u + 4)
                    if u % 4 == 0:
                        v.wait_ge(s["av_ps"], 2 * (G * n + u // 4) + 2)
                    v.tensor_copy(DT[(u // 4) % 2][:, 1, u % 4], t_ps[1][:, 0:L].rearrange("p (a b) -> p a b", b=128)).then_inc(s["dt1"], 1)

                def heads_a(m, k):
                    v.wait_ge(s["ot"], G * m + G + 1)
                    v.tensor_reduce(so[:, :], O[k][:, :, :, :].rearrange("p a b c -> p (a b) c"), AX_X, ALU.add).then_inc(s["so"], 1)
                    v.wait_ge(s["so"], m + 1)
                    v.tensor_scalar(no[:, :], so[:, :], -1 / DV, None, ALU.mult).then_inc(s["no"], 1)

                def heads_b(m):
                    v.wait_ge(s["o2"], m + 1)
                    v.tensor_reduce(so[:, :], o2[:, :, :], AX_X, ALU.add).then_inc(s["sso"], 1)
                    v.wait_ge(s["sso"], m + 1)
                    v.tensor_scalar(vo[:, :], so[:, :], 1 / DV, EPS, ALU.mult, ALU.add).then_inc(s["vo"], 1)

                def mix(m, k, c, part):
                    N = G * m + c
                    if part == 0:
                        v.wait_ge(s["ex"], U * m + 4 * c + 6)
                        v.reciprocal(rz[:, :, :], Z[k][:, 4 * c:4 * c + 4, :]).then_inc(s["rz"], 1)
                    if part == 1:
                        v.wait_ge(s["rz"], N + 1)
                        v.wait_ge(s["ot"], N + 1)
                        v.tensor_tensor(rzl[:, :, :], rz[:, :, :], lamv[:, :].unsqueeze(1).broadcast_to([128, 4, 2]), ALU.mult).then_inc(s["rzl"], 1)
                    if part == 2:
                        v.wait_ge(s["rzl"], N + 1)
                        v.wait_ge(s["ot_ps"], N + 3)
                        v.tensor_tensor(mixed[:, :, :, :], misc[:, 0:256].rearrange("p (m h c) -> p m h c", m=2, h=4),
                                        rzl[:, :, :].rearrange("p h m -> p m h").unsqueeze(3).broadcast_to([128, 2, 4, DV]), ALU.mult).then_inc(s["otm"], 1)
                    if part == 3:
                        v.wait_ge(s["otm"], N + 1)
                        v.tensor_tensor(O[k][:, c // 2, 4 * (c % 2):4 * (c % 2) + 4, :], mixed[:, 0], mixed[:, 1], ALU.add).then_inc(s["ot"], 1)

                def evac(name, c, m, k):
                    if name == "qk":
                        v.wait_ge(s["hi"], 4 * m + c + 1)
                        v.wait_ge(s["lo"], 4 * m + c + 1)
                        v.scalar_tensor_tensor(rest[c % 2][:, :], misc[:, 0:L], DH ** -0.5 if c < 2 else 1.0, parts[:, c, 0, :],
                                               ALU.mult, ALU.subtract).then_inc(s["rest"], 1)
                    if name == "op":
                        v.wait_ge(s["op_ps"], m + 1)
                        v.tensor_tensor(hp[:, :, :], misc[:, 0:NT * C].rearrange("p (a b) -> p a b", b=C), tiles(m), ALU.add).then_inc(s["hp"], 1)
                        v.wait_ge(s["hp"], m + 2)
                        v.tensor_tensor(tiles(m), hp[:, :, :], W("aoutb").unsqueeze(1).broadcast_to([128, NT, C]), ALU.add).then_inc(s["h"], 1)

                def prologue():
                    v.sem_inc(s["dt1"], 1)
                    v.sem_inc(s["ot"], 1)
                    v.sem_inc(s["hp"], 1)
                    v.memset(lamv[:, 0:1], 1.0)
                    v.memset(hn[:, NT, :], 0.0)
                    v.memset(hT[64:128, :], 0.0).then_inc(s["ones"], 1)
                    v.wait_ge(s["ones"], 1)
                    v.memset(hT[64:65, :], 1.0).then_inc(s["ones"], 1)
                    for j in range(2):
                        v.tensor_tensor(lp[:, j], W("lqk", 32 * j, 16), W("lqk", 32 * j + 16, 16), ALU.mult).then_inc(s["lp"], 1)
                    v.wait_ge(s["lp"], 2)
                    v.tensor_reduce(ls[:, :], lp[:, :, :], AX_X, ALU.add).then_inc(s["ls"], 1)
                    v.tensor_scalar(gam[:, :], W("gam"), 0.5 * (1.0 - LAMBDA_INIT), None, ALU.mult)
                    v.tensor_scalar(bet[:, :], W("bet"), 0.5 * (1.0 - LAMBDA_INIT), None, ALU.mult).then_inc(s["gb"], 1)
                    v.wait_ge(s["le"], 1)
                    v.tensor_tensor(ld[:, :], le[:, 1:2], le[:, 0:1], ALU.subtract).then_inc(s["ld"], 1)
                    v.wait_ge(s["ld"], 1)
                    v.tensor_scalar(lamv[:, 1:2], ld[:, :], -LAMBDA_INIT, None, ALU.add).then_inc(s["neglam"], 1)
                    v.wait_ge(s["neglam"], 1)
                    for part in range(7):
                        norm(0, part)
                    for c in range(4):
                        evac("qk", c, 0, 0)
                    maxima(0, 0)
                    maxima(0, 1)

                def body(n, k, first, last):
                    for u in range(U):
                        now, old = tasks(u, first, last), tasks(u - 1, first, last)
                        mixing = lambda t, part: t and t[0] == "ot" and mix(n + t[2], (k + t[2]) % 2, t[1], part)
                        mixing(old, 2)
                        if old and old[0] != "ot":
                            name, c, ahead = old
                            evac(name, c, n + ahead, (k + ahead) % 2)
                        if u < 3 and not last:
                            norm(n + 1, 3 * u)
                        if there(u + 2, first, last):
                            b, _, w = unit(n, k, u + 2)
                            maxima(b, w)
                        mixing(now, 0)
                        mixing(old, 3)
                        if u < 2 and not last:
                            norm(n + 1, 3 * u + 1)
                        if there(u - 1, first, last):
                            b, _, w = unit(n, k, u - 1)
                            second_map(b, w)
                        mixing(now, 1)
                        if u < 2 and not last:
                            norm(n + 1, 3 * u + 2)
                        if u == 7 and not first:
                            heads_a(n - 1, 1 - k)
                        if u == 12 and not first:
                            heads_b(n - 1)

                def epilogue():
                    second_map(B - 1, U - 1)
                    for c in (4, 5):
                        for part in range(4):
                            mix(B - 1, 1, c, part)
                    heads_a(B - 1, 1)
                    heads_b(B - 1)
                    evac("op", 0, B - 1, 1)

                bodies(v, body, prologue, epilogue)


GT, RT = 12, 16


def norm_names():
    return "sm nm hc hs ssq ve rs hn"


def layer_norm(v, s, m, h, t, bufs):
    sm, nm, ve, hc, hs = bufs
    each = lambda ap: ap.unsqueeze(2).broadcast_to([128, t, C])
    v.tensor_reduce(sm[:, :], h, AX_X, ALU.add).then_inc(s["sm"], 1)
    v.wait_ge(s["hn"], m + 1)
    v.wait_ge(s["sm"], m + 1)
    v.tensor_scalar(nm[:, :], sm[:, :], -1 / C, None, ALU.mult).then_inc(s["nm"], 1)
    v.wait_ge(s["nm"], m + 1)
    v.tensor_tensor(hc[:, :, :], h, each(nm[:, :]), ALU.add).then_inc(s["hc"], 1)
    v.wait_ge(s["hc"], m + 1)
    v.tensor_tensor(hs[:, :, :], hc[:, :, :], hc[:, :, :], ALU.mult).then_inc(s["hs"], 1)
    v.wait_ge(s["hs"], m + 1)
    v.tensor_reduce(sm[:, :], hs[:, :, :], AX_X, ALU.add).then_inc(s["ssq"], 1)
    v.wait_ge(s["ssq"], m + 1)
    v.tensor_scalar(ve[:, :], sm[:, :], 1 / C, EPS, ALU.mult, ALU.add).then_inc(s["ve"], 1)


def layer_norm_scale(v, s, m, rs, hc, hn, t):
    v.wait_ge(s["rs"], m + 1)
    v.tensor_tensor(hn, hc[:, :, :], rs[:, :].unsqueeze(2).broadcast_to([128, t, C]), ALU.mult).then_inc(s["hn"], 1)


def gate_buffers(sb, e):
    small = {n: sb("g" + n, [128, RT]) for n in ("m", "z", "rz", "gm", "zs", "rzs")}
    wide = {n: sb("g" + n, [128, RT, e]) for n in ("d", "e", "p", "rank", "sel", "dd", "ee", "es")}
    square = {n: sb("g" + n, [128, RT, e, e]) for n in ("gt", "eq", "el", "rk")}
    return {**small, **wide, **square}


GATE_NAMES = "gm gd ge gz grz gp ggt geq gel grk grank gsel ggm gdd gee ges gzs grzs gw"


def shifted(v, s, m, b, logits, e):
    v.tensor_reduce(b["m"][:, :], logits, AX_X, ALU.max).then_inc(s["gm"], 1)
    v.wait_ge(s["gm"], m + 1)
    v.tensor_tensor(b["d"][:, :, :], logits, b["m"][:, :].unsqueeze(2).broadcast_to([128, RT, e]), ALU.subtract).then_inc(s["gd"], 1)


def top_two(v, s, m, b, e, tie, w, again):
    each = lambda ap: ap.unsqueeze(2).broadcast_to([128, RT, e])
    v.wait_ge(s["ge"], m + 1)
    v.tensor_reduce(b["z"][:, :], b["e"][:, :, :], AX_X, ALU.add).then_inc(s["gz"], 1)
    v.wait_ge(s["gz"], m + 1)
    v.reciprocal(b["rz"][:, :], b["z"][:, :]).then_inc(s["grz"], 1)
    v.wait_ge(s["grz"], m + 1)
    p = b["p"]
    v.tensor_tensor(p[:, :, :], b["e"][:, :, :], each(b["rz"][:, :]), ALU.mult).then_inc(s["gp"], 1)
    v.wait_ge(s["gp"], m + 1)
    other = p[:, :, :].unsqueeze(2).broadcast_to([128, RT, e, e])
    own = p[:, :, :].unsqueeze(3).broadcast_to([128, RT, e, e])
    v.tensor_tensor(b["gt"][:, :, :, :], other, own, ALU.is_gt).then_inc(s["ggt"], 1)
    v.tensor_tensor(b["eq"][:, :, :, :], other, own, ALU.is_equal).then_inc(s["geq"], 1)
    v.wait_ge(s["geq"], m + 1)
    v.tensor_tensor(b["el"][:, :, :, :].rearrange("p a b c -> p a (b c)"), b["eq"][:, :, :, :].rearrange("p a b c -> p a (b c)"),
                    tie.unsqueeze(1).broadcast_to([128, RT, e * e]), ALU.mult).then_inc(s["gel"], 1)
    v.wait_ge(s["gel"], m + 1)
    v.tensor_tensor(b["rk"][:, :, :, :], b["el"][:, :, :, :], b["gt"][:, :, :, :], ALU.add).then_inc(s["grk"], 1)
    v.wait_ge(s["grk"], m + 1)
    v.tensor_reduce(b["rank"][:, :, :], b["rk"][:, :, :, :], AX_X, ALU.add).then_inc(s["grank"], 1)
    v.wait_ge(s["grank"], m + 1)
    v.tensor_scalar(b["sel"][:, :, :], b["rank"][:, :, :], 2.0, None, ALU.is_lt).then_inc(s["gsel"], 1)
    if again:
        v.tensor_reduce(b["gm"][:, :], p[:, :, :], AX_X, ALU.max).then_inc(s["ggm"], 1)
        v.wait_ge(s["ggm"], m + 1)
        v.tensor_tensor(b["dd"][:, :, :], p[:, :, :], each(b["gm"][:, :]), ALU.subtract).then_inc(s["gdd"], 1)
        v.wait_ge(s["gee"], m + 1)
        p = b["ee"]
    v.wait_ge(s["gsel"], m + 1)
    v.tensor_tensor(b["es"][:, :, :], p[:, :, :], b["sel"][:, :, :], ALU.mult).then_inc(s["ges"], 1)
    v.wait_ge(s["ges"], m + 1)
    v.tensor_reduce(b["zs"][:, :], b["es"][:, :, :], AX_X, ALU.add).then_inc(s["gzs"], 1)
    v.wait_ge(s["gzs"], m + 1)
    v.reciprocal(b["rzs"][:, :], b["zs"][:, :]).then_inc(s["grzs"], 1)
    v.wait_ge(s["grzs"], m + 1)
    v.tensor_tensor(w, b["es"][:, :, :], each(b["rzs"][:, :]), ALU.mult).then_inc(s["gw"], 1)


def groups(eng, n, prologue, body, epilogue):
    prologue()
    body(0, True, False)
    with eng.Fori(0, n - 2) as i:
        body(i + 1, False, False)
    body(n - 1, False, True)
    epilogue()


def norm_buffers(sb, t):
    b = {n: sb("n" + n, [128, t]) for n in ("sm", "nm", "ve", "rs")}
    b["hc"], b["hs"] = sb("nhc", [128, t, C]), sb("nhs", [128, t, C])
    b["hn"] = sb("nhn", [128, t + 1, C])
    b["half"] = sb("nhalf", [128, t])
    return b


def routing_stage(nc, mem, e, gate_w, tie, bias, again):
    h_all, W, hT_all, wT_all = mem["h"], mem["W"], mem["hT"], mem["wT"]
    with ExitStack() as ctx:
        pre = f"r{e}_"
        sb = lambda n, s, d=F32: ctx.enter_context(nc.sbuf_tensor(pre + n, s, d))
        ps = lambda n, s, d=F32: ctx.enter_context(nc.psum_tensor(pre + n, s, d))
        nb, gb = norm_buffers(sb, RT), gate_buffers(sb, e)
        hTg, wTg = sb("hTg", [128, RT * 128]), sb("wTg", [32, RT * 128])
        wg, rest = sb("wg", [128, RT, e]), sb("rest", [128, RT, e])
        pb = sb("pb", [128, RT, 2, e], BF16)
        wp = sb("wp", [128, RT, 32])
        t_ps, g_ps, b_ps = ps("t", [128, RT // 4, 512]), ps("g", [128, RT, e]), ps("b", [128, 2, 512])
        s = signals(nc, ctx, pre, "half ones ht_ps ht g_ps rows hi whi rest mid wp wt_ps wt b_ps biased " + norm_names() + " " + GATE_NAMES)
        bufs = [nb[n] for n in ("sm", "nm", "ve", "hc", "hs")]
        with nc.Block() as block:
            @block.gpsimd
            def _(pl):
                pl.memset(nb["half"][:, :], -0.5).then_inc(s["half"], 1)
                pl.wait_ge(s["half"], 1)

                def norm(g):
                    pl.wait_ge(s["ve"], g + 1)
                    pl.tensor_tensor(nb["rs"][:, :], nb["ve"][:, :], nb["half"][:, :], ALU.pow).then_inc(s["rs"], 1)
                groups(pl, TILES // RT, lambda: norm(0), lambda g, first, last: None if last else norm(g + 1), lambda: None)

            @block.tensor
            def _(pe):
                pe.wait_ge(s["ones"], 2)

                def logits(g):
                    pe.wait_ge(s["hn"], g + 2)
                    for j in range(RT):
                        mm = pe.transpose(t_ps[:, j // 4, 128 * (j % 4):128 * (j % 4) + 128],
                                          nb["hn"][:, j:j + 2, :].rearrange("p a b -> p (a b)"), W("ident"))
                        if j % 4 == 3:
                            mm.then_inc(s["ht_ps"], 1)
                    pe.wait_ge(s["ht"], (RT // 4) * (g + 1))
                    for j in range(RT):
                        mm = pe.matmul(g_ps[:, j, :], hTg[:, 128 * j:128 * j + 128], W(gate_w), start=True, stop=True)
                    mm.then_inc(s["g_ps"], 1)

                def body(g, first, last):
                    if not last:
                        logits(g + 1)
                    pe.wait_ge(s["wp"], g + 1)
                    for j in range(RT):
                        mm = pe.transpose(t_ps[0:32, j // 4, 128 * (j % 4):128 * (j % 4) + 128], wp[:, j, :], W("ident"))
                        if j % 4 == 3:
                            mm.then_inc(s["wt_ps"], 1)
                    pe.wait_ge(s["biased"], g + 1)
                    pe.wait_ge(s["wt"], (RT // 4) * (g + 1))
                    for j in range(RT):
                        mm = pe.matmul(b_ps[:, j // 8, 64 * (j % 8):64 * (j % 8) + 64], wTg[:, 128 * j:128 * j + 128], W(bias, rows=32),
                                       start=True, stop=True)
                    mm.then_inc(s["b_ps"], 1)
                groups(pe, TILES // RT, lambda: logits(0), body, lambda: None)

            @block.scalar
            def _(act):
                def transposed(g):
                    for q in range(RT // 4):
                        act.wait_ge(s["ht_ps"], (RT // 4) * g + q + 1)
                        act.copy(hTg[0:64, 512 * q:512 * q + 512], t_ps[0:64, q, :])
                        act.copy(hT_all[0:64, bass.ds(RT * 128 * g + 512 * q, 512)], t_ps[0:64, q, :]).then_inc(s["ht"], 1)

                def body(g, first, last):
                    act.wait_ge(s["gd"], g + 1)
                    act.activation(gb["e"][:, :, :], gb["d"][:, :, :], ACT.Exp).then_inc(s["ge"], 1)
                    if not last:
                        transposed(g + 1)
                    if again:
                        act.wait_ge(s["gdd"], g + 1)
                        act.activation(gb["ee"][:, :, :], gb["dd"][:, :, :], ACT.Exp).then_inc(s["gee"], 1)
                    for q in range(RT // 4):
                        act.wait_ge(s["wt_ps"], (RT // 4) * g + q + 1)
                        act.copy(wTg[:, 512 * q:512 * q + 512], t_ps[0:32, q, :])
                        act.copy(wT_all[:, bass.ds(RT * 128 * g + 512 * q, 512)], t_ps[0:32, q, :]).then_inc(s["wt"], 1)
                groups(act, TILES // RT, lambda: transposed(0), body, lambda: None)

            @block.vector
            def _(v):
                v.sem_inc(s["hn"], 1)
                v.sem_inc(s["biased"], 1)
                v.memset(nb["hn"][:, RT, :], 0.0)
                v.memset(hTg[64:128, :], 0.0)
                v.memset(wp[:, :, :], 0.0).then_inc(s["ones"], 1)
                v.wait_ge(s["ones"], 1)
                v.memset(wp[:, :, 24:25], 1.0)
                v.memset(hTg[64:65, :], 1.0).then_inc(s["ones"], 1)
                if bias == "bias0":
                    v.memset(hT_all[64:128, :], 0.0).then_inc(s["rows"], 1)
                    v.wait_ge(s["rows"], 1)
                    v.memset(hT_all[64:65, :], 1.0).then_inc(s["rows"], 1)
                v.wait_ge(s["ones"], 2)

                def tokens(g):
                    return h_all[:, bass.ds(RT * g, RT), :]

                def biased(g):
                    v.wait_ge(s["b_ps"], g + 1)
                    h = tokens(g).rearrange("p (a b) c -> p a (b c)", a=2)
                    v.tensor_tensor(h, h, b_ps[:, :, :], ALU.add).then_inc(s["biased"], 1)

                def scaled(g):
                    layer_norm_scale(v, s, g, nb["rs"], nb["hc"], nb["hn"][:, 0:RT, :], RT)

                def prologue():
                    layer_norm(v, s, 0, tokens(0), RT, bufs)
                    scaled(0)

                def body(g, first, last):
                    if not last:
                        layer_norm(v, s, g + 1, tokens(g + 1), RT, bufs)
                    v.wait_ge(s["g_ps"], g + 1)
                    shifted(v, s, g, gb, g_ps[:, :, :], e)
                    if not last:
                        scaled(g + 1)
                    top_two(v, s, g, gb, e, W(tie), wg[:, :, :], again)
                    v.wait_ge(s["gw"], g + 1)
                    v.tensor_copy(pb[:, :, 0], wg[:, :, :]).then_inc(s["hi"], 1)
                    v.wait_ge(s["hi"], g + 1)
                    v.tensor_copy(wp[:, :, 0:e], pb[:, :, 0]).then_inc(s["whi"], 1)
                    v.tensor_tensor(rest[:, :, :], wg[:, :, :], pb[:, :, 0], ALU.subtract).then_inc(s["rest"], 1)
                    v.wait_ge(s["rest"], g + 1)
                    v.tensor_copy(pb[:, :, 1], rest[:, :, :]).then_inc(s["mid"], 1)
                    v.wait_ge(s["mid"], g + 1)
                    v.tensor_copy(wp[:, :, 8:8 + e], pb[:, :, 1]).then_inc(s["whi"], 1)
                    v.tensor_tensor(wp[:, :, 16:16 + e], rest[:, :, :], pb[:, :, 1], ALU.subtract).then_inc(s["wp"], 1)
                    if not first:
                        biased(g - 1)

                groups(v, TILES // RT, prologue, body, lambda: biased(TILES // RT - 1))


def batches(eng, body, epilogue):
    body(0, 0, True)
    with eng.Fori(0, (B - 2) // 2) as i:
        body(2 * i + 1, 1, False)
        body(2 * i + 2, 0, False)
    body(B - 1, 1, False)
    epilogue()


def experts_stage(nc, mem):
    h_all, W, hT_all, wT_all = mem["h"], mem["W"], mem["hT"], mem["wT"]
    with ExitStack() as ctx:
        sb = lambda n, s, d=F32: ctx.enter_context(nc.sbuf_tensor("f_" + n, s, d))
        ps = lambda n, s, d=F32: ctx.enter_context(nc.psum_tensor("f_" + n, s, d))
        pick = sb("pick", [32, 2 * 128], BF16)
        h1 = [sb(f"h1{e}", [128, L]) for e in range(5)]
        h2 = [sb(f"h2{q}", [128, L]) for q in range(3)]
        h2w = [sb(f"h2w{q}", [128, L]) for q in range(2)]
        total = sb("total", [128, L])
        l1 = [ps(f"l1{k}", [128, 512]) for k in range(2)]
        l2 = [ps(f"l2{k}", [128, 512]) for k in range(2)]
        wb = [ps(f"wb{k}", [128, 512]) for k in range(2)]
        acc, o_ps = ps("acc", [128, 512]), ps("o", [128, NT, C])
        s = signals(nc, ctx, "f_", "pick l1_ps h1 wb_ps l2_ps h2 h2w l3_ps total o_ps h")

        with nc.Block() as block:
            @block.tensor
            def _(pe):
                pe.sem_inc(s["o_ps"], 1)
                pe.wait_ge(s["pick"], 1)

                def first_layer(n, k, e):
                    pe.wait_ge(s["h1"], 5 * n + e + 1)
                    w1 = W("ew1", 128 * e, 128) if e < 4 else W("sw1")
                    pe.matmul(l1[(k + e) % 2][:, 0:L], w1, hT_all[:, bass.ds(L * n, L)], start=True, stop=True).then_inc(s["l1_ps"], 1)

                def weights(n):
                    for q in range(2):
                        pe.matmul(wb[q][:, 0:L], pick[:, 128 * q:128 * q + 128], wT_all[:, bass.ds(L * n, L)], start=True, stop=True)\
                            .then_inc(s["wb_ps"], 1)

                def second_layer(n, k, q):
                    pe.wait_ge(s["h1"], 5 * n + (4, 6, 7)[q])
                    pe.wait_ge(s["h2"], 3 * n + q + 1)
                    bank = l2[(k + q) % 2]
                    if q < 2:
                        for half in range(2):
                            mm = pe.matmul(bank[64 * half:64 * half + 64, 0:L], W("ew2", 64 * (2 * q + half), 64), h1[2 * q + half][:, :],
                                           start=True, stop=True)
                    else:
                        mm = pe.matmul(bank[:, 0:L], W("sw2"), h1[4][:, :], start=True, stop=True)
                    mm.then_inc(s["l2_ps"], 1)

                def third_layer(n, q):
                    if q < 2:
                        pe.wait_ge(s["h2w"], 2 * n + q + 3)
                    else:
                        pe.wait_ge(s["h2"], 3 * n + 5)
                    if q == 0:
                        pe.wait_ge(s["total"], n + 1)
                    half = q % 2
                    pe.matmul(acc[64 * half:64 * half + 64, 0:L], W("sw3") if q == 2 else W("ew3", 64 * q, 64), (h2w + h2[2:])[q][:, :],
                              start=(q < 2), stop=(q > 0)).then_inc(s["l3_ps"], 1)

                def back(n):
                    pe.wait_ge(s["total"], n + 2)
                    pe.wait_ge(s["h"], n + 1)
                    for j in range(NT):
                        mm = pe.matmul(o_ps[:, j, :], total[:, 128 * j:128 * j + 128], W("both"), start=True, stop=True)
                    mm.then_inc(s["o_ps"], 1)

                def body(n, k, first):
                    first_layer(n, k, 0)
                    pe.wait_ge(s["h2w"], 2 * n + 2)
                    first_layer(n, k, 1)
                    weights(n)
                    if not first:
                        third_layer(n - 1, 0)
                        third_layer(n - 1, 1)
                    first_layer(n, k, 2)
                    second_layer(n, k, 0)
                    if not first:
                        third_layer(n - 1, 2)
                    first_layer(n, k, 3)
                    first_layer(n, k, 4)
                    second_layer(n, k, 1)
                    if not first:
                        back(n - 1)
                    second_layer(n, k, 2)

                def epilogue():
                    for q in range(3):
                        third_layer(B - 1, q)
                    back(B - 1)
                batches(pe, body, epilogue)

            @block.scalar
            def _(act):
                act.sem_inc(s["h1"], 2)
                act.sem_inc(s["h2"], 2)
                act.sem_inc(s["total"], 1)
                act.copy(pick[:, :], W("pick0", rows=32)).then_inc(s["pick"], 1)

                def first_relu(n, k, e, first):
                    act.wait_ge(s["l1_ps"], 5 * n + e + 1)
                    if not first:
                        act.wait_ge(s["l2_ps"], 3 * n - 2 + e // 2)
                    act.activation(h1[e][:, :], l1[(k + e) % 2][:, 0:L], ACT.Relu).then_inc(s["h1"], 1)

                def second_relu(n, k, q, first):
                    act.wait_ge(s["l2_ps"], 3 * n + q + 1)
                    if not first and q < 2:
                        act.wait_ge(s["h2w"], 2 * n + q + 1)
                    elif not first:
                        act.wait_ge(s["l3_ps"], 3 * n)
                    act.activation(h2[q][:, :], l2[(k + q) % 2][:, 0:L], ACT.Relu, bias=W("sb2") if q == 2 else W("eb2", q, 1)).then_inc(s["h2"], 1)

                def summed(n):
                    act.wait_ge(s["l3_ps"], 3 * n + 3)
                    act.wait_ge(s["o_ps"], n + 1)
                    act.copy(total[:, :], acc[:, 0:L]).then_inc(s["total"], 1)

                def body(n, k, first):
                    first_relu(n, k, 0, first)
                    first_relu(n, k, 1, first)
                    first_relu(n, k, 2, first)
                    second_relu(n, k, 0, first)
                    first_relu(n, k, 3, first)
                    if not first:
                        summed(n - 1)
                    first_relu(n, k, 4, first)
                    second_relu(n, k, 1, first)
                    second_relu(n, k, 2, first)
                batches(act, body, lambda: summed(B - 1))

            @block.vector
            def _(v):
                v.sem_inc(s["h2w"], 2)
                v.sem_inc(s["h"], 1)

                def weigh(n, q, first):
                    v.wait_ge(s["wb_ps"], 2 * n + q + 1)
                    v.wait_ge(s["h2"], 3 * n + q + 3)
                    if not first:
                        v.wait_ge(s["l3_ps"], 3 * n - 2 + q)
                    v.tensor_tensor(h2w[q][:, :], h2[q][:, :], wb[q][:, 0:L], ALU.mult).then_inc(s["h2w"], 1)

                def added(n):
                    v.wait_ge(s["o_ps"], n + 2)
                    h = h_all[:, bass.ds(NT * n, NT), :]
                    v.tensor_tensor(h, h, o_ps[:, :, :], ALU.add).then_inc(s["h"], 1)

                def body(n, k, first):
                    weigh(n, 0, first)
                    if not first:
                        added(n - 1)
                    weigh(n, 1, first)
                batches(v, body, lambda: added(B - 1))


def gate_stage(nc, mem):
    h_all, W = mem["h"], mem["W"]
    with ExitStack() as ctx:
        sb = lambda n, s, d=F32: ctx.enter_context(nc.sbuf_tensor("g_" + n, s, d))
        ps = lambda n, s, d=F32: ctx.enter_context(nc.psum_tensor("g_" + n, s, d))
        nb = norm_buffers(sb, GT)
        hTg = sb("hTg", [128, GT * 128])
        one = sb("one", [64, 1])
        halfb = sb("halfb", [64, 1])
        th, sg = (sb(n, [64, GT // 4, 512]) for n in ("th", "sg"))
        y = sb("y", [128, GT // 4, 512])
        t_ps, g_ps = ps("t", [128, GT // 4, 512]), ps("g", [128, GT // 4, 512])
        o_ps = ps("o", [128, 2, 512])
        s = signals(nc, ctx, "g_", "half ones ht_ps ht g_ps th sg y o_ps h " + norm_names())
        bufs = [nb[n] for n in ("sm", "nm", "ve", "hc", "hs")]
        with nc.Block() as block:
            @block.gpsimd
            def _(pl):
                pl.memset(one[:, :], 1.0)
                pl.memset(nb["half"][:, :], -0.5).then_inc(s["half"], 1)
                pl.wait_ge(s["half"], 1)

                def norm(g):
                    pl.wait_ge(s["ve"], g + 1)
                    pl.tensor_tensor(nb["rs"][:, :], nb["ve"][:, :], nb["half"][:, :], ALU.pow).then_inc(s["rs"], 1)

                def body(g, first, last):
                    if not last:
                        norm(g + 1)
                    pl.wait_ge(s["y"], g + 1)
                    for q in range(GT // 4):
                        pl.wait_ge(s["th"], 3 * g + q + 1)
                        pl.tensor_tensor(sg[:, q, :], th[:, q, :], one[:, :].broadcast_to([64, 512]), ALU.add).then_inc(s["sg"], 1)
                groups(pl, TILES // GT, lambda: norm(0), body, lambda: None)

            @block.tensor
            def _(pe):
                pe.wait_ge(s["ones"], 2)

                def gates(g):
                    pe.wait_ge(s["hn"], g + 2)
                    for j in range(GT):
                        mm = pe.transpose(t_ps[:, j // 4, 128 * (j % 4):128 * (j % 4) + 128],
                                          nb["hn"][:, j:j + 2, :].rearrange("p a b -> p (a b)"), W("ident"))
                        if j % 4 == 3:
                            mm.then_inc(s["ht_ps"], 1)
                    for q in range(GT // 4):
                        pe.wait_ge(s["ht"], 3 * g + q + 1)
                        pe.matmul(g_ps[:, q, :], W("glg", 0, 128), hTg[:, 512 * q:512 * q + 512], start=True, stop=True).then_inc(s["g_ps"], 1)

                def outputs(g):
                    pe.wait_ge(s["y"], g + 2)
                    for j in range(GT):
                        mm = pe.matmul(o_ps[:, j // 6, 64 * (j % 6):64 * (j % 6) + 64], y[:, j // 4, 128 * (j % 4):128 * (j % 4) + 128],
                                       W("glo"), start=True, stop=True)
                    mm.then_inc(s["o_ps"], 1)

                def body(g, first, last):
                    if not last:
                        gates(g + 1)
                    outputs(g)
                groups(pe, TILES // GT, lambda: gates(0), body, lambda: None)

            @block.scalar
            def _(act):
                def gates(g):
                    for q in range(GT // 4):
                        act.wait_ge(s["ht_ps"], 3 * g + q + 1)
                        act.copy(hTg[0:64, 512 * q:512 * q + 512], t_ps[0:64, q, :]).then_inc(s["ht"], 1)
                    for q in range(GT // 4):
                        act.wait_ge(s["g_ps"], 3 * g + q + 1)
                        act.activation(th[:, q, :], g_ps[0:64, q, :], ACT.Tanh, scale=0.5).then_inc(s["th"], 1)

                groups(act, TILES // GT, lambda: gates(0), lambda g, first, last: None if last else gates(g + 1), lambda: None)

            @block.vector
            def _(v):
                v.sem_inc(s["hn"], 1)
                v.sem_inc(s["y"], 1)
                v.memset(nb["hn"][:, GT, :], 0.0)
                v.memset(hTg[64:128, :], 0.0)
                v.tensor_scalar(halfb[:, :], W("gnb", rows=64), 0.5, None, ALU.mult)
                v.memset(y[64:128, :, :], 0.0).then_inc(s["ones"], 1)
                v.wait_ge(s["ones"], 1)
                v.memset(y[64:65, :, :], 1.0).then_inc(s["ones"], 1)
                v.wait_ge(s["ones"], 2)

                def tokens(g):
                    return h_all[:, bass.ds(GT * g, GT), :]

                def norm(g):
                    layer_norm(v, s, g, tokens(g), GT, bufs)

                def scaled(g):
                    layer_norm_scale(v, s, g, nb["rs"], nb["hc"], nb["hn"][:, 0:GT, :], GT)

                def added(g):
                    v.wait_ge(s["o_ps"], g + 1)
                    h = tokens(g).rearrange("p (a b) c -> p a (b c)", a=2)
                    v.tensor_tensor(h, h, o_ps[:, :, 0:384], ALU.add).then_inc(s["h"], 1)

                def prologue():
                    norm(0)
                    scaled(0)

                def body(g, first, last):
                    if not last:
                        norm(g + 1)
                    if not first:
                        added(g - 1)
                    v.wait_ge(s["sg"], 3 * g + 3)
                    v.scalar_tensor_tensor(y[0:64, :, :], g_ps[0:64, :, :], halfb[:, :], sg[:, :, :], ALU.mult, ALU.mult).then_inc(s["y"], 1)
                    if not last:
                        scaled(g + 1)
                groups(v, TILES // GT, prologue, body, lambda: added(TILES // GT - 1))


def gelu_experts_stage(nc, mem):
    h_all, W, hT_all, wT_all = mem["h"], mem["W"], mem["hT"], mem["wT"]
    NE, LAG = E1 + 1, 2
    with ExitStack() as ctx:
        sb = lambda n, s, d=F32: ctx.enter_context(nc.sbuf_tensor("x_" + n, s, d))
        ps = lambda n, s, d=F32: ctx.enter_context(nc.psum_tensor("x_" + n, s, d))
        pick = sb("pick", [32, E1 * 128], BF16)
        g = [sb(f"g{k}", [128, 2, L]) for k in range(3)]
        gw = [sb(f"gw{k}", [128, 2, L]) for k in range(2)]
        total = sb("total", [128, L])
        l1 = [ps(f"l1{k}", [128, 2, 512]) for k in range(2)]
        wb = [ps(f"wb{k}", [128, 512]) for k in range(2)]
        acc, o_ps = ps("acc", [128, 512]), ps("o", [128, NT, C])
        s = signals(nc, ctx, "x_", "pick l1_ps wb_ps g gw l2_ps total o_ps h")

        with nc.Block() as block:
            @block.tensor
            def _(pe):
                pe.sem_inc(s["o_ps"], 1)
                pe.wait_ge(s["pick"], 1)

                def second_layer(n, q):
                    if q < E1:
                        pe.wait_ge(s["gw"], E1 * n + q + 3)
                    else:
                        pe.wait_ge(s["g"], NE * n + q + 3)
                    if q == 0:
                        pe.wait_ge(s["total"], n + 1)
                    src = gw[q % 2] if q < E1 else g[q % 3]
                    for f in range(2):
                        mm = pe.matmul(acc[64 * f:64 * f + 64, 0:L], W("w2", 128 * q + C * f, C), src[:, f, :], start=(q == 0), stop=(q == NE - 1))
                    mm.then_inc(s["l2_ps"], 1)

                def back(n):
                    pe.wait_ge(s["total"], n + 2)
                    pe.wait_ge(s["h"], n + 1)
                    for j in range(NT):
                        mm = pe.matmul(o_ps[:, j, :], total[:, 128 * j:128 * j + 128], W("both"), start=True, stop=True)
                    mm.then_inc(s["o_ps"], 1)

                def body(n, k, first):
                    for e in range(NE):
                        pe.wait_ge(s["g"], NE * n + e + 1)
                        for f in range(2):
                            if f == 1 and e < E1:
                                pe.wait_ge(s["gw"], E1 * n + e + 1)
                            mm = pe.matmul(l1[(k + e) % 2][:, f, 0:L], W("w1", F1 * e + 128 * f, 128), hT_all[:, bass.ds(L * n, L)],
                                           start=True, stop=True)
                        mm.then_inc(s["l1_ps"], 1)
                        if e < E1:
                            pe.matmul(wb[e % 2][:, 0:L], pick[:, 128 * e:128 * e + 128], wT_all[:, bass.ds(L * n, L)], start=True, stop=True)\
                                .then_inc(s["wb_ps"], 1)
                        if e >= LAG:
                            second_layer(n, e - LAG)
                        elif not first:
                            second_layer(n - 1, e - LAG + NE)
                        if e == 3 and not first:
                            back(n - 1)

                def epilogue():
                    for q in range(NE - LAG, NE):
                        second_layer(B - 1, q)
                    back(B - 1)
                batches(pe, body, epilogue)

            @block.scalar
            def _(act):
                act.sem_inc(s["g"], 2)
                act.sem_inc(s["total"], 1)
                act.copy(pick[:, :], W("pick1", rows=32)).then_inc(s["pick"], 1)

                def summed(n):
                    act.wait_ge(s["l2_ps"], NE * n + NE)
                    act.wait_ge(s["o_ps"], n + 1)
                    act.copy(total[:, :], acc[:, 0:L]).then_inc(s["total"], 1)

                def body(n, k, first):
                    for e in range(NE):
                        act.wait_ge(s["l1_ps"], NE * n + e + 1)
                        if e >= 3:
                            act.wait_ge(s["gw"], E1 * n + e)
                        elif not first and e < 2:
                            act.wait_ge(s["gw"], E1 * n + e + 1)
                        elif not first:
                            act.wait_ge(s["l2_ps"], NE * n)
                        act.activation(g[e % 3][:, :, :], l1[(k + e) % 2][:, :, 0:L], ACT.Gelu).then_inc(s["g"], 1)
                        if e == 1 and not first:
                            summed(n - 1)
                batches(act, body, lambda: summed(B - 1))

            @block.vector
            def _(v):
                v.sem_inc(s["gw"], 2)
                v.sem_inc(s["h"], 1)

                def added(n):
                    v.wait_ge(s["o_ps"], n + 2)
                    h = h_all[:, bass.ds(NT * n, NT), :]
                    v.tensor_tensor(h, h, o_ps[:, :, :], ALU.add).then_inc(s["h"], 1)

                def body(n, k, first):
                    for e in range(E1):
                        v.wait_ge(s["g"], NE * n + e + 3)
                        v.wait_ge(s["wb_ps"], E1 * n + e + 1)
                        if e >= 2:
                            v.wait_ge(s["l2_ps"], NE * n + e - 1)
                        elif not first:
                            v.wait_ge(s["l2_ps"], NE * n - 2 + e)
                        v.tensor_tensor(gw[e % 2][:, :, :], g[e % 3][:, :, :], wb[e % 2][:, 0:L].unsqueeze(1).broadcast_to([128, 2, L]),
                                        ALU.mult).then_inc(s["gw"], 1)
                        if e == 4 and not first:
                            added(n - 1)
                batches(v, body, lambda: added(B - 1))


def early_fusion_program(nc, x, txt, pack, out):
    with ExitStack() as ctx:
        w = ctx.enter_context(nc.sbuf_tensor("w", [128, WCOLS], F32))
        h = ctx.enter_context(nc.sbuf_tensor("h", [128, TILES, C], F32))

        def W(name, col=0, cols=None, rows=128):
            at, width = AT[name]
            return w[0:rows, at + col:at + col + (width if cols is None else cols)]

        mem = {"w": w, "h": h, "W": W}
        load_stage(nc, mem, pack, txt)
        tok_stage(nc, mem, x)
        attention_stage(nc, mem)
        with (nc.sbuf_tensor("hT", [128, B * L], F32) as hT, nc.sbuf_tensor("wT", [32, B * L], BF16) as wT):
            mem["hT"], mem["wT"] = hT, wT
            routing_stage(nc, mem, E0, "gw", "tie0", "bias0", True)
            experts_stage(nc, mem)
            gate_stage(nc, mem)
            routing_stage(nc, mem, E1, "wr", "tie1", "bias1", False)
            gelu_experts_stage(nc, mem)
        store_stage(nc, mem, out)


def kernel(**inputs):
    import numpy as np
    import concourse.bacc as _bacc
    from concourse import mybir as _mybir
    from concourse.bass_utils import run_bass_kernel_spmd as _run

    f32 = np.float32
    w = {k: np.ascontiguousarray(v) for k, v in inputs.items()}
    pack = np.zeros((128, WCOLS), f32)

    def put(name, value, row=0, col=0):
        at, _ = AT[name]
        value = value.reshape(value.shape[0], -1)
        pack[row:row + value.shape[0], at + col:at + col + value.shape[1]] = value

    def rows(name, vector, col=0):
        put(name, np.broadcast_to(vector.reshape(1, -1), (128, vector.size)), 0, col)

    def twice(name, block):
        put(name, block)
        put(name, block, 64, 64)

    put("ident", np.eye(128, dtype=f32))
    head_of = np.repeat(np.eye(16, dtype=f32), 8, axis=0)
    full = np.zeros((128, 8, 8, 16), f32)
    for c in range(8):
        full[:, c, c, :] = head_of
    put("sel", full)
    put("selT", full.reshape(128, 8, 128).transpose(2, 1, 0))
    center = np.eye(64, dtype=f32) - np.full((64, 64), 1 / 64, f32)
    twice("center", center)
    for c in range(4):
        for image in range(2):
            put("blk", np.full((64, 1), 1 / 64, f32), 64 * image, 32 * c + 2 * c + image)
    lower = lambda n: np.array([[1.0 if j < i else 0.0 for j in range(n)] for i in range(n)], f32)
    rows("tie0", lower(E0))
    rows("tie1", lower(E1))
    twice("tq", w["L0_tok_Wq"].T)
    twice("tk", w["L0_tok_Wkv"][:64].T)
    twice("tv", w["L0_tok_Wkv"][64:].T)
    twice("tproj", w["L0_tok_proj_w"].T)
    for r in (0, 64):
        put("kvw", w["L0_tok_ln_kv_w"][:, None], r)
        put("kvb", w["L0_tok_ln_kv_b"][:, None], r)
    rows("lnqw", w["L0_tok_ln_q_w"])
    rows("lnqb", w["L0_tok_ln_q_b"])
    rows("projb", w["L0_tok_proj_b"])
    put("aqk", w["L0_attn_Wq"])
    put("aqk", w["L0_attn_Wkv"][:, :INNER], 0, INNER)
    put("avg", w["L0_attn_Wkv"][:, INNER:])
    put("avg", w["L0_attn_Wg"], 0, INNER)
    put("avg", w["L0_attn_bg"][None], 64, INNER)
    put("aout", w["L0_attn_Wout"][:128])
    put("aout", w["L0_attn_Wout"][128:], 0, 64)
    rows("aoutb", w["L0_attn_bout"])
    rows("gam", w["L0_attn_ln_gamma"])
    rows("bet", w["L0_attn_ln_beta"])
    for i, n in enumerate(("lq1", "lk1", "lq2", "lk2")):
        rows("lqk", w["L0_attn_" + n], 16 * i)
    put("sw1", w["L0_ffn_sW1"])
    put("sw1", w["L0_ffn_sb1"][None], 64)
    put("ew1", w["L0_ffn_eW1"].transpose(1, 0, 2))
    put("ew1", w["L0_ffn_eb1"].reshape(1, -1), 64)
    put("gw", w["L0_ffn_gW"])
    put("gw", w["L0_ffn_gb"][None], 64)
    put("sw2", w["L0_ffn_sW2"])
    put("sb2", w["L0_ffn_sb2"][:, None])
    put("sw3", w["L0_ffn_sW3"])
    put("ew2", w["L0_ffn_eW2"].transpose(1, 0, 2))
    put("eb2", w["L0_ffn_eb2"].reshape(2, 128).T)
    for e in range(E0):
        put("ew3", w["L0_ffn_eW3"][e], 64 * (e % 2), 64 * (e // 2))
    for part in range(3):
        put("bias0", w["L0_ffn_eb3"], 8 * part)
        put("bias1", w["L1_ffn_b2p"], 8 * part)
        put("pick0", np.repeat(np.eye(E0, dtype=f32), 64, axis=1), 8 * part)
        put("pick1", np.repeat(np.eye(E1, dtype=f32), 128, axis=1), 8 * part)
    put("bias0", w["L0_ffn_sb3"][None], 24)
    put("bias1", w["L1_ffn_b2s"][None], 24)
    put("both", np.tile(np.eye(64, dtype=f32), (2, 1)))
    put("glg", w["L1_attn_wg"])
    put("glo", w["L1_attn_wo"])
    put("gnb", w["L1_attn_gn_bias"][:, None])
    put("glo", w["L1_attn_bias"][None], 64)
    put("wr", w["L1_ffn_Wr"])
    put("w1", w["L1_ffn_W1p"].transpose(1, 0, 2))
    put("w1", w["L1_ffn_b1p"].reshape(1, -1), 64)
    put("w1", w["L1_ffn_W1s"], 0, 8 * F1)
    put("w1", w["L1_ffn_b1s"][None], 64, 8 * F1)
    put("w2", w["L1_ffn_W2p"].reshape(8, 2, 128, 64).transpose(2, 0, 1, 3))
    put("w2", w["L1_ffn_W2s"].reshape(2, 128, 64).transpose(1, 0, 2), 0, 8 * 128)

    arrays = {"x": w["x"].reshape(B // 2, 128, IMG * IMG), "txt": w["txt"], "pack": pack}
    nc = _bacc.Bacc("TRN2", target_bir_lowering=False, num_devices=1)
    args = [nc.dram_tensor(f"{k}_dram", a.shape, _mybir.dt.from_np(a.dtype), kind="ExternalInput").ap()
            for k, a in arrays.items()]
    args.append(nc.dram_tensor("out_dram", (B, L, C), _mybir.dt.float32, kind="ExternalOutput").ap())
    early_fusion_program(nc, *args)
    r = _run(nc, [{f"{k}_dram": a for k, a in arrays.items()}], core_ids=[0])
    return r.results[0]["out_dram"]
```
